# Optimizing a Trainium2 kernel written in Bass

```python
import numpy as np
import jax
import jax.numpy as jnp

def _softmax(x, axis=-1):
    return jax.nn.softmax(x, axis=axis)
def _gelu(x):
    return jax.nn.gelu(x, approximate=True)
def _silu(x):
    return jax.nn.silu(x)
def _sigmoid(x):
    return jax.nn.sigmoid(x)
def _layernorm(x, axis=-1, eps=1e-5):
    m = jnp.mean(x, axis=axis, keepdims=True)
    v = jnp.var(x, axis=axis, keepdims=True)
    return (x - m) / jnp.sqrt(v + eps)
def _scatter_add(tgt, idx, src, axis=0):
    return tgt.at[idx].add(src)
def _segment_sum(src, seg, n):
    return jax.ops.segment_sum(src, seg, n)

kernel_name = 'mk_conv_seq_d2_conv_nhwc256_8e558d'

def setup_inputs(seed: int = 0):
    np.random.seed(seed)
    _w = jnp.asarray
    def _rec_inputs():
        import jax
        import jax.numpy as jnp
        _gk = jax.random.key(seed)
        x = -0.0002023 + 1 * jax.random.normal(jax.random.fold_in(_gk, 1), (8, 56, 56, 256), jnp.float32)
        return x
    x = _rec_inputs()
    def _L0_conv_setup():
        import jax, jax.numpy as jnp
        import numpy as np
        N_WIN = 7
        NUM_HEADS = 8
        DIM = 256
        QK = 256
        TOPK = 4
        MLP_HID = 4 * DIM
        SCALE = QK ** (-0.5)

        def _layernorm(x, g, b, eps=1e-06):
            mu = jnp.mean(x, axis=-1, keepdims=True)
            var = jnp.mean(jnp.square(x - mu), axis=-1, keepdims=True)
            return (x - mu) * jax.lax.rsqrt(var + eps) * g + b

        def _dwconv(x, w, b):
            y = jax.lax.conv_general_dilated(x, w, window_strides=(1, 1), padding='SAME', feature_group_count=x.shape[-1], dimension_numbers=('NHWC', 'HWIO', 'NHWC'))
            return y + b

        def _bra(x, qkv_w, qkv_b, lepe_w, lepe_b, wo_w, wo_b):
            N, H, W, C = x.shape
            j = i = N_WIN
            h, w = (H // j, W // i)
            p2, w2, m = (j * i, h * w, NUM_HEADS)
            dq, dv = (QK // m, C // m)
            xw = x.reshape(N, j, h, i, w, C).transpose(0, 1, 3, 2, 4, 5).reshape(N, p2, h, w, C)
            qkv = xw @ qkv_w + qkv_b
            q = qkv[..., :QK]
            kv = qkv[..., QK:]
            q_pix = q.reshape(N, p2, w2, QK)
            kv_pix = kv.reshape(N, p2, w2, QK + C)
            q_win = jnp.mean(q, axis=(2, 3))
            k_win = jnp.mean(kv[..., :QK], axis=(2, 3))
            v_img = kv[..., QK:].reshape(N, j, i, h, w, C).transpose(0, 1, 3, 2, 4, 5).reshape(N, H, W, C)
            lepe = _dwconv(v_img, lepe_w, lepe_b)
            logit = jnp.einsum('npc,nqc->npq', q_win * SCALE, k_win)
            _, r_idx = jax.lax.top_k(logit, TOPK)
            kv_sel = kv_pix[jnp.arange(N)[:, None, None], r_idx]
            k_sel = kv_sel[..., :QK].reshape(N, p2, TOPK * w2, m, dq).transpose(0, 1, 3, 2, 4)
            v_sel = kv_sel[..., QK:].reshape(N, p2, TOPK * w2, m, dv).transpose(0, 1, 3, 2, 4)
            q_h = q_pix.reshape(N, p2, w2, m, dq).transpose(0, 1, 3, 2, 4)
            aw = jnp.einsum('npmqd,npmkd->npmqk', q_h * SCALE, k_sel)
            aw = jax.nn.softmax(aw, axis=-1)
            out = jnp.einsum('npmqk,npmkd->npmqd', aw, v_sel)
            out = out.transpose(0, 1, 3, 2, 4).reshape(N, j, i, h, w, C)
            out = out.transpose(0, 1, 3, 2, 4, 5).reshape(N, H, W, C)
            out = out + lepe
            return out @ wo_w + wo_b
        key = jax.random.key(seed)
        ks = jax.random.split(key, 8)
        s = 0.02
        return {'x': jax.random.normal(ks[0], (8, 56, 56, DIM), dtype=jnp.float32), 'ln1_g': jnp.ones((DIM,), jnp.float32), 'ln1_b': jnp.zeros((DIM,), jnp.float32), 'qkv_w': jax.random.normal(ks[1], (DIM, 2 * QK + DIM), jnp.float32) * s, 'qkv_b': jnp.zeros((2 * QK + DIM,), jnp.float32), 'lepe_w': jax.random.normal(ks[2], (5, 5, 1, DIM), jnp.float32) * s, 'lepe_b': jnp.zeros((DIM,), jnp.float32), 'wo_w': jax.random.normal(ks[3], (DIM, DIM), jnp.float32) * s, 'wo_b': jnp.zeros((DIM,), jnp.float32), 'ln2_g': jnp.ones((DIM,), jnp.float32), 'ln2_b': jnp.zeros((DIM,), jnp.float32), 'mlp_w1': jax.random.normal(ks[4], (DIM, MLP_HID), jnp.float32) * s, 'mlp_b1': jnp.zeros((MLP_HID,), jnp.float32), 'mlp_w2': jax.random.normal(ks[5], (MLP_HID, DIM), jnp.float32) * s, 'mlp_b2': jnp.zeros((DIM,), jnp.float32)}
    _L0_conv_all = _L0_conv_setup()
    _L0_conv_in = {k: v for k, v in _L0_conv_all.items() if k in ('ln1_g', 'ln1_b', 'qkv_w', 'qkv_b', 'lepe_w', 'lepe_b', 'wo_w', 'wo_b', 'ln2_g', 'ln2_b', 'mlp_w1', 'mlp_b1', 'mlp_w2', 'mlp_b2', )}
    del _L0_conv_all

    def _L1_conv_setup():
        import jax, jax.numpy as jnp
        import numpy as np
        EPS = 1e-05

        def _layernorm(x, g, b):
            mu = jnp.mean(x, axis=-1, keepdims=True)
            var = jnp.var(x, axis=-1, keepdims=True)
            return (x - mu) * jax.lax.rsqrt(var + EPS) * g + b
        key = jax.random.key(seed)
        ks = jax.random.split(key, 8)
        B, H, W, C = (4, 32, 32, 256)
        Dn, N, R = (512, 64, 16)
        f = lambda k, shape, s=0.02: jax.random.normal(k, shape, jnp.float32) * s
        A_log = jnp.log(jnp.tile(jnp.arange(1, N + 1, dtype=jnp.float32)[None, :], (Dn, 1)))
        return {'src': jax.random.normal(ks[0], (B, H, W, C), jnp.float32), 'ln1_g': jnp.ones((C,), jnp.float32), 'ln1_b': jnp.zeros((C,), jnp.float32), 'w_in': f(ks[1], (C, Dn)), 'b_in': jnp.zeros((Dn,), jnp.float32), 'conv_w': f(ks[2], (3, 3, 1, Dn), 0.1), 'conv_b': jnp.zeros((Dn,), jnp.float32), 'w_x': f(ks[3], (Dn, R + 2 * N)), 'w_dt': f(ks[4], (R, Dn), 0.1), 'dt_bias': jnp.full((Dn,), -4.6, jnp.float32), 'A_log': A_log, 'D_skip': jnp.ones((Dn,), jnp.float32), 'ln2_g': jnp.ones((Dn,), jnp.float32), 'ln2_b': jnp.zeros((Dn,), jnp.float32), 'w_out': f(ks[5], (Dn, C)), 'b_out': jnp.zeros((C,), jnp.float32)}
    _L1_conv_all = _L1_conv_setup()
    _L1_conv_in = {k: v for k, v in _L1_conv_all.items() if k in ('ln1_g', 'ln1_b', 'w_in', 'b_in', 'conv_w', 'conv_b', 'w_x', 'w_dt', 'dt_bias', 'A_log', 'D_skip', 'ln2_g', 'ln2_b', 'w_out', 'b_out', )}
    del _L1_conv_all

    return {
        "x": x,
        "L0_conv_ln1_g": _L0_conv_in["ln1_g"],
        "L0_conv_ln1_b": _L0_conv_in["ln1_b"],
        "L0_conv_qkv_w": _L0_conv_in["qkv_w"],
        "L0_conv_qkv_b": _L0_conv_in["qkv_b"],
        "L0_conv_lepe_w": _L0_conv_in["lepe_w"],
        "L0_conv_lepe_b": _L0_conv_in["lepe_b"],
        "L0_conv_wo_w": _L0_conv_in["wo_w"],
        "L0_conv_wo_b": _L0_conv_in["wo_b"],
        "L0_conv_ln2_g": _L0_conv_in["ln2_g"],
        "L0_conv_ln2_b": _L0_conv_in["ln2_b"],
        "L0_conv_mlp_w1": _L0_conv_in["mlp_w1"],
        "L0_conv_mlp_b1": _L0_conv_in["mlp_b1"],
        "L0_conv_mlp_w2": _L0_conv_in["mlp_w2"],
        "L0_conv_mlp_b2": _L0_conv_in["mlp_b2"],
        "L1_conv_ln1_g": _L1_conv_in["ln1_g"],
        "L1_conv_ln1_b": _L1_conv_in["ln1_b"],
        "L1_conv_w_in": _L1_conv_in["w_in"],
        "L1_conv_b_in": _L1_conv_in["b_in"],
        "L1_conv_conv_w": _L1_conv_in["conv_w"],
        "L1_conv_conv_b": _L1_conv_in["conv_b"],
        "L1_conv_w_x": _L1_conv_in["w_x"],
        "L1_conv_w_dt": _L1_conv_in["w_dt"],
        "L1_conv_dt_bias": _L1_conv_in["dt_bias"],
        "L1_conv_A_log": _L1_conv_in["A_log"],
        "L1_conv_D_skip": _L1_conv_in["D_skip"],
        "L1_conv_ln2_g": _L1_conv_in["ln2_g"],
        "L1_conv_ln2_b": _L1_conv_in["ln2_b"],
        "L1_conv_w_out": _L1_conv_in["w_out"],
        "L1_conv_b_out": _L1_conv_in["b_out"],
    }

def reference(x, L0_conv_ln1_g, L0_conv_ln1_b, L0_conv_qkv_w, L0_conv_qkv_b, L0_conv_lepe_w, L0_conv_lepe_b, L0_conv_wo_w, L0_conv_wo_b, L0_conv_ln2_g, L0_conv_ln2_b, L0_conv_mlp_w1, L0_conv_mlp_b1, L0_conv_mlp_w2, L0_conv_mlp_b2, L1_conv_ln1_g, L1_conv_ln1_b, L1_conv_w_in, L1_conv_b_in, L1_conv_conv_w, L1_conv_conv_b, L1_conv_w_x, L1_conv_w_dt, L1_conv_dt_bias, L1_conv_A_log, L1_conv_D_skip, L1_conv_ln2_g, L1_conv_ln2_b, L1_conv_w_out, L1_conv_b_out):
    import jax
    import jax.numpy as jnp
    def _L0_conv_ref(x, ln1_g, ln1_b, qkv_w, qkv_b, lepe_w, lepe_b, wo_w, wo_b, ln2_g, ln2_b, mlp_w1, mlp_b1, mlp_w2, mlp_b2):
        import jax, jax.numpy as jnp
        import numpy as np
        N_WIN = 7
        NUM_HEADS = 8
        DIM = 256
        QK = 256
        TOPK = 4
        MLP_HID = 4 * DIM
        SCALE = QK ** (-0.5)

        def _layernorm(x, g, b, eps=1e-06):
            mu = jnp.mean(x, axis=-1, keepdims=True)
            var = jnp.mean(jnp.square(x - mu), axis=-1, keepdims=True)
            return (x - mu) * jax.lax.rsqrt(var + eps) * g + b

        def _dwconv(x, w, b):
            y = jax.lax.conv_general_dilated(x, w, window_strides=(1, 1), padding='SAME', feature_group_count=x.shape[-1], dimension_numbers=('NHWC', 'HWIO', 'NHWC'))
            return y + b

        def _bra(x, qkv_w, qkv_b, lepe_w, lepe_b, wo_w, wo_b):
            N, H, W, C = x.shape
            j = i = N_WIN
            h, w = (H // j, W // i)
            p2, w2, m = (j * i, h * w, NUM_HEADS)
            dq, dv = (QK // m, C // m)
            xw = x.reshape(N, j, h, i, w, C).transpose(0, 1, 3, 2, 4, 5).reshape(N, p2, h, w, C)
            qkv = xw @ qkv_w + qkv_b
            q = qkv[..., :QK]
            kv = qkv[..., QK:]
            q_pix = q.reshape(N, p2, w2, QK)
            kv_pix = kv.reshape(N, p2, w2, QK + C)
            q_win = jnp.mean(q, axis=(2, 3))
            k_win = jnp.mean(kv[..., :QK], axis=(2, 3))
            v_img = kv[..., QK:].reshape(N, j, i, h, w, C).transpose(0, 1, 3, 2, 4, 5).reshape(N, H, W, C)
            lepe = _dwconv(v_img, lepe_w, lepe_b)
            logit = jnp.einsum('npc,nqc->npq', q_win * SCALE, k_win)
            _, r_idx = jax.lax.top_k(logit, TOPK)
            kv_sel = kv_pix[jnp.arange(N)[:, None, None], r_idx]
            k_sel = kv_sel[..., :QK].reshape(N, p2, TOPK * w2, m, dq).transpose(0, 1, 3, 2, 4)
            v_sel = kv_sel[..., QK:].reshape(N, p2, TOPK * w2, m, dv).transpose(0, 1, 3, 2, 4)
            q_h = q_pix.reshape(N, p2, w2, m, dq).transpose(0, 1, 3, 2, 4)
            aw = jnp.einsum('npmqd,npmkd->npmqk', q_h * SCALE, k_sel)
            aw = jax.nn.softmax(aw, axis=-1)
            out = jnp.einsum('npmqk,npmkd->npmqd', aw, v_sel)
            out = out.transpose(0, 1, 3, 2, 4).reshape(N, j, i, h, w, C)
            out = out.transpose(0, 1, 3, 2, 4, 5).reshape(N, H, W, C)
            out = out + lepe
            return out @ wo_w + wo_b
        x = x + _bra(_layernorm(x, ln1_g, ln1_b), qkv_w, qkv_b, lepe_w, lepe_b, wo_w, wo_b)
        h = _layernorm(x, ln2_g, ln2_b)
        h = jax.nn.gelu(h @ mlp_w1 + mlp_b1, approximate=False) @ mlp_w2 + mlp_b2
        return x + h

    def _L1_conv_ref(src, ln1_g, ln1_b, w_in, b_in, conv_w, conv_b, w_x, w_dt, dt_bias, A_log, D_skip, ln2_g, ln2_b, w_out, b_out):
        import jax, jax.numpy as jnp
        import numpy as np
        EPS = 1e-05

        def _layernorm(x, g, b):
            mu = jnp.mean(x, axis=-1, keepdims=True)
            var = jnp.var(x, axis=-1, keepdims=True)
            return (x - mu) * jax.lax.rsqrt(var + EPS) * g + b
        B, H, W, C = src.shape
        Dn = w_in.shape[1]
        R = w_dt.shape[0]
        N = A_log.shape[1]
        x = _layernorm(src, ln1_g, ln1_b)
        x = x @ w_in + b_in
        x = jax.lax.conv_general_dilated(x, conv_w, window_strides=(1, 1), padding='SAME', feature_group_count=Dn, dimension_numbers=('NHWC', 'HWIO', 'NHWC')) + conv_b
        x = jax.nn.gelu(x)
        L = H * W
        x = x.reshape(B, L, Dn)
        proj = x @ w_x
        dt_raw, Bm, Cm = jnp.split(proj, [R, R + N], axis=-1)
        dt = jax.nn.softplus(dt_raw @ w_dt + dt_bias)
        A = -jnp.exp(A_log)

        def step(h, inp):
            xt, dtt, Bt, Ct = inp
            dA = jnp.exp(dtt[:, :, None] * A)
            h = dA * h + (dtt * xt)[:, :, None] * Bt[:, None, :]
            y = jnp.einsum('bdn,bn->bd', h, Ct)
            return (h, y)
        h0 = jnp.zeros((B, Dn, N), x.dtype)
        xs = (x.transpose(1, 0, 2), dt.transpose(1, 0, 2), Bm.transpose(1, 0, 2), Cm.transpose(1, 0, 2))
        _, ys = jax.lax.scan(step, h0, xs)
        y = ys.transpose(1, 0, 2) + x * D_skip
        y = _layernorm(y, ln2_g, ln2_b)
        out = y @ w_out + b_out
        return src + out.reshape(B, H, W, C)

    def _gn(v, G=32, eps=1e-5):
        B_, H_, W_, C_ = v.shape
        g = v.reshape(B_, H_, W_, G, C_ // G)
        m = jnp.mean(g, axis=(1, 2, 4), keepdims=True)
        s = jnp.var(g, axis=(1, 2, 4), keepdims=True)
        return ((g - m) / jnp.sqrt(s + eps)).reshape(v.shape)

    def _ln_c(v, eps=1e-6):
        m = jnp.mean(v, axis=-1, keepdims=True)
        s = jnp.var(v, axis=-1, keepdims=True)
        return (v - m) / jnp.sqrt(s + eps)

    def _ln_t(v, eps=1e-5):
        m = jnp.mean(v, axis=-1, keepdims=True)
        s = jnp.var(v, axis=-1, keepdims=True)
        return (v - m) / jnp.sqrt(s + eps)

    def _to_tokens(v):
        B_, H_, W_, C_ = v.shape
        return v.reshape(B_, H_ * W_, C_)
    def _from_tokens(t, like):
        return t.reshape(like.shape)

    x = _L0_conv_ref(x, L0_conv_ln1_g, L0_conv_ln1_b, L0_conv_qkv_w, L0_conv_qkv_b, L0_conv_lepe_w, L0_conv_lepe_b, L0_conv_wo_w, L0_conv_wo_b, L0_conv_ln2_g, L0_conv_ln2_b, L0_conv_mlp_w1, L0_conv_mlp_b1, L0_conv_mlp_w2, L0_conv_mlp_b2)
    x = _L1_conv_ref(x, L1_conv_ln1_g, L1_conv_ln1_b, L1_conv_w_in, L1_conv_b_in, L1_conv_conv_w, L1_conv_conv_b, L1_conv_w_x, L1_conv_w_dt, L1_conv_dt_bias, L1_conv_A_log, L1_conv_D_skip, L1_conv_ln2_g, L1_conv_ln2_b, L1_conv_w_out, L1_conv_b_out)
    return x


_drawn_inputs = setup_inputs


def setup_inputs(seed=0):
    import zlib

    import numpy as np

    out = dict(_drawn_inputs(seed))
    spreads = {'L0_conv_ln1_g': (1.0, 0.6),
     'L0_conv_ln1_b': (0.0, 0.8),
     'L0_conv_qkv_b': (0.0, 0.1),
     'L0_conv_lepe_b': (0.0, 0.28),
     'L0_conv_wo_b': (0.0, 0.1),
     'L0_conv_ln2_g': (1.0, 0.6),
     'L0_conv_ln2_b': (0.0, 0.8),
     'L0_conv_mlp_b1': (0.0, 0.1),
     'L0_conv_mlp_b2': (0.0, 0.1),
     'L1_conv_ln1_g': (1.0, 0.2),
     'L1_conv_ln1_b': (0.0, 0.295),
     'L1_conv_b_in': (0.0, 0.1),
     'L1_conv_conv_b': (0.0, 0.1),
     'L1_conv_dt_bias': (-4.599999904632568, 0.6),
     'L1_conv_D_skip': (1.0, 0.6),
     'L1_conv_ln2_g': (1.0, 0.2),
     'L1_conv_ln2_b': (0.0, 0.1),
     'L1_conv_b_out': (0.0, 0.1)}
    factors = {'L0_conv_qkv_w': 3.941,
     'L0_conv_lepe_w': 5.552,
     'L1_conv_w_x': 21.585,
     'L1_conv_w_dt': 26.838,
     'L1_conv_A_log': 35.99}
    for name, (base, spread) in spreads.items():
        noise = np.random.default_rng([zlib.crc32(name.encode()), seed]).standard_normal(out[name].shape)
        drawn = base * np.exp(spread * noise) if base else spread * noise
        out[name] = jnp.asarray(drawn.astype(out[name].dtype))
    for name, factor in factors.items():
        out[name] = (out[name] * factor).astype(out[name].dtype)
    return out
```

```python
from contextlib import ExitStack

import concourse.bass as bass
from concourse import mybir

F32 = mybir.dt.float32
BF16 = mybir.dt.bfloat16
I32 = mybir.dt.int32
U32 = mybir.dt.uint32
ALU = mybir.AluOpType
ACT = mybir.ActivationFunctionType
AX = mybir.AxisListType

P = 128
NB, H, W, C = 8, 56, 56, 256
NWIN = 7
WS = H // NWIN
WT = WS * WS
WPI = NWIN * NWIN
T = WS * W
STRIPS = NB * NWIN
NK = 4
TK = T // NK
CT = C // P
HEADS, DH = 8, 32
TOPK = 4
HID = 4 * C
HT = HID // P
SCALE = float(C) ** -0.5
DN = 512
DT = DN // P
NS = 64
RK = 16
EPS0, EPS1 = 1e-6, 1e-5
VROWS = H + WS
LK, CK = 5, 3
XROWS = H + 2
NWSUM = NWIN * CT


class Chain:

    def __init__(self, eng, sem, base):
        self.eng, self.sem, self.base, self.n = eng, sem, base, 0

    def link(self, instruction):
        self.n += 1
        instruction.then_inc(self.sem, 1)
        self.eng.wait_ge(self.sem, self.base + self.n)


def by_window(tokens):
    return tokens.rearrange("p (w h x) -> p h w x", w=NWIN, h=WS)


def columns(v, n):
    return v.rearrange("(t p) -> p t", p=P)


def load(eng, dst, src, sem):
    eng.dma_start(dst, src, allow_slow_non_contiguous=True).then_inc(sem, 16)


def make_identity(nc, pool, tile, cleared, done):
    nc.gpsimd.memset(tile[:, :], 0.0).then_inc(cleared, 1)
    pool.wait_ge(cleared, 1)
    nc.gpsimd.affine_select(out=tile[:, :], in_=tile[:, :], compare_op=ALU.not_equal, fill=1.0, base=0,
                            pattern=[[-1, P]], channel_multiplier=1).then_inc(done, 1)


def layernorm_stats(nc, chain, x, stats, mv, var_eps, eps, var_ready):
    for k in range(NK - 1):
        nc.vector.bn_stats(stats[:TK, k, :], x[:TK, k, :])
    chain.link(nc.vector.bn_stats(stats[:TK, NK - 1, :], x[:TK, NK - 1, :]))
    even, odd = stats[:TK, :, 1], stats[:TK, :, 4]
    nc.vector.tensor_tensor(mv[:TK, :, 0], even, odd, ALU.add)
    nc.vector.tensor_tensor(mv[:TK, :, 1], even, odd, ALU.subtract)
    chain.link(nc.vector.tensor_tensor(mv[:TK, :, 2], stats[:TK, :, 2], stats[:TK, :, 5], ALU.add))
    nc.vector.tensor_scalar(mv[:TK, :, 0], mv[:TK, :, 0], 0.5, None, ALU.mult)
    nc.vector.tensor_tensor(mv[:TK, :, 1], mv[:TK, :, 1], mv[:TK, :, 1], ALU.mult)
    chain.link(nc.vector.tensor_scalar(mv[:TK, :, 2], mv[:TK, :, 2], 1.0 / C, eps, ALU.mult, ALU.add))
    nc.vector.scalar_tensor_tensor(var_eps[:TK, :], mv[:TK, :, 1], 0.25, mv[:TK, :, 2], ALU.mult,
                                   ALU.add).then_inc(var_ready, 1)


def normalise(nc, x, xn, mv, rstd):
    for k in range(NK):
        last = nc.vector.tensor_scalar(xn[:TK, k, :], x[:TK, k, :], mv[:TK, k, 0:1], rstd[:TK, k:k + 1],
                                       ALU.subtract, ALU.mult)
    return last


def phase_qkv(nc, x, ln_g, ln_b, qkv_w, qkv_b, QT, KT, VT, VN, qsum, ksum):
    with ExitStack() as ctx:
        def sb(name, shape, dt=F32):
            return ctx.enter_context(nc.sbuf_tensor("a_" + name, shape, dt))

        def ps(name, shape, dt=F32):
            return ctx.enter_context(nc.psum_tensor("a_" + name, shape, dt))

        def sem(name):
            return ctx.enter_context(nc.semaphore("a_" + name))

        ident = sb("ident", [P, P])
        w_sb = sb("w", [P, CT, 3 * C])
        b_cols = sb("b_cols", [P, 3 * CT])
        vb_rows = sb("vb_rows", [P, C])
        g_cols = sb("g_cols", [P, CT])
        bb_cols = sb("bb_cols", [P, CT])
        zeros = sb("zeros", [P, NB * CT, 2 * W])
        half = sb("half", [P, NK])
        xin = [sb(f"xin{u}", [P, NK, C]) for u in range(2)]
        xn = [sb(f"xn{u}", [P, NK, C]) for u in range(2)]
        stats = sb("stats", [P, NK, 6])
        mv = sb("mv", [P, NK, 3])
        var_eps = sb("var_eps", [P, NK])
        rstd = sb("rstd", [P, NK])
        xnT = [sb(f"xnT{u}", [P, CT, T]) for u in range(2)]
        q_out = [sb(f"q_out{u}", [P, NWIN, CT, WT]) for u in range(2)]
        k_out = [sb(f"k_out{u}", [P, NWIN, CT, WT]) for u in range(2)]
        vT_out = [sb(f"vT_out{u}", [P, CT, T]) for u in range(2)]
        vn_out = [sb(f"vn_out{u}", [P, NK, C]) for u in range(2)]

        tp = ps("tp", [P, CT, 512])
        qkv_ps = ps("qkv_ps", [P, 3, 512])
        vn_ps = ps("vn_ps", [P, 2, 512])

        s_const = sem("s_const")
        s_clear = sem("s_clear")
        s_ident = sem("s_ident")
        s_zeros = sem("s_zeros")
        s_halo = sem("s_halo")
        x_loaded = [sem(f"x_loaded{u}") for u in range(2)]
        dve_chain = sem("dve_chain")
        var_ready = sem("var_ready")
        rstd_ready = sem("rstd_ready")
        xn_ready = sem("xn_ready")
        tp_ready = sem("tp_ready")
        xnT_ready = sem("xnT_ready")
        qkv_ready = sem("qkv_ready")
        qkv_free = sem("qkv_free")
        vn_ready = sem("vn_ready")
        vn_free = sem("vn_free")
        wsum_done = sem("wsum_done")
        stored = [sem(f"stored{u}") for u in range(2)]
        NCONST = 6
        NSTORE = 5
        PAIRS = STRIPS // 2
        block = ctx.enter_context(nc.Block())

        x_tiles = x.rearrange("b h w c -> (b h w) c").rearrange("(g k p) c -> g p k c", g=STRIPS, k=NK)
        kt_strips = KT.rearrange("(g w) p n -> g p w n", g=STRIPS)
        vn_rows = VN.rearrange("w t c -> (w t) c").rearrange("(g r) c -> g r c", g=STRIPS)
        full = (T // P) * P

        @block.sync
        def _(sp):
            sp.dma_start(w_sb[:, :, :], qkv_w.rearrange("(t p) n -> p t n", p=P)).then_inc(s_const, 16)
            load(sp, b_cols[:, :], columns(qkv_b, 3 * CT), s_const)
            sp.dma_start(vb_rows[:, :], qkv_b[2 * C:3 * C].rearrange("(a n) -> a n", a=1).broadcast_to([P, C])
                         ).then_inc(s_const, 16)
            load(sp, g_cols[:, :], columns(ln_g, CT), s_const)
            load(sp, bb_cols[:, :], columns(ln_b, CT), s_const)
            sp.dma_start(xin[0][:TK, :, :], x_tiles[0]).then_inc(x_loaded[0], 16)
            sp.dma_start(xin[1][:TK, :, :], x_tiles[1]).then_inc(x_loaded[1], 16)
            sp.wait_ge(s_zeros, 1)
            vt_img = VT.rearrange("b t p n -> p (b t) n")
            sp.dma_start(vt_img[:, :, 0:2 * W], zeros[:, :, :]).then_inc(s_halo, 16)
            sp.dma_start(vt_img[:, :, (H + 2) * W:(H + 4) * W], zeros[:, :, :]).then_inc(s_halo, 16)

            def strip(p, u, prefetch):
                g = 2 * p + u
                img = g // NWIN
                row = (g % NWIN) * T + 2 * W
                sp.wait_ge(qkv_free, 6 * g + 9)
                sp.dma_start(QT[bass.ds(g, 1)].rearrange("g p n -> p (g n)"),
                             q_out[u][:, :, :, :].rearrange("p w t n -> p (w t n)")).then_inc(stored[u], 16)
                sp.dma_start(kt_strips[bass.ds(g, 1)].rearrange("g p w n -> p (g w) n"),
                             k_out[u][:, :, :, :].rearrange("p w t n -> p w (t n)")).then_inc(stored[u], 16)
                sp.dma_start(VT[bass.ds(img, 1), :, :, bass.ds(row, T)].rearrange("b t p n -> p (b t) n"),
                             vT_out[u][:, :, :]).then_inc(stored[u], 16)
                sp.wait_ge(vn_free, 4 * g + 6)
                rows = vn_rows[bass.ds(g, 1)]
                sp.dma_start(rows[:, 0:full, :].rearrange("g (k p) c -> p (g k) c", p=P),
                             vn_out[u][:, 0:T // P, :]).then_inc(stored[u], 16)
                sp.dma_start(rows[:, full:T, :].rearrange("g r c -> (g r) c"),
                             vn_out[u][0:WT, T // P, :]).then_inc(stored[u], 16)
                if prefetch:
                    sp.wait_ge(xn_ready, g + 1)
                    sp.dma_start(xin[u][:TK, :, :],
                                 x_tiles[bass.ds(g + 2, 1)].rearrange("g p k c -> p (g k) c")
                                 ).then_inc(x_loaded[u], 16)

            with sp.Fori(0, PAIRS - 1) as p:
                for u in range(2):
                    strip(p, u, True)
            for u in range(2):
                strip(PAIRS - 1, u, False)
            sp.wait_ge(s_halo, 32)
            for u in range(2):
                sp.wait_ge(stored[u], 16 * NSTORE * PAIRS)

        @block.gpsimd
        def _(pool):
            make_identity(nc, pool, ident, s_clear, s_ident)
            nc.gpsimd.memset(half[:, :], -0.5).then_inc(s_clear, 1)
            nc.gpsimd.memset(zeros[:, :, :], 0.0).then_inc(s_zeros, 1)
            pool.wait_ge(s_clear, 2)
            with pool.Fori(0, STRIPS) as g:
                pool.wait_ge(var_ready, g + 1)
                nc.gpsimd.tensor_tensor(rstd[:TK, :], var_eps[:TK, :], half[:TK, :], ALU.pow).then_inc(rstd_ready, 1)

        @block.vector
        def _(dve):
            dve.wait_ge(s_const, 16 * (NCONST - 1))
            dve.sem_inc(vn_free, 2)

            def strip(p, u):
                g = 2 * p + u
                chain = Chain(dve, dve_chain, 3 * g)
                dve.wait_ge(x_loaded[u], 16 * p + 16)
                layernorm_stats(nc, chain, xin[u], stats, mv, var_eps, EPS0, var_ready)
                dve.wait_ge(rstd_ready, g + 1)
                dve.wait_ge(tp_ready, CT * g)
                normalise(nc, xin[u], xn[u], mv, rstd).then_inc(xn_ready, 1)
                dve.wait_ge(stored[u], 16 * NSTORE * p)
                for k in range(NK):
                    n = P if k < T // P else WT
                    dve.wait_ge(vn_ready, NK * g + k + 1)
                    nc.vector.tensor_tensor(vn_out[u][:n, k, :], vn_ps[:n, k % 2, :C], vb_rows[:n, :],
                                            ALU.add).then_inc(vn_free, 1)
                dve.wait_ge(qkv_free, 6 * g + 9)
                for src, dst in ((q_out, qsum), (k_out, ksum)):
                    nc.vector.tensor_reduce(dst[:, bass.ds(g * NWSUM, NWSUM)],
                                            src[u][:, :, :, :].rearrange("p w t n -> p (w t) n"), AX.X,
                                            ALU.add).then_inc(wsum_done, 1)

            with dve.Fori(0, PAIRS) as p:
                for u in range(2):
                    strip(p, u)

        @block.tensor
        def _(pe):
            pe.wait_ge(s_ident, 1)
            pe.wait_ge(s_const, 16 * (NCONST - 1))

            def strip(p, u):
                g = 2 * p + u
                pe.wait_ge(xn_ready, g + 1)
                pe.wait_ge(xnT_ready, CT * g)
                for ct in range(CT):
                    for k in range(NK):
                        last = nc.tensor.transpose(tp[:, ct, k * TK:(k + 1) * TK],
                                                   xn[u][:TK, k, ct * P:(ct + 1) * P], ident[:TK, :TK])
                    last.then_inc(tp_ready, 1)
                pe.wait_ge(xnT_ready, CT * g + CT)
                for m in range(3 * CT):
                    pe.wait_ge(qkv_free, 6 * g + m + 1)
                    for ct in range(CT):
                        last = nc.tensor.matmul(qkv_ps[:, m % 3, :T], w_sb[:, ct, m * P:(m + 1) * P],
                                                xnT[u][:, ct, :], start=ct == 0, stop=ct == CT - 1)
                    last.then_inc(qkv_ready, 1)
                for k in range(NK):
                    n = 2 if k < T // P else 1
                    pe.wait_ge(vn_free, NK * g + k + 1)
                    for ct in range(CT):
                        tokens = xnT[u][:, ct, 2 * k * WT:(2 * k + n) * WT]
                        last = nc.tensor.matmul(vn_ps[:n * WT, k % 2, :C], tokens, w_sb[:, ct, 2 * C:3 * C],
                                                start=ct == 0, stop=ct == CT - 1)
                    last.then_inc(vn_ready, 1)

            with pe.Fori(0, PAIRS) as p:
                for u in range(2):
                    strip(p, u)

        @block.scalar
        def _(act):
            act.wait_ge(s_const, 16 * (NCONST - 1))
            act.sem_inc(qkv_free, 3)

            def strip(p, u):
                g = 2 * p + u
                act.wait_ge(vn_ready, NK * g)
                for ct in range(CT):
                    act.wait_ge(tp_ready, CT * g + ct + 1)
                    nc.scalar.activation(by_window(xnT[u][:, ct, :]), tp[:, ct, :T], ACT.Identity,
                                         bias=bb_cols[:, ct:ct + 1], scale=g_cols[:, ct:ct + 1]
                                         ).then_inc(xnT_ready, 1)
                act.wait_ge(stored[u], 16 * NSTORE * p)
                act.wait_ge(wsum_done, 2 * g)
                for m in range(3 * CT):
                    act.wait_ge(qkv_ready, 6 * g + m + 1)
                    if m < 2 * CT:
                        out, src = (q_out, k_out)[m // CT][u][:, :, m % CT, :], qkv_ps[:, m % 3, :T]
                    else:
                        out, src = vT_out[u][:, m % CT, :], by_window(qkv_ps[:, m % 3, :T])
                    nc.scalar.activation(out, src, ACT.Identity, bias=b_cols[:, m:m + 1]).then_inc(qkv_free, 1)

            with act.Fori(0, PAIRS) as p:
                for u in range(2):
                    strip(p, u)


def phase_route(nc, qsum, ksum, IDX):
    with ExitStack() as ctx:
        def sb(name, shape, dt=F32):
            return ctx.enter_context(nc.sbuf_tensor("r_" + name, shape, dt))

        def sem(name):
            return ctx.enter_context(nc.semaphore("r_" + name))

        logits_ps = ctx.enter_context(nc.psum_tensor("r_logits_ps", [P, NB, 512], F32))
        qmean = sb("qmean", [P, STRIPS * NWIN, CT])
        kmean = sb("kmean", [P, STRIPS * NWIN, CT])
        logits = sb("logits", [P, NB, WPI])
        top = sb("top", [P, NB, 8])
        top_at = sb("top_at", [P, NB, 8], U32)
        idx = sb("idx", [P, NB, TOPK], I32)
        means = sem("means")
        scored = sem("scored")
        chained = sem("chained")
        picked = sem("picked")
        stored = sem("stored")
        block = ctx.enter_context(nc.Block())

        @block.vector
        def _(dve):
            nc.vector.tensor_scalar(qmean[:, :, :].rearrange("p w t -> p (w t)"), qsum[:, :], 1.0 / WT, SCALE,
                                    ALU.mult, ALU.mult).then_inc(means, 1)
            nc.vector.tensor_scalar(kmean[:, :, :].rearrange("p w t -> p (w t)"), ksum[:, :], 1.0 / WT, None,
                                    ALU.mult).then_inc(means, 1)
            chain = Chain(dve, chained, 0)
            dve.wait_ge(scored, 1)
            chain.link(nc.vector.tensor_copy(logits[:WPI, :, :], logits_ps[:WPI, :, :WPI]))
            for b in range(NB):
                chain.link(nc.vector.max(top[:WPI, b, :], logits[:WPI, b, :]))
                chain.link(nc.vector.max_index(top_at[:WPI, b, :], top[:WPI, b, :], logits[:WPI, b, :]))
                nc.vector.tensor_scalar(idx[:WPI, b, :], top_at[:WPI, b, :TOPK], float(b * WPI), None,
                                        ALU.add).then_inc(picked, 1)

        @block.tensor
        def _(pe):
            pe.wait_ge(means, 2)
            for b in range(NB):
                for ct in range(CT):
                    last = nc.tensor.matmul(logits_ps[:WPI, b, :WPI], qmean[:, b * WPI:(b + 1) * WPI, ct],
                                            kmean[:, b * WPI:(b + 1) * WPI, ct], start=ct == 0, stop=ct == CT - 1)
            last.then_inc(scored, 1)

        @block.sync
        def _(sp):
            sp.wait_ge(picked, NB)
            sp.dma_start(IDX.rearrange("b w k -> w b k"), idx[:WPI, :, :]).then_inc(stored, 16)
            sp.wait_ge(stored, 16)


def phase_attention(nc, x, QT, KT, VT, VN, IDX, lepe_w, lepe_b, wo_w, wo_b, ln2_g, ln2_b, w1, b1, w2, b2,
                    l1_g, l1_b, w_in, b_in, X2, XI):
    with ExitStack() as ctx:
        def sb(name, shape, dt=F32):
            return ctx.enter_context(nc.sbuf_tensor("b_" + name, shape, dt))

        def ps(name, shape, dt=F32):
            return ctx.enter_context(nc.psum_tensor("b_" + name, shape, dt))

        def sem(name):
            return ctx.enter_context(nc.semaphore("b_" + name))

        PAIRS = STRIPS // 2
        NPAIR = HEADS // 2
        NKEY = TOPK * WT
        TAPS = LK * LK
        ident = sb("ident", [P, P])
        half = sb("half", [P, NK])
        zeros = sb("zeros", [P, NB * DT, W])
        idx = sb("idx", [1, STRIPS * NWIN * TOPK], I32)
        lepe_k = sb("lepe_k", [P, CT, TAPS])
        lepe_bias = sb("lepe_bias", [P, CT])
        wo_sb = sb("wo_sb", [P, CT, C])
        wob_rows = sb("wob_rows", [P, C])
        g2 = sb("g2", [P, CT])
        bb2 = sb("bb2", [P, CT])
        w1_sb = sb("w1_sb", [P, CT, HID])
        b1_cols = sb("b1_cols", [P, HT])
        w2_sb = sb("w2_sb", [P, HT, C])
        b2_rows = sb("b2_rows", [P, C])
        g3 = sb("g3", [P, CT])
        bb3 = sb("bb3", [P, CT])
        win_sb = sb("win_sb", [P, CT, DN])
        bin_cols = sb("bin_cols", [P, DT])

        xr = [sb(f"xr{u}", [P, NK, C]) for u in range(2)]
        q_blk = [sb(f"q_blk{u}", [P, NWIN, CT, 4, WT]) for u in range(2)]
        v_halo = sb("v_halo", [P, CT, (WS + LK - 1) * W])
        k_sel = [sb(f"k_sel{w}", [P, TOPK, CT, WT]) for w in range(2)]
        v_sel = [sb(f"v_sel{w}", [P, TOPK // 2, C]) for w in range(2)]
        row_max = sb("row_max", [P, 2, NPAIR])
        neg_max = sb("neg_max", [P, 2, NPAIR])
        row_sum = sb("row_sum", [P, 2, NPAIR])
        inv_sum = sb("inv_sum", [P, 2, NPAIR])
        probs = [sb(f"probs{w}", [P, NPAIR, NKEY]) for w in range(2)]
        probsT = [sb(f"probsT{w}", [P, 2, NPAIR, P]) for w in range(2)]
        attn = sb("attn", [P, CT, T])
        lepe = sb("lepe", [P, CT, T])
        stats = sb("stats", [P, NK, 6])
        mv = sb("mv", [P, NK, 3])
        var_eps = sb("var_eps", [P, NK])
        rstd = sb("rstd", [P, NK])
        xn = sb("xn", [P, NK, C])
        xnT = sb("xnT", [P, CT, T])
        hid = sb("hid", [P, HT, T])
        xi = sb("xi", [P, DT, T])

        scores = [ps(f"scores{w}", [P, 2, 512]) for w in range(2)]
        pt = ps("pt", [P, 2, 512])
        oT = ps("oT", [P, CT, 4 * WT])

        s_const = sem("s_const")
        s_clear = sem("s_clear")
        s_ident = sem("s_ident")
        s_zeros = sem("s_zeros")
        s_halo = sem("s_halo")
        q_zeroed = sem("q_zeroed")
        s_idx = sem("s_idx")
        x_loaded = [sem(f"x_loaded{u}") for u in range(2)]
        q_loaded = [sem(f"q_loaded{u}") for u in range(2)]
        v_loaded = sem("v_loaded")
        k_loaded = [sem(f"k_loaded{w}") for w in range(2)]
        vsel_loaded = [sem(f"vsel_loaded{w}") for w in range(2)]
        scored = sem("scored")
        negmax_ready = sem("negmax_ready")
        exp_done = sem("exp_done")
        probs_ready = sem("probs_ready")
        pt_ready = sem("pt_ready")
        pt_acted = sem("pt_acted")
        pt_veced = sem("pt_veced")
        oT_ready = sem("oT_ready")
        oT_taken = sem("oT_taken")
        dve_chain = sem("dve_chain")
        biased = sem("biased")
        attn_ready = sem("attn_ready")
        y_ready = sem("y_ready")
        var_ready = sem("var_ready")
        rstd_ready = sem("rstd_ready")
        xn_ready = sem("xn_ready")
        tp_ready = sem("tp_ready")
        xnT_ready = sem("xnT_ready")
        hid_scored = sem("hid_scored")
        hid_ready = sem("hid_ready")
        mlp_ready = sem("mlp_ready")
        x2_ready = sem("x2_ready")
        xi_scored = sem("xi_scored")
        xi_ready = sem("xi_ready")
        x2_stored = [sem(f"x2_stored{u}") for u in range(2)]
        xi_stored = sem("xi_stored")
        block = ctx.enter_context(nc.Block())

        x_tiles = x.rearrange("b h w c -> (b h w) c").rearrange("(g k p) c -> g p k c", g=STRIPS, k=NK)
        qt_heads = QT.rearrange("g (a d) (w t n) -> g a d w t n", a=4, w=NWIN, t=CT)

        consts = [
            (lepe_k, lepe_w.rearrange("a b o (t p) -> p t (a b o)", p=P)),
            (lepe_bias, columns(lepe_b, CT)),
            (wo_sb, wo_w.rearrange("(t p) n -> p t n", p=P)),
            (wob_rows, wo_b.rearrange("(a n) -> a n", a=1).broadcast_to([P, C])),
            (g2, columns(ln2_g, CT)),
            (bb2, columns(ln2_b, CT)),
            (w1_sb, w1.rearrange("(t p) n -> p t n", p=P)),
            (b1_cols, columns(b1, HT)),
            (w2_sb, w2.rearrange("(t p) n -> p t n", p=P)),
            (b2_rows, b2.rearrange("(a n) -> a n", a=1).broadcast_to([P, C])),
            (g3, columns(l1_g, CT)),
            (bb3, columns(l1_b, CT)),
            (win_sb, w_in.rearrange("(t p) n -> p t n", p=P)),
            (bin_cols, columns(b_in, DT)),
        ]
        NCONST = len(consts) + CT - 1

        def turn(p, u, i):
            return 7 * p + (7 * u + i) // 2

        @block.sync
        def _(sp):
            sp.dma_start(idx[:, :], IDX.rearrange("b w k -> (b w k)").rearrange("(a n) -> a n", a=1)
                         ).then_inc(s_idx, 16)
            for t in range(CT):
                load(sp, lepe_k[:, t, :], lepe_w.rearrange("a b o (t p) -> t p (a b o)", p=P)[t], s_const)
            for dst, src in consts[1:]:
                load(sp, dst[(slice(None),) * len(dst.shape)], src, s_const)
            sp.wait_ge(s_zeros, 1)
            xi_img = XI.rearrange("b t p n -> p (b t) n")
            sp.dma_start(xi_img[:, :, 0:W], zeros[:, :, :]).then_inc(s_halo, 16)
            sp.dma_start(xi_img[:, :, (H + 1) * W:XROWS * W], zeros[:, :, :]).then_inc(s_halo, 16)
            sp.wait_ge(s_idx, 16)
            sp.wait_ge(q_zeroed, 2)

            def strip(p, u):
                g = 2 * p + u
                img = g // NWIN
                row = (g % NWIN) * T
                sp.wait_ge(x2_stored[u], 16 * p)
                sp.dma_start(xr[u][:TK, :, :], x_tiles[bass.ds(g, 1)].rearrange("g p k c -> p (g k) c")
                             ).then_inc(x_loaded[u], 16)
                for a in range(4):
                    for t in range(CT):
                        sp.dma_start(q_blk[u][a * DH:(a + 1) * DH, :, t, a, :],
                                     qt_heads[bass.ds(g, 1), a, :, :, t, :].rearrange("g d w n -> d (g w) n")
                                     ).then_inc(q_loaded[u], 16)
                sp.wait_ge(attn_ready, g)
                sp.dma_start(v_halo[:, :, :],
                             VT[bass.ds(img, 1), :, :, bass.ds(row, (WS + LK - 1) * W)]
                             .rearrange("b t p n -> p (b t) n")).then_inc(v_loaded, 16)
                for i in range(NWIN):
                    w = (7 * u + i) % 2
                    wins = [sp.value_load(idx[0:1, bass.ds(g * (NWIN * TOPK) + (i * TOPK + s), 1)],
                                          min_val=0, max_val=NB * WPI - 1) for s in range(TOPK)]
                    sp.wait_ge(scored, 7 * g + i - 1 if u or i else 7 * g)
                    for s, win in enumerate(wins):
                        sp.dma_start(k_sel[w][:, s, :, :].rearrange("p t n -> p (t n)"),
                                     KT[bass.ds(win, 1)].rearrange("w p n -> p (w n)")
                                     ).then_inc(k_loaded[w], 16)
                    sp.wait_ge(oT_ready, 7 * g + i - 1 if u or i else 7 * g)
                    for s, win in enumerate(wins):
                        sp.dma_start(v_sel[w][(s % 2) * WT:(s % 2 + 1) * WT, s // 2, :],
                                     VN[bass.ds(win, 1)].rearrange("w t c -> t (w c)")
                                     ).then_inc(vsel_loaded[w], 16)
                sp.wait_ge(x2_ready, g + 1)
                sp.dma_start(X2[bass.ds(g, 1)].rearrange("g p n -> p (g n)"),
                             xr[u][:TK, :, :].rearrange("p k c -> p (k c)")).then_inc(x2_stored[u], 16)
                sp.wait_ge(xi_ready, DT * g + DT)
                sp.dma_start(XI[bass.ds(img, 1), :, :, bass.ds(row + W, T)].rearrange("b t p n -> p (b t) n"),
                             xi[:, :, :]).then_inc(xi_stored, 16)

            with sp.Fori(0, PAIRS) as p:
                for u in range(2):
                    strip(p, u)
            sp.wait_ge(s_halo, 32)
            sp.wait_ge(xi_stored, 16 * STRIPS)
            for u in range(2):
                sp.wait_ge(x2_stored[u], 16 * PAIRS)

        @block.gpsimd
        def _(pool):
            make_identity(nc, pool, ident, s_clear, s_ident)
            nc.gpsimd.memset(half[:, :], -0.5).then_inc(s_clear, 1)
            nc.gpsimd.memset(zeros[:, :, :], 0.0).then_inc(s_zeros, 1)
            for u in range(2):
                nc.gpsimd.memset(q_blk[u][:, :, :, :, :], 0.0).then_inc(q_zeroed, 1)
            pool.wait_ge(s_const, 16 * NCONST)
            pool.wait_ge(s_clear, 2)

            def strip(p, u):
                g = 2 * p + u
                pool.wait_ge(x_loaded[u], 16 * p + 16)
                nc.gpsimd.tensor_tensor(xr[u][:TK, :, :], xr[u][:TK, :, :],
                                        wob_rows[:TK, :].rearrange("p (a n) -> p a n", a=1).broadcast_to([TK, NK, C]),
                                        ALU.add).then_inc(biased, 1)
                pool.wait_ge(var_ready, 2 * g + 1)
                nc.gpsimd.tensor_tensor(rstd[:TK, :], var_eps[:TK, :], half[:TK, :], ALU.pow).then_inc(rstd_ready, 1)
                pool.wait_ge(xn_ready, 2 * g + 1)
                nc.gpsimd.tensor_tensor(xr[u][:TK, :, :], xr[u][:TK, :, :],
                                        b2_rows[:TK, :].rearrange("p (a n) -> p a n", a=1).broadcast_to([TK, NK, C]),
                                        ALU.add).then_inc(biased, 1)
                pool.wait_ge(var_ready, 2 * g + 2)
                nc.gpsimd.tensor_tensor(rstd[:TK, :], var_eps[:TK, :], half[:TK, :], ALU.pow).then_inc(rstd_ready, 1)

            with pool.Fori(0, PAIRS) as p:
                for u in range(2):
                    strip(p, u)

        @block.vector
        def _(dve):
            dve.wait_ge(s_const, 16 * NCONST)

            def lepe_taps(first, last, chain):
                order = [(LK // 2, LK // 2)] + [(a, b) for a in range(LK) for b in range(LK)
                                                if (a, b) != (LK // 2, LK // 2)]
                for n in range(first, last):
                    a, b = order[n]
                    dx = b - LK // 2
                    lo, hi = max(0, -dx), min(W, W - dx)
                    for t in range(CT):
                        grid = lepe[:, t, :].rearrange("p (h w) -> p h w", h=WS)[:, :, lo:hi]
                        src = v_halo[:, t, :].rearrange("p (h w) -> p h w", w=W)[:, a:a + WS, lo + dx:hi + dx]
                        tap = lepe_k[:, t, a * LK + b:a * LK + b + 1]
                        if n == 0:
                            step = nc.vector.tensor_scalar(grid, src, tap, lepe_bias[:, t:t + 1], ALU.mult, ALU.add)
                        else:
                            step = nc.vector.scalar_tensor_tensor(grid, src, tap, grid, ALU.mult, ALU.add)
                    chain.link(step)

            def window_max(g, i, w):
                dve.wait_ge(scored, 7 * g + i + 1)
                chain_max = row_max[:, w, :]
                nc.vector.tensor_reduce(chain_max, scores[w][:, :, :].rearrange("p a (b n) -> p (a b) n", b=2),
                                        AX.X, ALU.max)

            def strip(p, u):
                g = 2 * p + u
                TAPCUTS = [0, 3, 7, 11, 15, 18, 22, TAPS]
                links = NWIN * 2 + TAPS + 7
                chain = Chain(dve, dve_chain, links * g)

                def max_of(i):
                    w = (7 * u + i) % 2
                    dve.wait_ge(scored, 7 * g + i + 1)
                    chain.link(nc.vector.tensor_reduce(
                        row_max[:, w, :], scores[w][:, :, :].rearrange("p a (b n) -> p (a b) n", b=2), AX.X, ALU.max))
                    nc.vector.tensor_scalar(neg_max[:, w, :], row_max[:, w, :], -SCALE, None,
                                            ALU.mult).then_inc(negmax_ready, 1)

                max_of(0)
                max_of(1)
                for i in range(NWIN):
                    w = (7 * u + i) % 2
                    dve.wait_ge(exp_done, 7 * g + i + 1)
                    chain.link(nc.vector.reciprocal(inv_sum[:, w, :], row_sum[:, w, :]))
                    for j in range(NPAIR):
                        last = nc.vector.tensor_scalar(probs[w][:, j, :], probs[w][:, j, :], inv_sum[:, w, j:j + 1],
                                                       None, ALU.mult)
                    last.then_inc(probs_ready, 1)
                    if i == 0:
                        dve.wait_ge(v_loaded, 16 * g + 16)
                    lepe_taps(TAPCUTS[i], TAPCUTS[i + 1], chain)
                    dve.wait_ge(pt_ready, 14 * g + 2 * i + 2)
                    nc.vector.tensor_copy(probsT[w][:, 1, :, :].rearrange("p j q -> p (j q)"),
                                          pt[:, 1, :]).then_inc(pt_veced, 1)
                    if i + 2 < NWIN:
                        max_of(i + 2)
                    dve.wait_ge(oT_ready, 7 * g + i + 1)
                    if i == 0:
                        dve.wait_ge(y_ready, g)
                    out = attn[:, :, :].rearrange("p t (h w x) -> p t w h x", h=WS, w=NWIN)[:, :, i]
                    last = nc.vector.tensor_copy(out, oT[:, :, :WT].rearrange("p t (h x) -> p t h x", h=WS))
                    last.then_inc(oT_taken, 1)
                dve.wait_ge(oT_taken, 7 * g + NWIN)
                nc.vector.tensor_tensor(attn[:, :, :], attn[:, :, :], lepe[:, :, :], ALU.add).then_inc(attn_ready, 1)
                dve.wait_ge(y_ready, g + 1)
                dve.wait_ge(biased, 2 * g + 1)
                chain.link(nc.vector.tensor_tensor(
                    xr[u][:TK, :, :], xr[u][:TK, :, :],
                    scores[0][:TK, :, :].rearrange("p a (b n) -> p (a b) n", b=2), ALU.add))
                layernorm_stats(nc, chain, xr[u], stats, mv, var_eps, EPS0, var_ready)
                dve.wait_ge(rstd_ready, 2 * g + 1)
                dve.wait_ge(tp_ready, 4 * g)
                normalise(nc, xr[u], xn, mv, rstd).then_inc(xn_ready, 1)
                dve.wait_ge(mlp_ready, g + 1)
                dve.wait_ge(biased, 2 * g + 2)
                nc.vector.tensor_tensor(xr[u][:TK, :, :], xr[u][:TK, :, :],
                                        pt[:TK, :, :].rearrange("p a (b n) -> p (a b) n", b=2),
                                        ALU.add).then_inc(x2_ready, 1)
                dve.wait_ge(x2_ready, g + 1)
                layernorm_stats(nc, chain, xr[u], stats, mv, var_eps, EPS1, var_ready)
                dve.wait_ge(rstd_ready, 2 * g + 2)
                dve.wait_ge(tp_ready, 4 * g + 2)
                normalise(nc, xr[u], xn, mv, rstd).then_inc(xn_ready, 1)
                assert chain.n == links, chain.n

            with dve.Fori(0, PAIRS) as p:
                for u in range(2):
                    strip(p, u)

        @block.tensor
        def _(pe):
            pe.wait_ge(s_ident, 1)
            pe.wait_ge(s_const, 16 * NCONST)

            def strip(p, u):
                g = 2 * p + u

                def score(i):
                    w = (7 * u + i) % 2
                    pe.wait_ge(k_loaded[w], 16 * TOPK * turn(p, u, i) + 16 * TOPK)
                    if i < 2:
                        pe.wait_ge(xi_ready, DT * g)
                    else:
                        pe.wait_ge(exp_done, 7 * g + i - 1)
                    for j in range(NPAIR):
                        t = j // 2
                        last = nc.tensor.matmul(
                            scores[w][:, j // 2, (j % 2) * NKEY:(j % 2 + 1) * NKEY],
                            q_blk[u][:, i, t, 2 * (j % 2):2 * (j % 2) + 2, :],
                            k_sel[w][:, :, t, :], start=True, stop=True)
                    last.then_inc(scored, 1)

                def transpose_probs(i):
                    w = (7 * u + i) % 2
                    pe.wait_ge(probs_ready, 7 * g + i + 1)
                    pe.wait_ge(pt_acted, 7 * g + i)
                    pe.wait_ge(pt_veced, 7 * g + i)
                    for kk in range(2):
                        for j in range(NPAIR):
                            last = nc.tensor.transpose(pt[:, kk, j * P:(j + 1) * P],
                                                       probs[w][:, j, kk * P:(kk + 1) * P], ident[:, :])
                        last.then_inc(pt_ready, 1)

                def attend(i):
                    w = (7 * u + i) % 2
                    pe.wait_ge(pt_acted, 7 * g + i + 1)
                    pe.wait_ge(pt_veced, 7 * g + i + 1)
                    pe.wait_ge(oT_taken, 7 * g + i)
                    pe.wait_ge(vsel_loaded[w], 16 * TOPK * turn(p, u, i) + 16 * TOPK)
                    for h in range(HEADS):
                        a, t = h % 4, h // 4
                        for kk in range(2):
                            last = nc.tensor.matmul(
                                oT[a * DH:(a + 1) * DH, t, :WT], v_sel[w][:, kk, h * DH:(h + 1) * DH],
                                probsT[w][:, kk, h // 2, (h % 2) * WT:(h % 2 + 1) * WT],
                                start=kk == 0, stop=kk == 1)
                    last.then_inc(oT_ready, 1)

                pe.wait_ge(q_loaded[u], 16 * 8 * p + 16 * 8)
                score(0)
                score(1)
                for i in range(NWIN):
                    transpose_probs(i)
                    if i + 2 < NWIN:
                        score(i + 2)
                    attend(i)
                pe.wait_ge(attn_ready, g + 1)
                for k in range(NK):
                    for t in range(CT):
                        last = nc.tensor.matmul(scores[0][:TK, k // 2, (k % 2) * C:(k % 2 + 1) * C],
                                                attn[:, t, k * TK:(k + 1) * TK], wo_sb[:, t, :],
                                                start=t == 0, stop=t == CT - 1)
                last.then_inc(y_ready, 1)

                def transpose_xn(n, dst):
                    pe.wait_ge(xn_ready, 2 * g + n)
                    for ct in range(CT):
                        for k in range(NK):
                            last = nc.tensor.transpose(dst[:, ct, k * TK:(k + 1) * TK],
                                                       xn[:TK, k, ct * P:(ct + 1) * P], ident[:TK, :TK])
                        last.then_inc(tp_ready, 1)

                transpose_xn(1, pt)
                pe.wait_ge(xnT_ready, 4 * g + 2)
                banks = [scores[0][:, 0, :], scores[0][:, 1, :], scores[1][:, 0, :], scores[1][:, 1, :]]
                for m in range(HT):
                    if m >= 4:
                        pe.wait_ge(hid_ready, HT * g + m - 3)
                    for ct in range(CT):
                        last = nc.tensor.matmul(banks[m % 4][:, :T], w1_sb[:, ct, m * P:(m + 1) * P],
                                                xnT[:, ct, :], start=ct == 0, stop=ct == CT - 1)
                    last.then_inc(hid_scored, 1)
                pe.wait_ge(hid_ready, HT * g + HT)
                for k in range(NK):
                    for m in range(HT):
                        last = nc.tensor.matmul(pt[:TK, k // 2, (k % 2) * C:(k % 2 + 1) * C],
                                                hid[:, m, k * TK:(k + 1) * TK], w2_sb[:, m, :],
                                                start=m == 0, stop=m == HT - 1)
                last.then_inc(mlp_ready, 1)
                transpose_xn(2, scores[0])
                pe.wait_ge(xnT_ready, 4 * g + 4)
                banks = [scores[1][:, 0, :], scores[1][:, 1, :], pt[:, 0, :], pt[:, 1, :]]
                for m in range(DT):
                    for ct in range(CT):
                        last = nc.tensor.matmul(banks[m][:, :T], win_sb[:, ct, m * P:(m + 1) * P],
                                                xnT[:, ct, :], start=ct == 0, stop=ct == CT - 1)
                    last.then_inc(xi_scored, 1)

            with pe.Fori(0, PAIRS) as p:
                for u in range(2):
                    strip(p, u)

        @block.scalar
        def _(act):
            act.wait_ge(s_const, 16 * NCONST)

            def strip(p, u):
                g = 2 * p + u

                def exps(i):
                    w = (7 * u + i) % 2
                    act.wait_ge(negmax_ready, 7 * g + i + 1)
                    act.wait_ge(pt_ready, 14 * g + 2 * i - 2 if u or i else 14 * g)
                    for j in range(NPAIR):
                        last = nc.scalar.activation(
                            probs[w][:, j, :], scores[w][:, j // 2, (j % 2) * NKEY:(j % 2 + 1) * NKEY], ACT.Exp,
                            bias=neg_max[:, w, j:j + 1], scale=SCALE, accum_out=row_sum[:, w, j:j + 1])
                    last.then_inc(exp_done, 1)

                exps(0)
                for i in range(NWIN):
                    w = (7 * u + i) % 2
                    if i + 1 < NWIN:
                        exps(i + 1)
                    act.wait_ge(pt_ready, 14 * g + 2 * i + 1)
                    nc.scalar.activation(probsT[w][:, 0, :, :].rearrange("p j q -> p (j q)"), pt[:, 0, :],
                                         ACT.Copy).then_inc(pt_acted, 1)

                def affine(n, src, gain, shift):
                    for ct in range(CT):
                        act.wait_ge(tp_ready, 4 * g + 2 * n + ct + 1)
                        nc.scalar.activation(xnT[:, ct, :], src[:, ct, :T], ACT.Identity,
                                             bias=shift[:, ct:ct + 1], scale=gain[:, ct:ct + 1]
                                             ).then_inc(xnT_ready, 1)

                act.wait_ge(xi_scored, DT * g)
                affine(0, pt, g2, bb2)
                banks = [scores[0][:, 0, :], scores[0][:, 1, :], scores[1][:, 0, :], scores[1][:, 1, :]]
                act.wait_ge(mlp_ready, g)
                for m in range(HT):
                    act.wait_ge(hid_scored, HT * g + m + 1)
                    nc.scalar.activation(hid[:, m, :], banks[m % 4][:, :T], ACT.Gelu,
                                         bias=b1_cols[:, m:m + 1]).then_inc(hid_ready, 1)
                affine(1, scores[0], g3, bb3)
                banks = [scores[1][:, 0, :], scores[1][:, 1, :], pt[:, 0, :], pt[:, 1, :]]
                act.wait_ge(xi_stored, 16 * g)
                for m in range(DT):
                    act.wait_ge(xi_scored, DT * g + m + 1)
                    nc.scalar.activation(xi[:, m, :], banks[m][:, :T], ACT.Identity,
                                         bias=bin_cols[:, m:m + 1]).then_inc(xi_ready, 1)

            with act.Fori(0, PAIRS) as p:
                for u in range(2):
                    strip(p, u)


def phase_scan(nc, a, X2, XI, out):
    with ExitStack() as ctx:
        def sb(name, shape, dt=F32):
            return ctx.enter_context(nc.sbuf_tensor("c_" + name, shape, dt))

        def ps(name, shape, dt=F32):
            return ctx.enter_context(nc.psum_tensor("c_" + name, shape, dt))

        def sem(name):
            return ctx.enter_context(nc.semaphore("c_" + name))

        BB, CC, DTR, DT0, PRO = DT, DT + 1, DT + 2, DT + 3, DT + 3 + DT
        MEAN, VAR, WO, EPI = 0, 1, 2, 4
        A_LOG_MAX = 80.0
        TAPS = CK * CK
        T1 = T + 1

        ident = sb("ident", [P, P])
        ident_b = sb("ident_b", [P, P], BF16)
        hilo_b = sb("hilo_b", [P, NS], BF16)
        averager = sb("averager", [P, P])
        eps_col = sb("eps_col", [P, 1])
        ones_row = sb("ones_row", [1, TK])
        keep = sb("keep", [P, STRIPS])
        keep_now = [sb(f"keep_now{u}", [P, 1]) for u in range(2)]
        conv_k = sb("conv_k", [P, DT, TAPS])
        conv_diag = sb("conv_diag", [P, TAPS, DT, P])
        conv_bias = sb("conv_bias", [P, DT])
        wx_sb = sb("wx_sb", [P, DT, 4 * NS + RK])
        wdt_sb = sb("wdt_sb", [RK, DN])
        dt_bias = sb("dt_bias", [P, DT])
        A_sb = sb("A_sb", [P, DT, NS])
        D_cols = sb("D_cols", [P, DT])
        g_cols = sb("g_cols", [P, DT])
        b_cols = sb("b_cols", [P, DT])
        wout_sb = sb("wout_sb", [P, DT, C])
        bout_row = sb("bout_row", [1, C])

        x_halo = sb("x_halo", [P, DT, (WS + CK - 1) * W])
        xres = [sb(f"xres{u}", [P, NK, C]) for u in range(2)]
        xg = [sb(f"xg{u}", [P, DT, T]) for u in range(2)]
        dt = [sb(f"dt{u}", [P, DT, T]) for u in range(2)]
        dtx = [sb(f"dtx{u}", [P, DT, T]) for u in range(2)]
        pack = [[sb(f"pack{s}{u}", [P, T], BF16) for u in range(2)] for s in "BC"]
        low = [sb(f"low{u}", [P, T], BF16) for u in range(2)]
        rest = sb("rest", [P, T])
        mid = sb("mid", [P, T], BF16)
        dt_low = sb("dt_low", [RK, T])
        tmp = [sb(f"tmp{n}", [P, DT, T]) for n in range(4)]
        std = sb("std", [P, T])

        dA = [sb(f"dA{v}", [P, DT, T1]) for v in range(2)]
        wB = [sb(f"wB{v}", [P, DT, T1]) for v in range(2)]
        hs = [sb(f"hs{v}", [P, DT, T1]) for v in range(2)]
        hC = [sb(f"hC{v}", [P, DT, T]) for v in range(2)]
        Csb = [sb(f"Csb{v}", [P, T]) for v in range(2)]
        carry = sb("carry", [P, NS, DT])

        y_ps = ps("y_ps", [P, DT, 512])
        b_ps = ps("b_ps", [P, 2, 512])
        c_ps = ps("c_ps", [P, 512])
        aux = ps("aux", [P, 512])

        s_const = sem("s_const")
        s_clear = sem("s_clear")
        s_ready = sem("s_ready")
        diag_ready = sem("diag_ready")
        a_capped = sem("a_capped")
        a_exp = sem("a_exp")
        a_ready = sem("a_ready")
        halo_loaded = sem("halo_loaded")
        res_loaded = [sem(f"res_loaded{u}") for u in range(2)]
        out_stored = [sem(f"out_stored{u}") for u in range(2)]
        pro_full = sem("pro_full")
        pro_free = sem("pro_free")
        epi_full = sem("epi_full")
        epi_free = sem("epi_free")
        pack_ready = sem("pack_ready")
        mid_ready = sem("mid_ready")
        low_ready = sem("low_ready")
        pack_done = sem("pack_done")
        act_chain = sem("act_chain")
        soft_ready = sem("soft_ready")
        dve_chain = sem("dve_chain")
        dt_ready = sem("dt_ready")
        dtx_ready = sem("dtx_ready")
        keep_ready = sem("keep_ready")
        B_ready = sem("B_ready")
        C_ready = sem("C_ready")
        C_copied = sem("C_copied")
        wB_ready = sem("wB_ready")
        in_ready = sem("in_ready")
        dA_ready = sem("dA_ready")
        scanned = sem("scanned")
        carried = sem("carried")
        hC_ready = sem("hC_ready")
        summed = sem("summed")
        yv_ready = sem("yv_ready")
        sq_ready = sem("sq_ready")
        rs_ready = sem("rs_ready")
        yn_ready = sem("yn_ready")
        yo_ready = sem("yo_ready")
        block = ctx.enter_context(nc.Block())

        x2_tiles = X2.rearrange("g p (k c) -> g p k c", k=NK)
        out_tiles = out.rearrange("b h w c -> (b h w) c").rearrange("(g k p) c -> g p k c", g=STRIPS, k=NK)
        w_x, RN = a["L1_conv_w_x"].rearrange("(t p) n -> p t n", p=P), RK + NS
        consts = [
            (conv_bias[:, :], columns(a["L1_conv_conv_b"], DT)),
            (wx_sb[:, :, 0:NS], w_x[:, :, RK:RN]),
            (wx_sb[:, :, NS:2 * NS], w_x[:, :, RK:RN]),
            (wx_sb[:, :, 2 * NS:3 * NS], w_x[:, :, RN:RN + NS]),
            (wx_sb[:, :, 3 * NS:4 * NS], w_x[:, :, RN:RN + NS]),
            (wx_sb[:, :, 4 * NS:], w_x[:, :, 0:RK]),
            (wdt_sb[:, :], a["L1_conv_w_dt"]),
            (dt_bias[:, :], columns(a["L1_conv_dt_bias"], DT)),
            (A_sb[:, :, :], a["L1_conv_A_log"].rearrange("(t p) n -> p t n", p=P)),
            (D_cols[:, :], columns(a["L1_conv_D_skip"], DT)),
            (g_cols[:, :], columns(a["L1_conv_ln2_g"], DT)),
            (b_cols[:, :], columns(a["L1_conv_ln2_b"], DT)),
            (wout_sb[:, :, :], a["L1_conv_w_out"].rearrange("(t p) n -> p t n", p=P)),
            (bout_row[:, :], a["L1_conv_b_out"].rearrange("(a n) -> a n", a=1)),
        ] + [(conv_k[:, t, :], a["L1_conv_conv_w"].rearrange("a b o (t p) -> t p (a b o)", p=P)[t])
             for t in range(DT)]
        NCONST = len(consts)
        NREADY = 7

        def wait(eng, semaphore, value):
            if not isinstance(value, int) or value > 0:
                eng.wait_ge(semaphore, value)

        def over_tiles(row):
            return row.rearrange("p (a n) -> p a n", a=1).broadcast_to([P, DT, T])

        def run(eng, strip):
            strip(0, 0, False, True)
            with eng.Fori(0, STRIPS // 2 - 1) as p:
                strip(2 * p + 1, 1, True, True)
                strip(2 * p + 2, 0, True, True)
            strip(STRIPS - 1, 1, True, False)

        @block.sync
        def _(sp):
            for dst, src in consts:
                load(sp, dst, src, s_const)

            def load_halo(g):
                sp.dma_start(x_halo[:, :, :],
                             XI[bass.ds(g // NWIN, 1), :, :, bass.ds((g % NWIN) * T, (WS + CK - 1) * W)]
                             .rearrange("b t p n -> p (b t) n")).then_inc(halo_loaded, 16)

            def load_residual(g, u):
                sp.dma_start(xres[u][:TK, :, :], x2_tiles[bass.ds(g, 1)].rearrange("g p k c -> p (g k) c")
                             ).then_inc(res_loaded[u], 16)

            def store(g, u):
                sp.wait_ge(epi_free, EPI * g + EPI)
                sp.dma_start(out_tiles[bass.ds(g, 1)].rearrange("g p k c -> p (g k) c"),
                             xres[u][:TK, :, :]).then_inc(out_stored[u], 16)

            def strip(g, u, epi, pro):
                if pro:
                    sp.wait_ge(pro_full, PRO * g + DT)
                    load_halo(g + 1)
                if epi:
                    store(g - 1, 1 - u)
                if pro:
                    if epi:
                        sp.wait_ge(out_stored[1 - u], 8 * (g + 1) if u else 8 * g)
                    load_residual(g + 1, 1 - u)

            load_halo(0)
            load_residual(0, 0)
            run(sp, strip)
            store(STRIPS - 1, 1)
            for u in range(2):
                sp.wait_ge(out_stored[u], 8 * STRIPS)

        @block.gpsimd
        def _(pool):
            make_identity(nc, pool, ident, s_clear, s_ready)
            nc.gpsimd.memset(averager[:, :], 1.0 / DN).then_inc(s_ready, 1)
            nc.gpsimd.memset(eps_col[:, :], EPS1).then_inc(s_ready, 1)
            nc.gpsimd.memset(ones_row[:, :], 1.0).then_inc(s_ready, 1)
            nc.gpsimd.memset(carry[:, :, :], 0.0).then_inc(s_ready, 1)
            nc.gpsimd.memset(keep[:, :], 1.0).then_inc(s_clear, 1)
            pool.wait_ge(s_clear, 2)
            nc.gpsimd.memset(keep[:, :].rearrange("p (b s) -> p b s", s=NWIN)[:, :, 0], 0.0).then_inc(s_ready, 1)
            for v in range(2):
                last = nc.gpsimd.memset(dA[v][:, :, 0], 0.0)
            last.then_inc(s_ready, 1)

            def strip(g, u, epi, pro):
                for n in range(NS):
                    N, v = g * NS + n, n % 2
                    pool.wait_ge(scanned, N + 1)
                    pool.wait_ge(C_copied, N + 1)
                    wait(pool, summed, N - 1)
                    nc.gpsimd.tensor_tensor(hC[v][:, :, :], hs[v][:, :, 1:], over_tiles(Csb[v][:, :]),
                                            ALU.mult).then_inc(hC_ready, 1)

            run(pool, strip)

        @block.vector
        def _(dve):
            dve.wait_ge(s_ready, NREADY)
            dve.wait_ge(s_const, 16 * NCONST)
            nc.vector.tensor_copy(ident_b[:, :], ident[:, :]).then_inc(diag_ready, 1)
            nc.vector.tensor_tensor(hilo_b[:, :], ident[:, 0:NS], ident[:, NS:2 * NS], ALU.add).then_inc(diag_ready, 1)
            nc.vector.tensor_scalar(A_sb[:, :, :], A_sb[:, :, :], A_LOG_MAX, None, ALU.min).then_inc(a_capped, 1)
            for tap in range(TAPS):
                for t in range(DT):
                    last = nc.vector.tensor_scalar(conv_diag[:, tap, t, :], ident[:, :], conv_k[:, t, tap:tap + 1],
                                                   None, ALU.mult)
            last.then_inc(diag_ready, 1)
            dve.wait_ge(a_exp, 1)
            nc.vector.tensor_scalar(A_sb[:, :, :], A_sb[:, :, :], -1.0, None, ALU.mult).then_inc(a_ready, 1)

            def residue(g, u, s):
                dve.wait_ge(pack_ready, 2 * g + s + 1)
                wait(dve, low_ready, 2 * g + s)
                nc.vector.tensor_tensor(rest[:, :], aux[:, :T], pack[s][u][:, :], ALU.subtract).then_inc(pro_free, 1)

            def low_part(g, u, s):
                dve.wait_ge(mid_ready, 2 * g + s + 1)
                rows = slice(s * NS, (s + 1) * NS)
                nc.vector.tensor_tensor(low[u][rows, :], rest[rows, :], mid[rows, :],
                                        ALU.subtract).then_inc(low_ready, 1)

            def softplus_a(g, u):
                chain = Chain(dve, dve_chain, 3 * g)
                dve.wait_ge(soft_ready, g + 1)
                chain.link(nc.vector.tensor_scalar(tmp[3][:, :, :], tmp[1][:, :, :], 1.0, -1.0, ALU.add, ALU.add))
                chain.link(nc.vector.tensor_tensor(tmp[1][:, :, :], tmp[1][:, :, :], tmp[3][:, :, :], ALU.subtract))

            def softplus_b(g, u):
                chain = Chain(dve, dve_chain, 3 * g + 2)
                chain.link(nc.vector.scalar_tensor_tensor(flat(tmp[2]), flat(tmp[0]), 0.0, flat(tmp[2]),
                                                          ALU.max, ALU.add))
                nc.vector.tensor_tensor(dt[u][:, :, :], tmp[2][:, :, :], tmp[1][:, :, :], ALU.add).then_inc(dt_ready, 1)

            def scale_input(g, u):
                dve.wait_ge(dt_ready, g + 1)
                nc.vector.tensor_tensor(dtx[u][:, :, :], dt[u][:, :, :], xg[u][:, :, :], ALU.mult
                                        ).then_inc(dtx_ready, 1)

            def skip(g, u):
                dve.wait_ge(summed, NS * g + NS)
                for t in range(DT):
                    last = nc.vector.scalar_tensor_tensor(tmp[0][:, t, :], xg[u][:, t, :], D_cols[:, t:t + 1],
                                                          y_ps[:, t, :T], ALU.mult, ALU.add)
                last.then_inc(yv_ready, 1)

            def centre(g, u):
                dve.wait_ge(epi_full, EPI * g + MEAN + 1)
                nc.vector.tensor_tensor(tmp[0][:, :, :], tmp[0][:, :, :], over_tiles(aux[:, :T]),
                                        ALU.subtract).then_inc(epi_free, 1)

            def invert(g, u):
                dve.wait_ge(epi_free, EPI * g + VAR + 1)
                nc.vector.reciprocal(std[:, :], std[:, :]).then_inc(rs_ready, 1)

            def rescale(g, u):
                dve.wait_ge(rs_ready, g + 1)
                nc.vector.tensor_tensor(tmp[0][:, :, :], tmp[0][:, :, :], over_tiles(std[:, :]),
                                        ALU.mult).then_inc(yn_ready, 1)

            def add_residual(g, u, half):
                dve.wait_ge(epi_full, EPI * g + WO + half + 1)
                if half == 0:
                    dve.wait_ge(res_loaded[u], 8 * g + 8 * (2 - u))
                rows = xres[u][:TK, 2 * half:2 * half + 2, :]
                nc.vector.tensor_tensor(rows, rows, aux[:TK, :].rearrange("p (k c) -> p k c", k=2),
                                        ALU.add).then_inc(epi_free, 1)

            def flat(t):
                return t[:, :, :].rearrange("p a n -> p (a n)")

            def inject(g, u, n):
                N, v = g * NS + n, n % 2
                dve.wait_ge(B_ready, N + 1)
                wait(dve, scanned, N - 1)
                nc.vector.tensor_tensor(wB[v][:, :, 1:], dtx[u][:, :, :], over_tiles(b_ps[:, v, :T]),
                                        ALU.mult).then_inc(wB_ready, 1)

            def scan(g, n):
                N, v = g * NS + n, n % 2
                dve.wait_ge(wB_ready, N + 1)
                dve.wait_ge(in_ready, N + 1)
                dve.wait_ge(dA_ready, N + 1)
                wait(dve, hC_ready, N - 1)
                wait(dve, carried, N - 1)
                nc.vector.tensor_tensor_scan(flat(hs[v]), flat(dA[v]), flat(wB[v]), 0.0, ALU.mult,
                                             ALU.add).then_inc(scanned, 1)

            def strip(g, u, epi, pro):
                for n in range(NS):
                    if n + 1 < NS:
                        inject(g, u, n + 1)
                    elif pro:
                        dve.wait_ge(dtx_ready, g + 2)
                        inject(g + 1, 1 - u, 0)
                    scan(g, n)
                    if epi:
                        if n == 0:
                            skip(g - 1, 1 - u)
                        if n == 3:
                            centre(g - 1, 1 - u)
                        if n == 7:
                            invert(g - 1, 1 - u)
                        if n == 8:
                            rescale(g - 1, 1 - u)
                        if n in (11, 13):
                            add_residual(g - 1, 1 - u, (n - 11) // 2)
                    if pro:
                        if n in (39, 42):
                            residue(g + 1, 1 - u, (n - 39) // 3)
                        if n in (41, 44):
                            low_part(g + 1, 1 - u, (n - 41) // 3)
                        if n == 57:
                            softplus_a(g + 1, 1 - u)
                        if n == 58:
                            softplus_b(g + 1, 1 - u)
                        if n == 60:
                            scale_input(g + 1, 1 - u)

            for s in range(2):
                residue(0, 0, s)
                low_part(0, 0, s)
            softplus_a(0, 0)
            softplus_b(0, 0)
            scale_input(0, 0)
            dve.wait_ge(dtx_ready, 1)
            inject(0, 0, 0)
            run(dve, strip)
            last = STRIPS - 1
            skip(last, 1)
            centre(last, 1)
            invert(last, 1)
            rescale(last, 1)
            for half in range(2):
                add_residual(last, 1, half)

        @block.tensor
        def _(pe):
            pe.wait_ge(s_ready, NREADY)
            pe.wait_ge(s_const, 16 * NCONST)
            pe.wait_ge(diag_ready, 3)

            def convolve(g, t, first, last):
                order = [(1, 1)] + [(y, x) for y in range(CK) for x in range(CK) if (y, x) != (1, 1)]
                if first == 0:
                    pe.wait_ge(halo_loaded, 16 * g + 16)
                    wait(pe, pro_free, PRO * g + t)
                    if t == 0:
                        wait(pe, epi_free, EPI * g - EPI)
                for n in range(first, last):
                    y, x = order[n]
                    dx = x - 1
                    lo, hi = max(0, -dx), min(W, W - dx)
                    step = nc.tensor.matmul(
                        aux[:, :T].rearrange("p (h w) -> p h w", w=W)[:, :, lo:hi], conv_diag[:, CK * y + x, t, :],
                        x_halo[:, t, :].rearrange("p (h w) -> p h w", w=W)[:, y:y + WS, lo + dx:hi + dx],
                        start=n == 0, stop=n == TAPS - 1)
                if last == TAPS:
                    step.then_inc(pro_full, 1)

            def project(g, u, use):
                pe.wait_ge(pro_free, PRO * g + use)
                first = {BB: 0, CC: 2 * NS, DTR: 4 * NS}[use]
                width = RK if use == DTR else 2 * NS
                for t in range(DT):
                    step = nc.tensor.matmul(aux[:width, :T], wx_sb[:, t, first:first + width], xg[u][:, t, :],
                                            start=t == 0, stop=t == DT - 1)
                step.then_inc(pro_full, 1)

            def step_size(g, t):
                pe.wait_ge(pro_free, PRO * g + DT0 + t)
                nc.tensor.matmul(aux[:, :T], wdt_sb[:, t * P:(t + 1) * P], dt_low[:, :], start=True,
                                 stop=True).then_inc(pro_full, 1)

            def average(g, use):
                if use == MEAN:
                    pe.wait_ge(yv_ready, g + 1)
                    if not isinstance(g, int):
                        pe.wait_ge(pro_free, PRO * g + 2 * PRO)
                else:
                    pe.wait_ge(sq_ready, g + 1)
                    pe.wait_ge(epi_free, EPI * g + use)
                src = tmp[0] if use == MEAN else tmp[1]
                for t in range(DT):
                    step = nc.tensor.matmul(aux[:, :T], averager[:, :], src[:, t, :], start=t == 0, stop=t == DT - 1)
                step.then_inc(epi_full, 1)

            def out_project(g, half):
                pe.wait_ge(yo_ready, g + 1)
                pe.wait_ge(epi_free, EPI * g + WO + half)
                for k in range(2):
                    tokens = slice((2 * half + k) * TK, (2 * half + k + 1) * TK)
                    dst = aux[:TK, k * C:(k + 1) * C]
                    nc.tensor.matmul(dst, ones_row[:, :], bout_row[:, :], start=True, stop=False)
                    for t in range(DT):
                        step = nc.tensor.matmul(dst, tmp[3][:, t, tokens], wout_sb[:, t, :], start=False,
                                                stop=t == DT - 1)
                step.then_inc(epi_full, 1)

            def spread(g, u, n):
                N, v = g * NS + n, n % 2
                wait(pe, wB_ready, N - 1)
                for s, dst, semaphore in ((0, b_ps[:, v, :T], B_ready), (1, c_ps[:, :T], C_ready)):
                    if s == 1:
                        wait(pe, C_copied, N)
                    nc.tensor.matmul(dst, hilo_b[:, n:n + 1].broadcast_to([P, P]), pack[s][u][:, :],
                                     start=True, stop=False)
                    nc.tensor.matmul(dst, ident_b[:, s * NS + n:s * NS + n + 1].broadcast_to([P, P]), low[u][:, :],
                                     start=False, stop=True).then_inc(semaphore, 1)

            def accumulate(g, n):
                pe.wait_ge(hC_ready, g * NS + n + 1)
                if n == 0:
                    wait(pe, yv_ready, g)
                for t in range(DT):
                    step = nc.tensor.matmul(y_ps[:, t, :T], ident[:, :], hC[n % 2][:, t, :], start=n == 0,
                                            stop=n == NS - 1)
                step.then_inc(summed, 1)

            CUTS = [0, 3, 5, 7, 9]

            def strip(g, u, epi, pro):
                pe.wait_ge(pack_done, 2 * g + 2)
                pe.wait_ge(low_ready, 2 * g + 2)
                for n in range(NS):
                    spread(g, u, n)
                    if n >= 2:
                        accumulate(g, n - 2)
                    elif epi:
                        accumulate(g - 1, NS - 2 + n)
                    if epi:
                        if n == 3:
                            average(g - 1, MEAN)
                        if n == 6:
                            average(g - 1, VAR)
                        if n in (11, 13):
                            out_project(g - 1, (n - 11) // 2)
                    if pro:
                        if 18 <= n < 38 and (n - 18) % 5 < 4:
                            part = (n - 18) % 5
                            convolve(g + 1, (n - 18) // 5, CUTS[part], CUTS[part + 1])
                        if n in (38, 41, 44):
                            project(g + 1, 1 - u, (BB, CC, DTR)[(n - 38) // 3])
                        if n in (46, 48, 50, 52):
                            step_size(g + 1, (n - 46) // 2)

            for t in range(DT):
                convolve(0, t, 0, TAPS)
            for use in (BB, CC, DTR):
                project(0, 0, use)
            for t in range(DT):
                step_size(0, t)
            run(pe, strip)
            last = STRIPS - 1
            accumulate(last, NS - 2)
            accumulate(last, NS - 1)
            average(last, MEAN)
            average(last, VAR)
            for half in range(2):
                out_project(last, half)

        @block.scalar
        def _(act):
            act.wait_ge(s_const, 16 * NCONST)
            act.wait_ge(a_capped, 1)
            nc.scalar.activation(A_sb[:, :, :], A_sb[:, :, :], ACT.Exp).then_inc(a_exp, 1)
            act.wait_ge(a_ready, 1)
            act.wait_ge(s_ready, NREADY)

            def gelu(g, u, t):
                act.wait_ge(pro_full, PRO * g + t + 1)
                if t == 0:
                    wait(act, yv_ready, g - 1)
                nc.scalar.activation(xg[u][:, t, :], aux[:, :T], ACT.Gelu_apprx_tanh,
                                     bias=conv_bias[:, t:t + 1]).then_inc(pro_free, 1)

            def high_part(g, u, s):
                act.wait_ge(pro_full, PRO * g + BB + s + 1)
                nc.scalar.activation(pack[s][u][:, :], aux[:, :T], ACT.Copy).then_inc(pack_ready, 1)

            def mid_part(g, s):
                act.wait_ge(pro_free, PRO * g + BB + s + 1)
                wait(act, low_ready, 2 * g + s)
                nc.scalar.activation(mid[:, :], rest[:, :], ACT.Copy).then_inc(mid_ready, 1)

            def place_mid(g, u, s):
                act.wait_ge(mid_ready, 2 * g + s + 1)
                nc.scalar.activation(pack[s][u][NS:, :], mid[NS:, :], ACT.Copy).then_inc(pack_done, 1)

            def low_rank(g):
                act.wait_ge(pro_full, PRO * g + DTR + 1)
                nc.scalar.activation(dt_low[:, :], aux[:RK, :T], ACT.Copy).then_inc(pro_free, 1)

            def step_bias(g, t):
                act.wait_ge(pro_full, PRO * g + DT0 + t + 1)
                nc.scalar.activation(tmp[0][:, t, :], aux[:, :T], ACT.Identity,
                                     bias=dt_bias[:, t:t + 1]).then_inc(pro_free, 1)

            def softplus_exp(g):
                act.wait_ge(pro_free, PRO * g + PRO)
                chain = Chain(act, act_chain, 2 * g)
                chain.link(nc.scalar.activation(tmp[1][:, :, :], tmp[0][:, :, :], ACT.Abs))
                chain.link(nc.scalar.activation(tmp[1][:, :, :], tmp[1][:, :, :], ACT.Exp, scale=-1.0))
                nc.scalar.activation(tmp[2][:, :, :], tmp[1][:, :, :], ACT.Ln, bias=1.0).then_inc(soft_ready, 1)

            def square(g):
                act.wait_ge(epi_free, EPI * g + MEAN + 1)
                nc.scalar.activation(tmp[1][:, :, :], tmp[0][:, :, :], ACT.Square).then_inc(sq_ready, 1)

            def deviation(g):
                act.wait_ge(epi_full, EPI * g + VAR + 1)
                wait(act, yn_ready, g)
                nc.scalar.activation(std[:, :], aux[:, :T], ACT.Sqrt, bias=eps_col[:, :]).then_inc(epi_free, 1)

            def affine(g):
                act.wait_ge(yn_ready, g + 1)
                for t in range(DT):
                    last = nc.scalar.activation(tmp[3][:, t, :], tmp[0][:, t, :], ACT.Identity,
                                                bias=b_cols[:, t:t + 1], scale=g_cols[:, t:t + 1])
                last.then_inc(yo_ready, 1)

            def carry_out(g, n):
                act.wait_ge(in_ready, g * NS + n + 1)
                nc.scalar.activation(carry[:, n, :], hs[n % 2][:, :, T], ACT.Copy).then_inc(carried, 1)

            def decay(g, u, n):
                N, v = g * NS + n, n % 2
                wait(act, scanned, N - 1)
                if n >= 2:
                    carry_out(g, n - 2)
                elif not isinstance(g, int) or g > 0:
                    carry_out(g - 1, NS - 2 + n)
                wait(act, carried, N - NS + 1)
                nc.scalar.activation(wB[v][:, :, 0], carry[:, n, :], ACT.Copy,
                                     scale=keep_now[u][:, :]).then_inc(in_ready, 1)
                for t in range(DT):
                    last = nc.scalar.activation(dA[v][:, t, 1:], dt[u][:, t, :], ACT.Exp, scale=A_sb[:, t, n:n + 1])
                last.then_inc(dA_ready, 1)

            def copy_C(g, n):
                N, v = g * NS + n, n % 2
                act.wait_ge(C_ready, N + 1)
                wait(act, hC_ready, N - 1)
                nc.scalar.activation(Csb[v][:, :], c_ps[:, :T], ACT.Copy).then_inc(C_copied, 1)

            def strip(g, u, epi, pro):
                nc.scalar.activation(keep_now[u][:, :], keep[:, bass.ds(g, 1)], ACT.Copy).then_inc(keep_ready, 1)
                act.wait_ge(keep_ready, g + 1)
                act.wait_ge(dt_ready, g + 1)
                for n in range(NS):
                    decay(g, u, n)
                    copy_C(g, n)
                    if epi:
                        if n == 5:
                            square(g - 1)
                        if n == 7:
                            deviation(g - 1)
                        if n == 10:
                            affine(g - 1)
                    if pro:
                        if n in (22, 27, 32, 37):
                            gelu(g + 1, 1 - u, (n - 22) // 5)
                        if n in (39, 42):
                            high_part(g + 1, 1 - u, (n - 39) // 3)
                        if n in (41, 44):
                            mid_part(g + 1, (n - 41) // 3)
                            place_mid(g + 1, 1 - u, (n - 41) // 3)
                        if n == 45:
                            low_rank(g + 1)
                        if n in (47, 49, 51, 53):
                            step_bias(g + 1, (n - 47) // 2)
                        if n == 55:
                            softplus_exp(g + 1)

            for t in range(DT):
                gelu(0, 0, t)
            for s in range(2):
                high_part(0, 0, s)
                mid_part(0, s)
                place_mid(0, 0, s)
            low_rank(0)
            for t in range(DT):
                step_bias(0, t)
            softplus_exp(0)
            run(act, strip)
            last = STRIPS - 1
            square(last)
            deviation(last)
            affine(last)


def program(nc, a, out):
    QT = nc.dram_tensor("QT", [STRIPS, P, NWIN * CT * WT], F32).ap()
    KT = nc.dram_tensor("KT", [STRIPS * NWIN, P, CT * WT], F32).ap()
    VT = nc.dram_tensor("VT", [NB, CT, P, VROWS * W], F32).ap()
    VN = nc.dram_tensor("VN", [STRIPS * NWIN, WT, C], F32).ap()
    IDX = nc.dram_tensor("IDX", [NB, WPI, TOPK], I32).ap()
    X2 = nc.dram_tensor("X2", [STRIPS, TK, NK * C], F32).ap()
    XI = nc.dram_tensor("XI", [NB, DT, P, XROWS * W], F32).ap()
    with ExitStack() as ctx:
        qsum = ctx.enter_context(nc.sbuf_tensor("qsum", [P, STRIPS * NWSUM], F32))
        ksum = ctx.enter_context(nc.sbuf_tensor("ksum", [P, STRIPS * NWSUM], F32))
        phase_qkv(nc, a["x"], a["L0_conv_ln1_g"], a["L0_conv_ln1_b"], a["L0_conv_qkv_w"], a["L0_conv_qkv_b"],
                  QT, KT, VT, VN, qsum, ksum)
        phase_route(nc, qsum, ksum, IDX)
    phase_attention(nc, a["x"], QT, KT, VT, VN, IDX, a["L0_conv_lepe_w"], a["L0_conv_lepe_b"], a["L0_conv_wo_w"],
                    a["L0_conv_wo_b"], a["L0_conv_ln2_g"], a["L0_conv_ln2_b"], a["L0_conv_mlp_w1"],
                    a["L0_conv_mlp_b1"], a["L0_conv_mlp_w2"], a["L0_conv_mlp_b2"], a["L1_conv_ln1_g"],
                    a["L1_conv_ln1_b"], a["L1_conv_w_in"], a["L1_conv_b_in"], X2, XI)
    phase_scan(nc, a, X2, XI, out)


_INS = ["x", "L0_conv_ln1_g", "L0_conv_ln1_b", "L0_conv_qkv_w", "L0_conv_qkv_b", "L0_conv_lepe_w",
        "L0_conv_lepe_b", "L0_conv_wo_w", "L0_conv_wo_b", "L0_conv_ln2_g", "L0_conv_ln2_b", "L0_conv_mlp_w1",
        "L0_conv_mlp_b1", "L0_conv_mlp_w2", "L0_conv_mlp_b2", "L1_conv_ln1_g", "L1_conv_ln1_b", "L1_conv_w_in",
        "L1_conv_b_in", "L1_conv_conv_w", "L1_conv_conv_b", "L1_conv_w_x", "L1_conv_w_dt", "L1_conv_dt_bias",
        "L1_conv_A_log", "L1_conv_D_skip", "L1_conv_ln2_g", "L1_conv_ln2_b", "L1_conv_w_out", "L1_conv_b_out"]


def kernel(**inputs):
    import numpy as _np
    import concourse.bacc as _bacc
    from concourse import mybir as _mybir
    from concourse.bass_utils import run_bass_kernel_spmd as _run

    nc = _bacc.Bacc("TRN2", target_bir_lowering=False, num_devices=1)
    arrays, args = {}, {}
    for name in _INS:
        a = _np.ascontiguousarray(inputs[name])
        arrays[f"in_{name}_dram"] = a
        args[name] = nc.dram_tensor(f"in_{name}_dram", a.shape, _mybir.dt.from_np(a.dtype), kind="ExternalInput").ap()
    out = nc.dram_tensor("out_0_dram", (NB, H, W, C), _mybir.dt.from_np(_np.dtype("float32")),
                         kind="ExternalOutput").ap()
    program(nc, args, out)
    r = _run(nc, [arrays], core_ids=[0])
    return r.results[0]["out_0_dram"]
```

```python
from contextlib import ExitStack

import concourse.bass as bass
from concourse import mybir

F32 = mybir.dt.float32
BF16 = mybir.dt.bfloat16
I32 = mybir.dt.int32
U32 = mybir.dt.uint32
ALU = mybir.AluOpType
ACT = mybir.ActivationFunctionType
AX = mybir.AxisListType

P = 128
NB, H, W, C = 8, 56, 56, 256
NWIN = 7
WS = H // NWIN
WT = WS * WS
WPI = NWIN * NWIN
T = WS * W
STRIPS = NB * NWIN
NK = 4
TK = T // NK
CT = C // P
HEADS, DH = 8, 32
TOPK = 4
HID = 4 * C
HT = HID // P
SCALE = float(C) ** -0.5
DN = 512
DT = DN // P
NS = 64
RK = 16
EPS0, EPS1 = 1e-6, 1e-5
VROWS = H + WS
LK, CK = 5, 3
XROWS = H + 2
NWSUM = NWIN * CT


class Chain:

    def __init__(self, eng, sem, base):
        self.eng, self.sem, self.base, self.n = eng, sem, base, 0

    def link(self, instruction):
        self.n += 1
        instruction.then_inc(self.sem, 1)
        self.eng.wait_ge(self.sem, self.base + self.n)


def by_window(tokens):
    return tokens.rearrange("p (w h x) -> p h w x", w=NWIN, h=WS)


def columns(v, n):
    return v.rearrange("(t p) -> p t", p=P)


def wait(eng, semaphore, value):
    if not isinstance(value, int) or value > 0:
        eng.wait_ge(semaphore, value)


def load(eng, dst, src, sem):
    eng.dma_start(dst, src, allow_slow_non_contiguous=True).then_inc(sem, 16)


def make_identity(nc, pool, tile, cleared, done):
    nc.gpsimd.memset(tile[:, :], 0.0).then_inc(cleared, 1)
    pool.wait_ge(cleared, 1)
    nc.gpsimd.affine_select(out=tile[:, :], in_=tile[:, :], compare_op=ALU.not_equal, fill=1.0, base=0,
                            pattern=[[-1, P]], channel_multiplier=1).then_inc(done, 1)


def layernorm_stats(nc, chain, x, stats, mv, var_eps, eps, var_ready):
    for k in range(NK - 1):
        nc.vector.bn_stats(stats[:TK, k, :], x[:TK, k, :])
    chain.link(nc.vector.bn_stats(stats[:TK, NK - 1, :], x[:TK, NK - 1, :]))
    even, odd = stats[:TK, :, 1], stats[:TK, :, 4]
    nc.vector.tensor_tensor(mv[:TK, :, 0], even, odd, ALU.add)
    nc.vector.tensor_tensor(mv[:TK, :, 1], even, odd, ALU.subtract)
    chain.link(nc.vector.tensor_tensor(mv[:TK, :, 2], stats[:TK, :, 2], stats[:TK, :, 5], ALU.add))
    nc.vector.tensor_scalar(mv[:TK, :, 0], mv[:TK, :, 0], 0.5, None, ALU.mult)
    nc.vector.tensor_tensor(mv[:TK, :, 1], mv[:TK, :, 1], mv[:TK, :, 1], ALU.mult)
    chain.link(nc.vector.tensor_scalar(mv[:TK, :, 2], mv[:TK, :, 2], 1.0 / C, eps, ALU.mult, ALU.add))
    nc.vector.scalar_tensor_tensor(var_eps[:TK, :], mv[:TK, :, 1], 0.25, mv[:TK, :, 2], ALU.mult,
                                   ALU.add).then_inc(var_ready, 1)


def normalise(nc, x, xn, mv, rstd):
    for k in range(NK):
        last = nc.vector.tensor_scalar(xn[:TK, k, :], x[:TK, k, :], mv[:TK, k, 0:1], rstd[:TK, k:k + 1],
                                       ALU.subtract, ALU.mult)
    return last


def phase_qkv(nc, x, ln_g, ln_b, qkv_w, qkv_b, QT, KT, VT, VN, qsum, ksum):
    with ExitStack() as ctx:
        def sb(name, shape, dt=F32):
            return ctx.enter_context(nc.sbuf_tensor("a_" + name, shape, dt))

        def ps(name, shape, dt=F32):
            return ctx.enter_context(nc.psum_tensor("a_" + name, shape, dt))

        def sem(name):
            return ctx.enter_context(nc.semaphore("a_" + name))

        ident = sb("ident", [P, P])
        w_sb = sb("w", [P, CT, 3 * C])
        b_cols = sb("b_cols", [P, 3 * CT])
        vb_rows = sb("vb_rows", [P, C])
        g_cols = sb("g_cols", [P, CT])
        bb_cols = sb("bb_cols", [P, CT])
        zeros = sb("zeros", [P, NB * CT, 2 * W])
        half = sb("half", [P, NK])
        xin = [sb(f"xin{u}", [P, NK, C]) for u in range(2)]
        xn = [sb(f"xn{u}", [P, NK, C]) for u in range(2)]
        stats = sb("stats", [P, NK, 6])
        mv = sb("mv", [P, NK, 3])
        var_eps = sb("var_eps", [P, NK])
        rstd = sb("rstd", [P, NK])
        xnT = [sb(f"xnT{u}", [P, CT, T]) for u in range(2)]
        q_out = [sb(f"q_out{u}", [P, NWIN, CT, WT]) for u in range(2)]
        k_out = [sb(f"k_out{u}", [P, NWIN, CT, WT]) for u in range(2)]
        vT_out = [sb(f"vT_out{u}", [P, CT, T]) for u in range(2)]
        vn_out = [sb(f"vn_out{u}", [P, NK, C]) for u in range(2)]

        tp = ps("tp", [P, CT, 512])
        qkv_ps = ps("qkv_ps", [P, 3, 512])
        vn_ps = ps("vn_ps", [P, 2, 512])

        s_const = sem("s_const")
        s_clear = sem("s_clear")
        s_ident = sem("s_ident")
        s_zeros = sem("s_zeros")
        s_halo = sem("s_halo")
        x_loaded = [sem(f"x_loaded{u}") for u in range(2)]
        dve_chain = sem("dve_chain")
        var_ready = sem("var_ready")
        rstd_ready = sem("rstd_ready")
        xn_ready = sem("xn_ready")
        tp_ready = sem("tp_ready")
        xnT_ready = sem("xnT_ready")
        qkv_ready = sem("qkv_ready")
        qkv_free = sem("qkv_free")
        vn_ready = sem("vn_ready")
        vn_free = sem("vn_free")
        wsum_done = sem("wsum_done")
        stored = [sem(f"stored{u}") for u in range(2)]
        NCONST = 6
        NSTORE = 5
        PAIRS = STRIPS // 2
        block = ctx.enter_context(nc.Block())

        x_tiles = x.rearrange("b h w c -> (b h w) c").rearrange("(g k p) c -> g p k c", g=STRIPS, k=NK)
        kt_strips = KT.rearrange("(g w) p n -> g p w n", g=STRIPS)
        vn_rows = VN.rearrange("w t c -> (w t) c").rearrange("(g r) c -> g r c", g=STRIPS)
        full = (T // P) * P

        def run(eng, strip):
            strip(0, 0, True)
            strip(1, 1, True)
            with eng.Fori(1, PAIRS - 1) as p:
                strip(2 * p, 0, True)
                strip(2 * p + 1, 1, True)
            strip(STRIPS - 2, 0, True)
            strip(STRIPS - 1, 1, False)

        @block.sync
        def _(sp):
            sp.dma_start(w_sb[:, :, :], qkv_w.rearrange("(t p) n -> p t n", p=P)).then_inc(s_const, 16)
            load(sp, b_cols[:, :], columns(qkv_b, 3 * CT), s_const)
            sp.dma_start(vb_rows[:, :], qkv_b[2 * C:3 * C].rearrange("(a n) -> a n", a=1).broadcast_to([P, C])
                         ).then_inc(s_const, 16)
            load(sp, g_cols[:, :], columns(ln_g, CT), s_const)
            load(sp, bb_cols[:, :], columns(ln_b, CT), s_const)
            sp.dma_start(xin[0][:TK, :, :], x_tiles[0]).then_inc(x_loaded[0], 16)
            sp.dma_start(xin[1][:TK, :, :], x_tiles[1]).then_inc(x_loaded[1], 16)
            sp.wait_ge(s_zeros, 1)
            vt_img = VT.rearrange("b t p n -> p (b t) n")
            sp.dma_start(vt_img[:, :, 0:2 * W], zeros[:, :, :]).then_inc(s_halo, 16)
            sp.dma_start(vt_img[:, :, (H + 2) * W:(H + 4) * W], zeros[:, :, :]).then_inc(s_halo, 16)

            def strip(p, u, prefetch):
                g = 2 * p + u
                img = g // NWIN
                row = (g % NWIN) * T + 2 * W
                sp.wait_ge(qkv_free, 6 * g + 9)
                sp.dma_start(QT[bass.ds(g, 1)].rearrange("g p n -> p (g n)"),
                             q_out[u][:, :, :, :].rearrange("p w t n -> p (w t n)")).then_inc(stored[u], 16)
                sp.dma_start(kt_strips[bass.ds(g, 1)].rearrange("g p w n -> p (g w) n"),
                             k_out[u][:, :, :, :].rearrange("p w t n -> p w (t n)")).then_inc(stored[u], 16)
                sp.dma_start(VT[bass.ds(img, 1), :, :, bass.ds(row, T)].rearrange("b t p n -> p (b t) n"),
                             vT_out[u][:, :, :]).then_inc(stored[u], 16)
                sp.wait_ge(vn_free, 4 * g + 6)
                rows = vn_rows[bass.ds(g, 1)]
                sp.dma_start(rows[:, 0:full, :].rearrange("g (k p) c -> p (g k) c", p=P),
                             vn_out[u][:, 0:T // P, :]).then_inc(stored[u], 16)
                sp.dma_start(rows[:, full:T, :].rearrange("g r c -> (g r) c"),
                             vn_out[u][0:WT, T // P, :]).then_inc(stored[u], 16)
                if prefetch:
                    sp.wait_ge(xn_ready, g + 1)
                    sp.dma_start(xin[u][:TK, :, :],
                                 x_tiles[bass.ds(g + 2, 1)].rearrange("g p k c -> p (g k) c")
                                 ).then_inc(x_loaded[u], 16)

            with sp.Fori(0, PAIRS - 1) as p:
                for u in range(2):
                    strip(p, u, True)
            for u in range(2):
                strip(PAIRS - 1, u, False)
            sp.wait_ge(s_halo, 32)
            for u in range(2):
                sp.wait_ge(stored[u], 16 * NSTORE * PAIRS)

        @block.gpsimd
        def _(pool):
            make_identity(nc, pool, ident, s_clear, s_ident)
            nc.gpsimd.memset(half[:, :], -0.5).then_inc(s_clear, 1)
            nc.gpsimd.memset(zeros[:, :, :], 0.0).then_inc(s_zeros, 1)
            pool.wait_ge(s_clear, 2)
            with pool.Fori(0, STRIPS) as g:
                pool.wait_ge(var_ready, g + 1)
                nc.gpsimd.tensor_tensor(rstd[:TK, :], var_eps[:TK, :], half[:TK, :], ALU.pow).then_inc(rstd_ready, 1)

        @block.vector
        def _(dve):
            dve.wait_ge(s_const, 16 * (NCONST - 1))
            dve.sem_inc(vn_free, 2)

            def norm(g, u):
                chain = Chain(dve, dve_chain, 3 * g)
                dve.wait_ge(x_loaded[u], 8 * g + 8 * (2 - u))
                layernorm_stats(nc, chain, xin[u], stats, mv, var_eps, EPS0, var_ready)
                dve.wait_ge(rstd_ready, g + 1)
                wait(dve, tp_ready, CT * g)
                normalise(nc, xin[u], xn[u], mv, rstd).then_inc(xn_ready, 1)

            def strip(g, u, ahead):
                if ahead:
                    norm(g + 1, 1 - u)
                wait(dve, stored[u], 8 * NSTORE * (g - u))
                for k in range(NK):
                    n = P if k < T // P else WT
                    dve.wait_ge(vn_ready, NK * g + k + 1)
                    nc.vector.tensor_tensor(vn_out[u][:n, k, :], vn_ps[:n, k % 2, :C], vb_rows[:n, :],
                                            ALU.add).then_inc(vn_free, 1)
                dve.wait_ge(qkv_free, 6 * g + 9)
                for src, dst in ((q_out, qsum), (k_out, ksum)):
                    nc.vector.tensor_reduce(dst[:, bass.ds(g * NWSUM, NWSUM)],
                                            src[u][:, :, :, :].rearrange("p w t n -> p (w t) n"), AX.X,
                                            ALU.add).then_inc(wsum_done, 1)

            norm(0, 0)
            run(dve, strip)

        @block.tensor
        def _(pe):
            pe.wait_ge(s_ident, 1)
            pe.wait_ge(s_const, 16 * (NCONST - 1))

            def transpose(g, u):
                pe.wait_ge(xn_ready, g + 1)
                wait(pe, xnT_ready, CT * g)
                for ct in range(CT):
                    for k in range(NK):
                        last = nc.tensor.transpose(tp[:, ct, k * TK:(k + 1) * TK],
                                                   xn[u][:TK, k, ct * P:(ct + 1) * P], ident[:TK, :TK])
                    last.then_inc(tp_ready, 1)

            def strip(g, u, ahead):
                pe.wait_ge(xnT_ready, CT * g + CT)
                for m in range(3 * CT):
                    pe.wait_ge(qkv_free, 6 * g + m + 1)
                    for ct in range(CT):
                        last = nc.tensor.matmul(qkv_ps[:, m % 3, :T], w_sb[:, ct, m * P:(m + 1) * P],
                                                xnT[u][:, ct, :], start=ct == 0, stop=ct == CT - 1)
                    last.then_inc(qkv_ready, 1)
                if ahead:
                    transpose(g + 1, 1 - u)
                for k in range(NK):
                    n = 2 if k < T // P else 1
                    pe.wait_ge(vn_free, NK * g + k + 1)
                    for ct in range(CT):
                        tokens = xnT[u][:, ct, 2 * k * WT:(2 * k + n) * WT]
                        last = nc.tensor.matmul(vn_ps[:n * WT, k % 2, :C], tokens, w_sb[:, ct, 2 * C:3 * C],
                                                start=ct == 0, stop=ct == CT - 1)
                    last.then_inc(vn_ready, 1)

            transpose(0, 0)
            run(pe, strip)

        @block.scalar
        def _(act):
            act.wait_ge(s_const, 16 * (NCONST - 1))
            act.sem_inc(qkv_free, 3)

            def affine(g, u):
                wait(act, vn_ready, NK * g - NK)
                for ct in range(CT):
                    act.wait_ge(tp_ready, CT * g + ct + 1)
                    nc.scalar.activation(by_window(xnT[u][:, ct, :]), tp[:, ct, :T], ACT.Identity,
                                         bias=bb_cols[:, ct:ct + 1], scale=g_cols[:, ct:ct + 1]
                                         ).then_inc(xnT_ready, 1)

            def strip(g, u, ahead):
                wait(act, stored[u], 8 * NSTORE * (g - u))
                wait(act, wsum_done, 2 * g)
                for m in range(3 * CT):
                    act.wait_ge(qkv_ready, 6 * g + m + 1)
                    if m < 2 * CT:
                        out, src = (q_out, k_out)[m // CT][u][:, :, m % CT, :], qkv_ps[:, m % 3, :T]
                    else:
                        out, src = vT_out[u][:, m % CT, :], by_window(qkv_ps[:, m % 3, :T])
                    nc.scalar.activation(out, src, ACT.Identity, bias=b_cols[:, m:m + 1]).then_inc(qkv_free, 1)
                if ahead:
                    affine(g + 1, 1 - u)

            affine(0, 0)
            run(act, strip)


def phase_route(nc, qsum, ksum, IDX):
    with ExitStack() as ctx:
        def sb(name, shape, dt=F32):
            return ctx.enter_context(nc.sbuf_tensor("r_" + name, shape, dt))

        def sem(name):
            return ctx.enter_context(nc.semaphore("r_" + name))

        logits_ps = ctx.enter_context(nc.psum_tensor("r_logits_ps", [P, NB, 512], F32))
        qmean = sb("qmean", [P, STRIPS * NWIN, CT])
        kmean = sb("kmean", [P, STRIPS * NWIN, CT])
        logits = sb("logits", [P, NB, WPI])
        top = sb("top", [P, NB, 8])
        top_at = sb("top_at", [P, NB, 8], U32)
        idx = sb("idx", [P, NB, TOPK], I32)
        means = sem("means")
        scored = sem("scored")
        chained = sem("chained")
        picked = sem("picked")
        stored = sem("stored")
        block = ctx.enter_context(nc.Block())

        @block.vector
        def _(dve):
            nc.vector.tensor_scalar(qmean[:, :, :].rearrange("p w t -> p (w t)"), qsum[:, :], 1.0 / WT, SCALE,
                                    ALU.mult, ALU.mult).then_inc(means, 1)
            nc.vector.tensor_scalar(kmean[:, :, :].rearrange("p w t -> p (w t)"), ksum[:, :], 1.0 / WT, None,
                                    ALU.mult).then_inc(means, 1)
            chain = Chain(dve, chained, 0)
            dve.wait_ge(scored, 1)
            chain.link(nc.vector.tensor_copy(logits[:WPI, :, :], logits_ps[:WPI, :, :WPI]))
            for b in range(NB):
                chain.link(nc.vector.max(top[:WPI, b, :], logits[:WPI, b, :]))
                chain.link(nc.vector.max_index(top_at[:WPI, b, :], top[:WPI, b, :], logits[:WPI, b, :]))
                nc.vector.tensor_scalar(idx[:WPI, b, :], top_at[:WPI, b, :TOPK], float(b * WPI), None,
                                        ALU.add).then_inc(picked, 1)

        @block.tensor
        def _(pe):
            pe.wait_ge(means, 2)
            for b in range(NB):
                for ct in range(CT):
                    last = nc.tensor.matmul(logits_ps[:WPI, b, :WPI], qmean[:, b * WPI:(b + 1) * WPI, ct],
                                            kmean[:, b * WPI:(b + 1) * WPI, ct], start=ct == 0, stop=ct == CT - 1)
            last.then_inc(scored, 1)

        @block.sync
        def _(sp):
            sp.wait_ge(picked, NB)
            sp.dma_start(IDX.rearrange("b w k -> w b k"), idx[:WPI, :, :]).then_inc(stored, 16)
            sp.wait_ge(stored, 16)


def phase_attention(nc, x, QT, KT, VT, VN, IDX, lepe_w, lepe_b, wo_w, wo_b, ln2_g, ln2_b, w1, b1, w2, b2,
                    l1_g, l1_b, w_in, b_in, X2, XI):
    with ExitStack() as ctx:
        def sb(name, shape, dt=F32):
            return ctx.enter_context(nc.sbuf_tensor("b_" + name, shape, dt))

        def ps(name, shape, dt=F32):
            return ctx.enter_context(nc.psum_tensor("b_" + name, shape, dt))

        def sem(name):
            return ctx.enter_context(nc.semaphore("b_" + name))

        PAIRS = STRIPS // 2
        NPAIR = HEADS // 2
        NKEY = TOPK * WT
        TAPS = LK * LK
        ident = sb("ident", [P, P])
        half = sb("half", [P, NK])
        zeros = sb("zeros", [P, NB * DT, W])
        idx = sb("idx", [1, STRIPS * NWIN * TOPK], I32)
        lepe_k = sb("lepe_k", [P, CT, TAPS])
        lepe_bias = sb("lepe_bias", [P, CT])
        wo_sb = sb("wo_sb", [P, CT, C])
        wob_rows = sb("wob_rows", [P, C])
        g2 = sb("g2", [P, CT])
        bb2 = sb("bb2", [P, CT])
        w1_sb = sb("w1_sb", [P, CT, HID])
        b1_cols = sb("b1_cols", [P, HT])
        w2_sb = sb("w2_sb", [P, HT, C])
        b2_rows = sb("b2_rows", [P, C])
        g3 = sb("g3", [P, CT])
        bb3 = sb("bb3", [P, CT])
        win_sb = sb("win_sb", [P, CT, DN])
        bin_cols = sb("bin_cols", [P, DT])

        xr = [sb(f"xr{u}", [P, NK, C]) for u in range(2)]
        q_blk = [sb(f"q_blk{u}", [P, NWIN, CT, 4, WT]) for u in range(2)]
        v_halo = sb("v_halo", [P, CT, (WS + LK - 1) * W])
        k_sel = [sb(f"k_sel{w}", [P, TOPK, CT, WT]) for w in range(2)]
        v_sel = [sb(f"v_sel{w}", [P, TOPK // 2, C]) for w in range(2)]
        row_max = sb("row_max", [P, 2, NPAIR])
        neg_max = sb("neg_max", [P, 2, NPAIR])
        row_sum = sb("row_sum", [P, 2, NPAIR])
        inv_sum = sb("inv_sum", [P, 2, NPAIR])
        probs = [sb(f"probs{w}", [P, NPAIR, NKEY]) for w in range(2)]
        probsT = [sb(f"probsT{w}", [P, 2, NPAIR, P]) for w in range(2)]
        attn = sb("attn", [P, CT, T])
        lepe = sb("lepe", [P, CT, T])
        stats = sb("stats", [P, NK, 6])
        mv = sb("mv", [P, NK, 3])
        var_eps = sb("var_eps", [P, NK])
        rstd = sb("rstd", [P, NK])
        xn = sb("xn", [P, NK, C])
        xnT = sb("xnT", [P, CT, T])
        hid = sb("hid", [P, HT, T])
        xi = sb("xi", [P, DT, T])

        scores = ps("scores", [P, 2, 512])
        tail_ps = ps("tail_ps", [P, 2, 512])
        spare = ps("spare", [P, 512])
        pt = ps("pt", [P, 2, 512])
        oT = ps("oT", [P, CT, 4 * WT])

        s_const = sem("s_const")
        s_clear = sem("s_clear")
        s_ident = sem("s_ident")
        s_zeros = sem("s_zeros")
        s_halo = sem("s_halo")
        q_zeroed = sem("q_zeroed")
        s_idx = sem("s_idx")
        x_loaded = [sem(f"x_loaded{u}") for u in range(2)]
        q_loaded = [sem(f"q_loaded{u}") for u in range(2)]
        v_loaded = sem("v_loaded")
        k_loaded = [sem(f"k_loaded{w}") for w in range(2)]
        vsel_loaded = [sem(f"vsel_loaded{w}") for w in range(2)]
        scored = sem("scored")
        negmax_ready = sem("negmax_ready")
        exp_done = sem("exp_done")
        probs_ready = sem("probs_ready")
        pt_ready = sem("pt_ready")
        pt_taken = sem("pt_taken")
        max_done = sem("max_done")
        inverted = sem("inverted")
        tapped = sem("tapped")
        taps_done = sem("taps_done")
        oT_ready = sem("oT_ready")
        oT_taken = sem("oT_taken")
        dve_chain = sem("dve_chain")
        biased = sem("biased")
        attn_ready = sem("attn_ready")
        y_ready = sem("y_ready")
        var_ready = sem("var_ready")
        rstd_ready = sem("rstd_ready")
        xn_ready = sem("xn_ready")
        tp_ready = sem("tp_ready")
        xnT_ready = sem("xnT_ready")
        hid_scored = sem("hid_scored")
        hid_ready = sem("hid_ready")
        mlp_ready = sem("mlp_ready")
        x2_ready = sem("x2_ready")
        xi_scored = sem("xi_scored")
        xi_ready = sem("xi_ready")
        x2_stored = [sem(f"x2_stored{u}") for u in range(2)]
        xi_stored = sem("xi_stored")
        block = ctx.enter_context(nc.Block())

        x_tiles = x.rearrange("b h w c -> (b h w) c").rearrange("(g k p) c -> g p k c", g=STRIPS, k=NK)
        qt_heads = QT.rearrange("g (a d) (w t n) -> g a d w t n", a=4, w=NWIN, t=CT)

        consts = [
            (lepe_k, lepe_w.rearrange("a b o (t p) -> p t (a b o)", p=P)),
            (lepe_bias, columns(lepe_b, CT)),
            (wo_sb, wo_w.rearrange("(t p) n -> p t n", p=P)),
            (wob_rows, wo_b.rearrange("(a n) -> a n", a=1).broadcast_to([P, C])),
            (g2, columns(ln2_g, CT)),
            (bb2, columns(ln2_b, CT)),
            (w1_sb, w1.rearrange("(t p) n -> p t n", p=P)),
            (b1_cols, columns(b1, HT)),
            (w2_sb, w2.rearrange("(t p) n -> p t n", p=P)),
            (b2_rows, b2.rearrange("(a n) -> a n", a=1).broadcast_to([P, C])),
            (g3, columns(l1_g, CT)),
            (bb3, columns(l1_b, CT)),
            (win_sb, w_in.rearrange("(t p) n -> p t n", p=P)),
            (bin_cols, columns(b_in, DT)),
        ]
        NCONST = len(consts) + CT - 1

        def loads(g, u, i):
            return 8 * TOPK * (7 * (g - u)) + 16 * TOPK * ((7 * u + i) // 2 + 1)

        def run(eng, strip):
            strip(0, 0, False, False)
            strip(1, 1, True, False)
            with eng.Fori(1, PAIRS) as p:
                strip(2 * p, 0, True, True)
                strip(2 * p + 1, 1, True, True)

        @block.sync
        def _(sp):
            sp.dma_start(idx[:, :], IDX.rearrange("b w k -> (b w k)").rearrange("(a n) -> a n", a=1)
                         ).then_inc(s_idx, 16)
            for t in range(CT):
                load(sp, lepe_k[:, t, :], lepe_w.rearrange("a b o (t p) -> t p (a b o)", p=P)[t], s_const)
            for dst, src in consts[1:]:
                load(sp, dst[(slice(None),) * len(dst.shape)], src, s_const)
            sp.wait_ge(s_zeros, 1)
            xi_img = XI.rearrange("b t p n -> p (b t) n")
            sp.dma_start(xi_img[:, :, 0:W], zeros[:, :, :]).then_inc(s_halo, 16)
            sp.dma_start(xi_img[:, :, (H + 1) * W:XROWS * W], zeros[:, :, :]).then_inc(s_halo, 16)
            sp.wait_ge(s_idx, 16)
            sp.wait_ge(q_zeroed, 2)

            def load_q(g, u):
                for h in range(4):
                    for t in range(CT):
                        sp.dma_start(q_blk[u][h * DH:(h + 1) * DH, :, t, h, :],
                                     qt_heads[bass.ds(g, 1), h, :, :, t, :].rearrange("g d w n -> d (g w) n")
                                     ).then_inc(q_loaded[u], 16)

            def load_window(g, u, i):
                w = (7 * u + i) % 2
                wins = [sp.value_load(idx[0:1, bass.ds(g * (NWIN * TOPK) + (i * TOPK + s), 1)],
                                      min_val=0, max_val=NB * WPI - 1) for s in range(TOPK)]
                wait(sp, scored, 7 * g + i - 1)
                for s, win in enumerate(wins):
                    sp.dma_start(k_sel[w][:, s, :, :].rearrange("p t n -> p (t n)"),
                                 KT[bass.ds(win, 1)].rearrange("w p n -> p (w n)")).then_inc(k_loaded[w], 16)
                wait(sp, oT_ready, 7 * g + i - 1)
                for s, win in enumerate(wins):
                    sp.dma_start(v_sel[w][(s % 2) * WT:(s % 2 + 1) * WT, s // 2, :],
                                 VN[bass.ds(win, 1)].rearrange("w t c -> t (w c)")).then_inc(vsel_loaded[w], 16)

            def store_x2(g, u):
                sp.wait_ge(x2_ready, g + 1)
                sp.wait_ge(xn_ready, 2 * g + 2)
                sp.dma_start(X2[bass.ds(g, 1)].rearrange("g p n -> p (g n)"),
                             xr[u][:TK, :, :].rearrange("p k c -> p (k c)")).then_inc(x2_stored[u], 16)

            def store_xi(g):
                sp.wait_ge(xi_ready, DT * g + DT)
                sp.dma_start(XI[bass.ds(g // NWIN, 1), :, :, bass.ds((g % NWIN) * T + W, T)]
                             .rearrange("b t p n -> p (b t) n"), xi[:, :, :]).then_inc(xi_stored, 16)

            def strip(g, u, tail, tail_end):
                wait(sp, taps_done, g)
                sp.dma_start(v_halo[:, :, :],
                             VT[bass.ds(g // NWIN, 1), :, :, bass.ds((g % NWIN) * T, (WS + LK - 1) * W)]
                             .rearrange("b t p n -> p (b t) n")).then_inc(v_loaded, 16)
                load_window(g, u, 1)
                if tail_end:
                    store_x2(g - 2, u)
                    sp.wait_ge(x2_stored[u], 8 * (g - u))
                sp.dma_start(xr[u][:TK, :, :], x_tiles[bass.ds(g, 1)].rearrange("g p k c -> p (g k) c")
                             ).then_inc(x_loaded[u], 16)
                load_window(g, u, 2)
                if not isinstance(g, int) or g > 0:
                    load_q(g + 1, 1 - u)
                for i in range(3, NWIN):
                    load_window(g, u, i)
                    if i == 3 and tail_end:
                        store_xi(g - 2)
                load_window(g + 1, 1 - u, 0)

            sp.sem_inc(xi_stored, 16)
            load_q(0, 0)
            load_q(1, 1)
            load_window(0, 0, 0)
            strip(0, 0, False, False)
            strip(1, 1, True, False)
            with sp.Fori(1, PAIRS - 1) as p:
                strip(2 * p, 0, True, True)
                strip(2 * p + 1, 1, True, True)
            strip(STRIPS - 2, 0, True, True)
            g, u = STRIPS - 1, 1
            sp.wait_ge(taps_done, g)
            sp.dma_start(v_halo[:, :, :],
                         VT[g // NWIN:g // NWIN + 1, :, :, (g % NWIN) * T:(g % NWIN) * T + (WS + LK - 1) * W]
                         .rearrange("b t p n -> p (b t) n")).then_inc(v_loaded, 16)
            load_window(g, u, 1)
            store_x2(g - 2, u)
            sp.wait_ge(x2_stored[u], 8 * (g - u))
            sp.dma_start(xr[u][:TK, :, :], x_tiles[g]).then_inc(x_loaded[u], 16)
            for i in range(2, NWIN):
                load_window(g, u, i)
            store_xi(g - 2)
            store_x2(g - 1, 0)
            store_xi(g - 1)
            store_x2(g, 1)
            store_xi(g)
            sp.wait_ge(s_halo, 32)
            sp.wait_ge(xi_stored, 16 * STRIPS + 16)
            for u in range(2):
                sp.wait_ge(x2_stored[u], 8 * STRIPS)

        @block.gpsimd
        def _(pool):
            make_identity(nc, pool, ident, s_clear, s_ident)
            nc.gpsimd.memset(half[:, :], -0.5).then_inc(s_clear, 1)
            nc.gpsimd.memset(zeros[:, :, :], 0.0).then_inc(s_zeros, 1)
            for u in range(2):
                nc.gpsimd.memset(q_blk[u][:, :, :, :, :], 0.0).then_inc(q_zeroed, 1)
            pool.wait_ge(s_const, 16 * NCONST)
            pool.wait_ge(s_clear, 2)

            def strip(p, u):
                g = 2 * p + u
                pool.wait_ge(x_loaded[u], 16 * p + 16)
                nc.gpsimd.tensor_tensor(xr[u][:TK, :, :], xr[u][:TK, :, :],
                                        wob_rows[:TK, :].rearrange("p (a n) -> p a n", a=1).broadcast_to([TK, NK, C]),
                                        ALU.add).then_inc(biased, 1)
                pool.wait_ge(var_ready, 2 * g + 1)
                nc.gpsimd.tensor_tensor(rstd[:TK, :], var_eps[:TK, :], half[:TK, :], ALU.pow).then_inc(rstd_ready, 1)
                pool.wait_ge(xn_ready, 2 * g + 1)
                nc.gpsimd.tensor_tensor(xr[u][:TK, :, :], xr[u][:TK, :, :],
                                        b2_rows[:TK, :].rearrange("p (a n) -> p a n", a=1).broadcast_to([TK, NK, C]),
                                        ALU.add).then_inc(biased, 1)
                pool.wait_ge(var_ready, 2 * g + 2)
                nc.gpsimd.tensor_tensor(rstd[:TK, :], var_eps[:TK, :], half[:TK, :], ALU.pow).then_inc(rstd_ready, 1)

            with pool.Fori(0, PAIRS) as p:
                for u in range(2):
                    strip(p, u)

        @block.vector
        def _(dve):
            dve.wait_ge(s_const, 16 * NCONST)
            ORDER = [(LK // 2, LK // 2)] + [(y, x) for y in range(LK) for x in range(LK)
                                            if (y, x) != (LK // 2, LK // 2)]

            def lepe_taps(g, first, last):
                for n in range(first, last):
                    y, x = ORDER[n]
                    dx = x - LK // 2
                    lo, hi = max(0, -dx), min(W, W - dx)
                    for t in range(CT):
                        wait(dve, tapped, CT * TAPS * g + CT * n + t - 1)
                        grid = lepe[:, t, :].rearrange("p (h w) -> p h w", h=WS)[:, :, lo:hi]
                        src = v_halo[:, t, :].rearrange("p (h w) -> p h w", w=W)[:, y:y + WS, lo + dx:hi + dx]
                        tap = lepe_k[:, t, y * LK + x:y * LK + x + 1]
                        if n == 0:
                            step = nc.vector.tensor_scalar(grid, src, tap, lepe_bias[:, t:t + 1], ALU.mult, ALU.add)
                        else:
                            step = nc.vector.scalar_tensor_tensor(grid, src, tap, grid, ALU.mult, ALU.add)
                        step.then_inc(tapped, 1)
                if last == TAPS:
                    dve.wait_ge(tapped, CT * TAPS * g + CT * TAPS)
                    dve.sem_inc(taps_done, 1)

            def maximum(g, u, i):
                w = (7 * u + i) % 2
                dve.wait_ge(scored, 7 * g + i + 1)
                nc.vector.tensor_reduce(row_max[:, w, :], scores[:, :, :].rearrange("p a (b n) -> p (a b) n", b=2),
                                        AX.X, ALU.max).then_inc(max_done, 1)
                dve.wait_ge(max_done, 7 * g + i + 1)
                nc.vector.tensor_scalar(neg_max[:, w, :], row_max[:, w, :], -SCALE, None,
                                        ALU.mult).then_inc(negmax_ready, 1)

            def divide(g, u, i):
                w = (7 * u + i) % 2
                dve.wait_ge(exp_done, 7 * g + i + 1)
                nc.vector.reciprocal(inv_sum[:, w, :], row_sum[:, w, :]).then_inc(inverted, 1)
                dve.wait_ge(inverted, 7 * g + i + 1)
                for j in range(NPAIR):
                    last = nc.vector.tensor_scalar(probs[w][:, j, :], probs[w][:, j, :], inv_sum[:, w, j:j + 1],
                                                   None, ALU.mult)
                last.then_inc(probs_ready, 1)

            def take_output(g, i):
                dve.wait_ge(oT_ready, 7 * g + i + 1)
                if i == 0:
                    wait(dve, y_ready, g)
                out = attn[:, :, :].rearrange("p t (h w x) -> p t w h x", h=WS, w=NWIN)[:, :, i]
                nc.vector.tensor_copy(out, oT[:, :, :WT].rearrange("p t (h x) -> p t h x", h=WS)
                                      ).then_inc(oT_taken, 1)

            def add_lepe(g):
                dve.wait_ge(oT_taken, 7 * g + NWIN)
                dve.wait_ge(taps_done, g + 1)
                nc.vector.tensor_tensor(attn[:, :, :], attn[:, :, :], lepe[:, :, :], ALU.add).then_inc(attn_ready, 1)

            def residual_norm(g, u):
                chain = Chain(dve, dve_chain, 7 * g)
                dve.wait_ge(y_ready, g + 1)
                dve.wait_ge(biased, 2 * g + 1)
                chain.link(nc.vector.tensor_tensor(xr[u][:TK, :, :], xr[u][:TK, :, :],
                                                   tail_ps[:TK, :, :].rearrange("p a (b n) -> p (a b) n", b=2),
                                                   ALU.add))
                layernorm_stats(nc, chain, xr[u], stats, mv, var_eps, EPS0, var_ready)
                dve.wait_ge(rstd_ready, 2 * g + 1)
                wait(dve, tp_ready, 4 * g)
                normalise(nc, xr[u], xn, mv, rstd).then_inc(xn_ready, 1)

            def mlp_norm(g, u):
                chain = Chain(dve, dve_chain, 7 * g + 4)
                dve.wait_ge(mlp_ready, g + 1)
                dve.wait_ge(biased, 2 * g + 2)
                nc.vector.tensor_tensor(xr[u][:TK, :, :], xr[u][:TK, :, :],
                                        tail_ps[:TK, :, :].rearrange("p a (b n) -> p (a b) n", b=2),
                                        ALU.add).then_inc(x2_ready, 1)
                dve.wait_ge(x2_ready, g + 1)
                layernorm_stats(nc, chain, xr[u], stats, mv, var_eps, EPS1, var_ready)
                dve.wait_ge(rstd_ready, 2 * g + 2)
                dve.wait_ge(tp_ready, 4 * g + 2)
                normalise(nc, xr[u], xn, mv, rstd).then_inc(xn_ready, 1)

            CUTS = [0, 4, 6, 11, 15, 19, 23, TAPS]

            def strip(g, u, tail, tail_end):
                for i in range(NWIN):
                    maximum(g, u, i)
                    if i > 0:
                        lepe_taps(g, CUTS[i], CUTS[i + 1])
                    divide(g, u, i)
                    if i > 0:
                        take_output(g, i - 1)
                    elif tail:
                        take_output(g - 1, NWIN - 1)
                        add_lepe(g - 1)
                    if i == 0:
                        dve.wait_ge(v_loaded, 16 * g + 16)
                        if tail:
                            dve.wait_ge(attn_ready, g)
                        lepe_taps(g, CUTS[0], CUTS[1])
                    if i == 1 and tail:
                        residual_norm(g - 1, 1 - u)
                    if i == 6 and tail:
                        mlp_norm(g - 1, 1 - u)

            run(dve, strip)
            last = STRIPS - 1
            take_output(last, NWIN - 1)
            add_lepe(last)
            residual_norm(last, 1)
            mlp_norm(last, 1)

        @block.tensor
        def _(pe):
            pe.wait_ge(s_ident, 1)
            pe.wait_ge(s_const, 16 * NCONST)
            banks = [tail_ps[:, 0, :], tail_ps[:, 1, :], spare[:, :]]

            def score(g, u, i):
                w = (7 * u + i) % 2
                if i == 0:
                    pe.wait_ge(q_loaded[u], 64 * (g - u) + 128)
                pe.wait_ge(k_loaded[w], loads(g, u, i))
                wait(pe, exp_done, 7 * g + i)
                for j in range(NPAIR):
                    last = nc.tensor.matmul(
                        scores[:, j // 2, (j % 2) * NKEY:(j % 2 + 1) * NKEY],
                        q_blk[u][:, i, j // 2, 2 * (j % 2):2 * (j % 2) + 2, :],
                        k_sel[w][:, :, j // 2, :], start=True, stop=True)
                last.then_inc(scored, 1)

            def transpose_probs(g, u, i):
                w = (7 * u + i) % 2
                pe.wait_ge(probs_ready, 7 * g + i + 1)
                wait(pe, pt_taken, 7 * g + i)
                for kk in range(2):
                    for j in range(NPAIR):
                        last = nc.tensor.transpose(pt[:, kk, j * P:(j + 1) * P],
                                                   probs[w][:, j, kk * P:(kk + 1) * P], ident[:, :])
                last.then_inc(pt_ready, 1)

            def attend(g, u, i):
                w = (7 * u + i) % 2
                pe.wait_ge(pt_taken, 7 * g + i + 1)
                wait(pe, oT_taken, 7 * g + i)
                pe.wait_ge(vsel_loaded[w], loads(g, u, i))
                for h in range(HEADS):
                    rows = slice((h % 4) * DH, (h % 4 + 1) * DH)
                    for kk in range(2):
                        last = nc.tensor.matmul(
                            oT[rows, h // 4, :WT], v_sel[w][:, kk, h * DH:(h + 1) * DH],
                            probsT[w][:, kk, h // 2, (h % 2) * WT:(h % 2 + 1) * WT],
                            start=kk == 0, stop=kk == 1)
                last.then_inc(oT_ready, 1)

            def project_out(g):
                pe.wait_ge(attn_ready, g + 1)
                wait(pe, xi_ready, DT * g)
                for k in range(NK):
                    for t in range(CT):
                        last = nc.tensor.matmul(tail_ps[:TK, k // 2, (k % 2) * C:(k % 2 + 1) * C],
                                                attn[:, t, k * TK:(k + 1) * TK], wo_sb[:, t, :],
                                                start=t == 0, stop=t == CT - 1)
                last.then_inc(y_ready, 1)

            def transpose_xn(g, n):
                pe.wait_ge(xn_ready, 2 * g + n)
                for ct in range(CT):
                    for k in range(NK):
                        last = nc.tensor.transpose(tail_ps[:, ct, k * TK:(k + 1) * TK],
                                                   xn[:TK, k, ct * P:(ct + 1) * P], ident[:TK, :TK])
                    last.then_inc(tp_ready, 1)

            def mlp_up(g, first, last):
                if first == 0:
                    pe.wait_ge(xnT_ready, 4 * g + 2)
                for m in range(first, last):
                    if m >= 3:
                        pe.wait_ge(hid_ready, HT * g + m - 2)
                    for ct in range(CT):
                        step = nc.tensor.matmul(banks[m % 3][:, :T], w1_sb[:, ct, m * P:(m + 1) * P],
                                                xnT[:, ct, :], start=ct == 0, stop=ct == CT - 1)
                    step.then_inc(hid_scored, 1)

            def mlp_down(g, k):
                if k == 0:
                    pe.wait_ge(hid_ready, HT * g + HT)
                for m in range(HT):
                    step = nc.tensor.matmul(tail_ps[:TK, k // 2, (k % 2) * C:(k % 2 + 1) * C],
                                            hid[:, m, k * TK:(k + 1) * TK], w2_sb[:, m, :],
                                            start=m == 0, stop=m == HT - 1)
                if k == NK - 1:
                    step.then_inc(mlp_ready, 1)

            def project_in(g):
                pe.wait_ge(xnT_ready, 4 * g + 4)
                for m in range(DT):
                    if m >= 3:
                        pe.wait_ge(xi_ready, DT * g + m - 2)
                    for ct in range(CT):
                        step = nc.tensor.matmul(banks[m % 3][:, :T], win_sb[:, ct, m * P:(m + 1) * P],
                                                xnT[:, ct, :], start=ct == 0, stop=ct == CT - 1)
                    step.then_inc(xi_scored, 1)

            def strip(g, u, tail, tail_end):
                for i in range(NWIN):
                    score(g, u, i)
                    if i == 0 and tail_end:
                        transpose_xn(g - 2, 2)
                    if i > 0 and tail:
                        if i == 1:
                            project_out(g - 1)
                        if i == 2:
                            transpose_xn(g - 1, 1)
                        if i == 3:
                            mlp_up(g - 1, 2, 4)
                        if i == 4:
                            mlp_up(g - 1, 6, 8)
                        if i == 5:
                            mlp_down(g - 1, 1)
                        if i == 6:
                            mlp_down(g - 1, 3)
                    if i > 0:
                        transpose_probs(g, u, i - 1)
                    elif tail:
                        transpose_probs(g - 1, 1 - u, NWIN - 1)
                    if i == 2 and tail:
                        mlp_up(g - 1, 0, 1)
                    if i == 3 and tail:
                        mlp_up(g - 1, 4, 5)
                    if i == 0 and tail_end:
                        project_in(g - 2)
                    if i > 0:
                        attend(g, u, i - 1)
                    elif tail:
                        attend(g - 1, 1 - u, NWIN - 1)
                    if tail:
                        if i == 2:
                            mlp_up(g - 1, 1, 2)
                        if i == 3:
                            mlp_up(g - 1, 5, 6)
                        if i == 4:
                            mlp_down(g - 1, 0)
                        if i == 5:
                            mlp_down(g - 1, 2)

            run(pe, strip)
            last = STRIPS - 1
            transpose_xn(last - 1, 2)
            transpose_probs(last, 1, NWIN - 1)
            project_in(last - 1)
            attend(last, 1, NWIN - 1)
            project_out(last)
            transpose_xn(last, 1)
            mlp_up(last, 0, HT)
            for k in range(NK):
                mlp_down(last, k)
            transpose_xn(last, 2)
            project_in(last)

        @block.scalar
        def _(act):
            act.wait_ge(s_const, 16 * NCONST)
            banks = [tail_ps[:, 0, :], tail_ps[:, 1, :], spare[:, :]]

            def exps(g, u, i):
                w = (7 * u + i) % 2
                act.wait_ge(negmax_ready, 7 * g + i + 1)
                wait(act, pt_ready, 7 * g + i - 1)
                for j in range(NPAIR):
                    last = nc.scalar.activation(
                        probs[w][:, j, :], scores[:, j // 2, (j % 2) * NKEY:(j % 2 + 1) * NKEY], ACT.Exp,
                        bias=neg_max[:, w, j:j + 1], scale=SCALE, accum_out=row_sum[:, w, j:j + 1])
                last.then_inc(exp_done, 1)

            def take_probs(g, u, i):
                w = (7 * u + i) % 2
                act.wait_ge(pt_ready, 7 * g + i + 1)
                wait(act, oT_ready, 7 * g + i - 1)
                nc.scalar.activation(probsT[w][:, :, :, :].rearrange("p k j q -> p k (j q)"), pt[:, :, :],
                                     ACT.Copy).then_inc(pt_taken, 1)

            def affine(g, n, gain, shift):
                for ct in range(CT):
                    act.wait_ge(tp_ready, 4 * g + 2 * n + ct + 1)
                    if ct == 0:
                        wait(act, xi_scored if n == 0 else hid_scored, DT * g if n == 0 else HT * g + HT)
                    nc.scalar.activation(xnT[:, ct, :], tail_ps[:, ct, :T], ACT.Identity,
                                         bias=shift[:, ct:ct + 1], scale=gain[:, ct:ct + 1]
                                         ).then_inc(xnT_ready, 1)

            def gelus(g, first, last):
                if first == 0:
                    wait(act, mlp_ready, g)
                for m in range(first, last):
                    act.wait_ge(hid_scored, HT * g + m + 1)
                    nc.scalar.activation(hid[:, m, :], banks[m % 3][:, :T], ACT.Gelu,
                                         bias=b1_cols[:, m:m + 1]).then_inc(hid_ready, 1)

            def take_xi(g):
                act.wait_ge(xi_stored, 16 * g + 16)
                for m in range(DT):
                    act.wait_ge(xi_scored, DT * g + m + 1)
                    nc.scalar.activation(xi[:, m, :], banks[m % 3][:, :T], ACT.Identity,
                                         bias=bin_cols[:, m:m + 1]).then_inc(xi_ready, 1)

            def strip(g, u, tail, tail_end):
                for i in range(NWIN):
                    if i == 0 and tail_end:
                        affine(g - 2, 1, g3, bb3)
                    exps(g, u, i)
                    if i == 2 and tail:
                        affine(g - 1, 0, g2, bb2)
                    if i > 0:
                        take_probs(g, u, i - 1)
                    elif tail:
                        take_probs(g - 1, 1 - u, NWIN - 1)
                    if i == 0 and tail_end:
                        take_xi(g - 2)
                    if tail:
                        if i in (2, 3, 4):
                            first = (0, 2, 6)[i - 2]
                            gelus(g - 1, first, (2, 6, 8)[i - 2])

            run(act, strip)
            last = STRIPS - 1
            affine(last - 1, 1, g3, bb3)
            take_probs(last, 1, NWIN - 1)
            take_xi(last - 1)
            affine(last, 0, g2, bb2)
            gelus(last, 0, HT)
            affine(last, 1, g3, bb3)
            take_xi(last)


def phase_scan(nc, a, X2, XI, out):
    with ExitStack() as ctx:
        def sb(name, shape, dt=F32):
            return ctx.enter_context(nc.sbuf_tensor("c_" + name, shape, dt))

        def ps(name, shape, dt=F32):
            return ctx.enter_context(nc.psum_tensor("c_" + name, shape, dt))

        def sem(name):
            return ctx.enter_context(nc.semaphore("c_" + name))

        QS = 32
        QUARTERS = 2 * NS // QS
        TRI = 3 * QS
        BC, DTR, DT0, PRO = DT, DT + QUARTERS, DT + QUARTERS + 1, DT + QUARTERS + 1 + DT
        MEAN, VAR, WO, EPI = 0, 1, 2, 4
        A_LOG_MAX = 80.0
        TAPS = CK * CK
        T1 = T + 1

        ident = sb("ident", [P, P])
        tri_f = sb("tri_f", [P, QS])
        tri_b = sb("tri_b", [P, QS], BF16)
        averager = sb("averager", [P, P])
        eps_col = sb("eps_col", [P, 1])
        ones_row = sb("ones_row", [1, TK])
        keep = sb("keep", [P, STRIPS])
        keep_now = [sb(f"keep_now{u}", [P, 1]) for u in range(2)]
        conv_k = sb("conv_k", [P, DT, TAPS])
        conv_diag = sb("conv_diag", [P, TAPS, DT, P])
        conv_bias = sb("conv_bias", [P, DT])
        wx_sb = sb("wx_sb", [P, DT, QUARTERS * TRI + RK])
        wdt_sb = sb("wdt_sb", [RK, DN])
        dt_bias = sb("dt_bias", [P, DT])
        A_sb = sb("A_sb", [P, DT, NS])
        D_cols = sb("D_cols", [P, DT])
        g_cols = sb("g_cols", [P, DT])
        b_cols = sb("b_cols", [P, DT])
        wout_sb = sb("wout_sb", [P, DT, C])
        bout_row = sb("bout_row", [1, C])

        x_halo = sb("x_halo", [P, DT, (WS + CK - 1) * W])
        xres = [sb(f"xres{u}", [P, NK, C]) for u in range(2)]
        xg = [sb(f"xg{u}", [P, DT, T]) for u in range(2)]
        dt = [sb(f"dt{u}", [P, DT, T]) for u in range(2)]
        dtx = [sb(f"dtx{u}", [P, DT, T]) for u in range(2)]
        pack = [[sb(f"pack{q}{u}", [P, T], BF16) for u in range(2)] for q in range(QUARTERS)]
        rest = sb("rest", [P, T])
        mid = sb("mid", [P, T], BF16)
        dt_low = sb("dt_low", [RK, T])
        tmp = [sb(f"tmp{n}", [P, DT, T]) for n in range(4)]
        std = sb("std", [P, T])

        dA = [sb(f"dA{v}", [P, DT, T1]) for v in range(2)]
        wB = [sb(f"wB{v}", [P, DT, T1]) for v in range(2)]
        hs = [sb(f"hs{v}", [P, DT, T1]) for v in range(2)]
        hC = [sb(f"hC{v}", [P, DT, T]) for v in range(2)]
        Csb = [sb(f"Csb{v}", [P, T]) for v in range(2)]
        carry = sb("carry", [P, NS, DT])

        y_ps = ps("y_ps", [P, DT, 512])
        b_ps = ps("b_ps", [P, 2, 512])
        c_ps = ps("c_ps", [P, 512])
        aux = ps("aux", [P, 512])

        s_const = sem("s_const")
        s_clear = sem("s_clear")
        s_ready = sem("s_ready")
        diag_ready = sem("diag_ready")
        a_capped = sem("a_capped")
        a_exp = sem("a_exp")
        a_ready = sem("a_ready")
        halo_loaded = sem("halo_loaded")
        res_loaded = [sem(f"res_loaded{u}") for u in range(2)]
        out_stored = [sem(f"out_stored{u}") for u in range(2)]
        pro_full = sem("pro_full")
        pro_free = sem("pro_free")
        epi_full = sem("epi_full")
        epi_free = sem("epi_free")
        pack_ready = sem("pack_ready")
        mid_ready = sem("mid_ready")
        low_ready = sem("low_ready")
        pack_done = sem("pack_done")
        act_chain = sem("act_chain")
        soft_ready = sem("soft_ready")
        dve_chain = sem("dve_chain")
        dt_ready = sem("dt_ready")
        dtx_ready = sem("dtx_ready")
        keep_ready = sem("keep_ready")
        B_ready = sem("B_ready")
        C_ready = sem("C_ready")
        C_copied = sem("C_copied")
        wB_ready = sem("wB_ready")
        in_ready = sem("in_ready")
        dA_ready = sem("dA_ready")
        scanned = sem("scanned")
        carried = sem("carried")
        hC_ready = sem("hC_ready")
        summed = sem("summed")
        yv_ready = sem("yv_ready")
        sq_ready = sem("sq_ready")
        rs_ready = sem("rs_ready")
        yn_ready = sem("yn_ready")
        yo_ready = sem("yo_ready")
        block = ctx.enter_context(nc.Block())

        x2_tiles = X2.rearrange("g p (k c) -> g p k c", k=NK)
        out_tiles = out.rearrange("b h w c -> (b h w) c").rearrange("(g k p) c -> g p k c", g=STRIPS, k=NK)
        w_x = a["L1_conv_w_x"].rearrange("(t p) n -> p t n", p=P)
        consts = [
            (conv_bias[:, :], columns(a["L1_conv_conv_b"], DT)),
            (wx_sb[:, :, QUARTERS * TRI:], w_x[:, :, 0:RK]),
            (wdt_sb[:, :], a["L1_conv_w_dt"]),
            (dt_bias[:, :], columns(a["L1_conv_dt_bias"], DT)),
            (A_sb[:, :, :], a["L1_conv_A_log"].rearrange("(t p) n -> p t n", p=P)),
            (D_cols[:, :], columns(a["L1_conv_D_skip"], DT)),
            (g_cols[:, :], columns(a["L1_conv_ln2_g"], DT)),
            (b_cols[:, :], columns(a["L1_conv_ln2_b"], DT)),
            (wout_sb[:, :, :], a["L1_conv_w_out"].rearrange("(t p) n -> p t n", p=P)),
            (bout_row[:, :], a["L1_conv_b_out"].rearrange("(a n) -> a n", a=1)),
        ] + [(conv_k[:, t, :], a["L1_conv_conv_w"].rearrange("a b o (t p) -> t p (a b o)", p=P)[t])
             for t in range(DT)] + [
            (wx_sb[:, :, (3 * q + c) * QS:(3 * q + c + 1) * QS], w_x[:, :, RK + q * QS:RK + (q + 1) * QS])
            for q in range(QUARTERS) for c in range(3)]
        NCONST = len(consts)
        NREADY = 7

        def over_tiles(row):
            return row.rearrange("p (a n) -> p a n", a=1).broadcast_to([P, DT, T])

        def run(eng, strip):
            strip(0, 0, False, True)
            with eng.Fori(0, STRIPS // 2 - 1) as p:
                strip(2 * p + 1, 1, True, True)
                strip(2 * p + 2, 0, True, True)
            strip(STRIPS - 1, 1, True, False)

        @block.sync
        def _(sp):
            for dst, src in consts:
                load(sp, dst, src, s_const)

            def load_halo(g):
                sp.dma_start(x_halo[:, :, :],
                             XI[bass.ds(g // NWIN, 1), :, :, bass.ds((g % NWIN) * T, (WS + CK - 1) * W)]
                             .rearrange("b t p n -> p (b t) n")).then_inc(halo_loaded, 16)

            def load_residual(g, u):
                sp.dma_start(xres[u][:TK, :, :], x2_tiles[bass.ds(g, 1)].rearrange("g p k c -> p (g k) c")
                             ).then_inc(res_loaded[u], 16)

            def store(g, u):
                sp.wait_ge(epi_free, EPI * g + EPI)
                sp.dma_start(out_tiles[bass.ds(g, 1)].rearrange("g p k c -> p (g k) c"),
                             xres[u][:TK, :, :]).then_inc(out_stored[u], 16)

            def strip(g, u, epi, pro):
                if pro:
                    sp.wait_ge(pro_full, PRO * g + DT)
                    load_halo(g + 1)
                if epi:
                    store(g - 1, 1 - u)
                if pro:
                    if epi:
                        sp.wait_ge(out_stored[1 - u], 8 * (g + 1) if u else 8 * g)
                    load_residual(g + 1, 1 - u)

            load_halo(0)
            load_residual(0, 0)
            run(sp, strip)
            store(STRIPS - 1, 1)
            for u in range(2):
                sp.wait_ge(out_stored[u], 8 * STRIPS)

        @block.gpsimd
        def _(pool):
            make_identity(nc, pool, ident, s_clear, s_ready)
            nc.gpsimd.memset(averager[:, :], 1.0 / DN).then_inc(s_ready, 1)
            nc.gpsimd.memset(eps_col[:, :], EPS1).then_inc(s_ready, 1)
            nc.gpsimd.memset(ones_row[:, :], 1.0).then_inc(s_ready, 1)
            nc.gpsimd.memset(carry[:, :, :], 0.0).then_inc(s_ready, 1)
            nc.gpsimd.memset(keep[:, :], 1.0).then_inc(s_clear, 1)
            pool.wait_ge(s_clear, 2)
            nc.gpsimd.memset(keep[:, :].rearrange("p (b s) -> p b s", s=NWIN)[:, :, 0], 0.0).then_inc(s_ready, 1)
            for v in range(2):
                last = nc.gpsimd.memset(dA[v][:, :, 0], 0.0)
            last.then_inc(s_ready, 1)

            def strip(g, u, epi, pro):
                for n in range(NS):
                    N, v = g * NS + n, n % 2
                    pool.wait_ge(scanned, N + 1)
                    pool.wait_ge(C_copied, N + 1)
                    wait(pool, summed, N - 1)
                    nc.gpsimd.tensor_tensor(hC[v][:, :, :], hs[v][:, :, 1:], over_tiles(Csb[v][:, :]),
                                            ALU.mult).then_inc(hC_ready, 1)

            run(pool, strip)

        @block.vector
        def _(dve):
            dve.wait_ge(s_ready, NREADY)
            dve.wait_ge(s_const, 16 * NCONST)
            nc.vector.tensor_tensor(tri_f[:, :], ident[:, 0:QS], ident[:, QS:2 * QS], ALU.add).then_inc(diag_ready, 1)
            dve.wait_ge(diag_ready, 1)
            nc.vector.tensor_tensor(tri_b[:, :], tri_f[:, :], ident[:, 2 * QS:TRI], ALU.add).then_inc(diag_ready, 1)
            nc.vector.tensor_scalar(A_sb[:, :, :], A_sb[:, :, :], A_LOG_MAX, None, ALU.min).then_inc(a_capped, 1)
            for tap in range(TAPS):
                for t in range(DT):
                    last = nc.vector.tensor_scalar(conv_diag[:, tap, t, :], ident[:, :], conv_k[:, t, tap:tap + 1],
                                                   None, ALU.mult)
            last.then_inc(diag_ready, 1)
            dve.wait_ge(a_exp, 1)
            nc.vector.tensor_scalar(A_sb[:, :, :], A_sb[:, :, :], -1.0, None, ALU.mult).then_inc(a_ready, 1)

            def residue(g, u, q):
                dve.wait_ge(pack_ready, QUARTERS * g + q + 1)
                wait(dve, low_ready, QUARTERS * g + q)
                nc.vector.tensor_tensor(rest[:TRI, :], aux[:TRI, :T], pack[q][u][:TRI, :],
                                        ALU.subtract).then_inc(pro_free, 1)

            def low_part(g, u, q):
                dve.wait_ge(mid_ready, QUARTERS * g + q + 1)
                rows = slice(2 * QS, TRI)
                nc.vector.tensor_tensor(pack[q][u][rows, :], rest[rows, :], mid[rows, :],
                                        ALU.subtract).then_inc(low_ready, 1)

            def softplus_a(g, u):
                chain = Chain(dve, dve_chain, 3 * g)
                dve.wait_ge(soft_ready, g + 1)
                chain.link(nc.vector.tensor_scalar(tmp[3][:, :, :], tmp[1][:, :, :], 1.0, -1.0, ALU.add, ALU.add))
                chain.link(nc.vector.tensor_tensor(tmp[1][:, :, :], tmp[1][:, :, :], tmp[3][:, :, :], ALU.subtract))

            def softplus_b(g, u):
                chain = Chain(dve, dve_chain, 3 * g + 2)
                chain.link(nc.vector.scalar_tensor_tensor(flat(tmp[2]), flat(tmp[0]), 0.0, flat(tmp[2]),
                                                          ALU.max, ALU.add))
                nc.vector.tensor_tensor(dt[u][:, :, :], tmp[2][:, :, :], tmp[1][:, :, :], ALU.add).then_inc(dt_ready, 1)

            def scale_input(g, u):
                dve.wait_ge(dt_ready, g + 1)
                nc.vector.tensor_tensor(dtx[u][:, :, :], dt[u][:, :, :], xg[u][:, :, :], ALU.mult
                                        ).then_inc(dtx_ready, 1)

            def skip(g, u):
                dve.wait_ge(summed, NS * g + NS)
                for t in range(DT):
                    last = nc.vector.scalar_tensor_tensor(tmp[0][:, t, :], xg[u][:, t, :], D_cols[:, t:t + 1],
                                                          y_ps[:, t, :T], ALU.mult, ALU.add)
                last.then_inc(yv_ready, 1)

            def centre(g, u):
                dve.wait_ge(epi_full, EPI * g + MEAN + 1)
                nc.vector.tensor_tensor(tmp[0][:, :, :], tmp[0][:, :, :], over_tiles(aux[:, :T]),
                                        ALU.subtract).then_inc(epi_free, 1)

            def invert(g, u):
                dve.wait_ge(epi_free, EPI * g + VAR + 1)
                nc.vector.reciprocal(std[:, :], std[:, :]).then_inc(rs_ready, 1)

            def rescale(g, u):
                dve.wait_ge(rs_ready, g + 1)
                nc.vector.tensor_tensor(tmp[0][:, :, :], tmp[0][:, :, :], over_tiles(std[:, :]),
                                        ALU.mult).then_inc(yn_ready, 1)

            def add_residual(g, u, half):
                dve.wait_ge(epi_full, EPI * g + WO + half + 1)
                if half == 0:
                    dve.wait_ge(res_loaded[u], 8 * g + 8 * (2 - u))
                rows = xres[u][:TK, 2 * half:2 * half + 2, :]
                nc.vector.tensor_tensor(rows, rows, aux[:TK, :].rearrange("p (k c) -> p k c", k=2),
                                        ALU.add).then_inc(epi_free, 1)

            def flat(t):
                return t[:, :, :].rearrange("p a n -> p (a n)")

            def inject(g, u, n):
                N, v = g * NS + n, n % 2
                dve.wait_ge(B_ready, N + 1)
                wait(dve, scanned, N - 1)
                nc.vector.tensor_tensor(wB[v][:, :, 1:], dtx[u][:, :, :], over_tiles(b_ps[:, v, :T]),
                                        ALU.mult).then_inc(wB_ready, 1)

            def scan(g, n):
                N, v = g * NS + n, n % 2
                dve.wait_ge(wB_ready, N + 1)
                dve.wait_ge(in_ready, N + 1)
                dve.wait_ge(dA_ready, N + 1)
                wait(dve, hC_ready, N - 1)
                wait(dve, carried, N - 1)
                nc.vector.tensor_tensor_scan(flat(hs[v]), flat(dA[v]), flat(wB[v]), 0.0, ALU.mult,
                                             ALU.add).then_inc(scanned, 1)

            def strip(g, u, epi, pro):
                for n in range(NS):
                    if n + 1 < NS:
                        inject(g, u, n + 1)
                    elif pro:
                        dve.wait_ge(dtx_ready, g + 2)
                        inject(g + 1, 1 - u, 0)
                    scan(g, n)
                    if epi:
                        if n == 2:
                            skip(g - 1, 1 - u)
                        if n == 4:
                            centre(g - 1, 1 - u)
                        if n == 7:
                            invert(g - 1, 1 - u)
                        if n == 8:
                            rescale(g - 1, 1 - u)
                        if n in (12, 14):
                            add_residual(g - 1, 1 - u, (n - 12) // 2)
                    if pro:
                        if n in (39, 41, 43, 45):
                            residue(g + 1, 1 - u, (n - 39) // 2)
                        if n in (40, 42, 44, 46):
                            low_part(g + 1, 1 - u, (n - 40) // 2)
                        if n == 58:
                            softplus_a(g + 1, 1 - u)
                        if n == 59:
                            softplus_b(g + 1, 1 - u)
                        if n == 61:
                            scale_input(g + 1, 1 - u)

            for q in range(QUARTERS):
                residue(0, 0, q)
                low_part(0, 0, q)
            softplus_a(0, 0)
            softplus_b(0, 0)
            scale_input(0, 0)
            dve.wait_ge(dtx_ready, 1)
            inject(0, 0, 0)
            run(dve, strip)
            last = STRIPS - 1
            skip(last, 1)
            centre(last, 1)
            invert(last, 1)
            rescale(last, 1)
            for half in range(2):
                add_residual(last, 1, half)

        @block.tensor
        def _(pe):
            pe.wait_ge(s_ready, NREADY)
            pe.wait_ge(s_const, 16 * NCONST)
            pe.wait_ge(diag_ready, 3)

            def convolve(g, t, first, last):
                order = [(1, 1)] + [(y, x) for y in range(CK) for x in range(CK) if (y, x) != (1, 1)]
                if first == 0:
                    pe.wait_ge(halo_loaded, 16 * g + 16)
                    wait(pe, pro_free, PRO * g + t)
                    if t == 0:
                        wait(pe, epi_free, EPI * g - EPI)
                for n in range(first, last):
                    y, x = order[n]
                    dx = x - 1
                    lo, hi = max(0, -dx), min(W, W - dx)
                    step = nc.tensor.matmul(
                        aux[:, :T].rearrange("p (h w) -> p h w", w=W)[:, :, lo:hi], conv_diag[:, CK * y + x, t, :],
                        x_halo[:, t, :].rearrange("p (h w) -> p h w", w=W)[:, y:y + WS, lo + dx:hi + dx],
                        start=n == 0, stop=n == TAPS - 1)
                if last == TAPS:
                    step.then_inc(pro_full, 1)

            def project(g, u, use):
                pe.wait_ge(pro_free, PRO * g + use)
                first = (use - BC) * TRI
                width = RK if use == DTR else TRI
                for t in range(DT):
                    step = nc.tensor.matmul(aux[:width, :T], wx_sb[:, t, first:first + width], xg[u][:, t, :],
                                            start=t == 0, stop=t == DT - 1)
                step.then_inc(pro_full, 1)

            def step_size(g, t):
                pe.wait_ge(pro_free, PRO * g + DT0 + t)
                nc.tensor.matmul(aux[:, :T], wdt_sb[:, t * P:(t + 1) * P], dt_low[:, :], start=True,
                                 stop=True).then_inc(pro_full, 1)

            def average(g, use):
                if use == MEAN:
                    pe.wait_ge(yv_ready, g + 1)
                    if not isinstance(g, int):
                        pe.wait_ge(pro_free, PRO * g + 2 * PRO)
                else:
                    pe.wait_ge(sq_ready, g + 1)
                    pe.wait_ge(epi_free, EPI * g + use)
                src = tmp[0] if use == MEAN else tmp[1]
                for t in range(DT):
                    step = nc.tensor.matmul(aux[:, :T], averager[:, :], src[:, t, :], start=t == 0, stop=t == DT - 1)
                step.then_inc(epi_full, 1)

            def out_project(g, half):
                pe.wait_ge(yo_ready, g + 1)
                pe.wait_ge(epi_free, EPI * g + WO + half)
                for k in range(2):
                    tokens = slice((2 * half + k) * TK, (2 * half + k + 1) * TK)
                    dst = aux[:TK, k * C:(k + 1) * C]
                    nc.tensor.matmul(dst, ones_row[:, :], bout_row[:, :], start=True, stop=False)
                    for t in range(DT):
                        step = nc.tensor.matmul(dst, tmp[3][:, t, tokens], wout_sb[:, t, :], start=False,
                                                stop=t == DT - 1)
                step.then_inc(epi_full, 1)

            def spread(g, u, n, s):
                N = g * NS + n
                if s == 0:
                    dst, semaphore = b_ps[:, n % 2, :T], B_ready
                    wait(pe, wB_ready, N - 1)
                else:
                    dst, semaphore = c_ps[:, :T], C_ready
                    wait(pe, C_copied, N)
                q, r = divmod(s * NS + n, QS)
                nc.tensor.matmul(dst, tri_b[:TRI, r:r + 1].broadcast_to([TRI, P]), pack[q][u][:TRI, :],
                                 start=True, stop=True).then_inc(semaphore, 1)

            def accumulate(g, n):
                pe.wait_ge(hC_ready, g * NS + n + 1)
                if n == 0:
                    wait(pe, yv_ready, g)
                for t in range(DT):
                    step = nc.tensor.matmul(y_ps[:, t, :T], ident[:, :], hC[n % 2][:, t, :], start=n == 0,
                                            stop=n == NS - 1)
                step.then_inc(summed, 1)

            def packs_placed(g):
                pe.wait_ge(pack_done, QUARTERS * g + QUARTERS)
                pe.wait_ge(low_ready, QUARTERS * g + QUARTERS)

            CUTS = [0, 3, 5, 7, 9]

            def strip(g, u, epi, pro):
                for n in range(NS):
                    if n + 2 < NS:
                        spread(g, u, n + 2, 0)
                    elif pro:
                        if n + 2 == NS:
                            packs_placed(g + 1)
                        spread(g + 1, 1 - u, n + 2 - NS, 0)
                    if n >= 2:
                        accumulate(g, n - 2)
                    elif epi:
                        accumulate(g - 1, NS - 2 + n)
                    if n + 1 < NS:
                        spread(g, u, n + 1, 1)
                    elif pro:
                        spread(g + 1, 1 - u, 0, 1)
                    if epi:
                        if n == 3:
                            average(g - 1, MEAN)
                        if n == 6:
                            average(g - 1, VAR)
                        if n in (11, 13):
                            out_project(g - 1, (n - 11) // 2)
                    if pro:
                        if 18 <= n < 38 and (n - 18) % 5 < 4:
                            part = (n - 18) % 5
                            convolve(g + 1, (n - 18) // 5, CUTS[part], CUTS[part + 1])
                        if n in (38, 40, 42, 44, 46):
                            project(g + 1, 1 - u, BC + (n - 38) // 2)
                        if n in (48, 50, 52, 54):
                            step_size(g + 1, (n - 48) // 2)

            for t in range(DT):
                convolve(0, t, 0, TAPS)
            for use in range(BC, DT0):
                project(0, 0, use)
            for t in range(DT):
                step_size(0, t)
            packs_placed(0)
            for n in range(2):
                spread(0, 0, n, 0)
            spread(0, 0, 0, 1)
            run(pe, strip)
            last = STRIPS - 1
            accumulate(last, NS - 2)
            accumulate(last, NS - 1)
            average(last, MEAN)
            average(last, VAR)
            for half in range(2):
                out_project(last, half)

        @block.scalar
        def _(act):
            act.wait_ge(s_const, 16 * NCONST)
            act.wait_ge(a_capped, 1)
            nc.scalar.activation(A_sb[:, :, :], A_sb[:, :, :], ACT.Exp).then_inc(a_exp, 1)
            act.wait_ge(a_ready, 1)
            act.wait_ge(s_ready, NREADY)

            def gelu(g, u, t):
                act.wait_ge(pro_full, PRO * g + t + 1)
                if t == 0:
                    wait(act, yv_ready, g - 1)
                nc.scalar.activation(xg[u][:, t, :], aux[:, :T], ACT.Gelu_apprx_tanh,
                                     bias=conv_bias[:, t:t + 1]).then_inc(pro_free, 1)

            def high_part(g, u, q):
                act.wait_ge(pro_full, PRO * g + BC + q + 1)
                nc.scalar.activation(pack[q][u][:TRI, :], aux[:TRI, :T], ACT.Copy).then_inc(pack_ready, 1)

            def mid_part(g, u, q):
                act.wait_ge(pro_free, PRO * g + BC + q + 1)
                wait(act, low_ready, QUARTERS * g + q)
                wait(act, pack_done, QUARTERS * g + q)
                nc.scalar.activation(mid[:TRI, :], rest[:TRI, :], ACT.Copy).then_inc(mid_ready, 1)

            def place_mid(g, u, q):
                act.wait_ge(mid_ready, QUARTERS * g + q + 1)
                nc.scalar.activation(pack[q][u][QS:2 * QS, :], mid[QS:2 * QS, :], ACT.Copy).then_inc(pack_done, 1)

            def low_rank(g):
                act.wait_ge(pro_full, PRO * g + DTR + 1)
                nc.scalar.activation(dt_low[:, :], aux[:RK, :T], ACT.Copy).then_inc(pro_free, 1)

            def step_bias(g, t):
                act.wait_ge(pro_full, PRO * g + DT0 + t + 1)
                nc.scalar.activation(tmp[0][:, t, :], aux[:, :T], ACT.Identity,
                                     bias=dt_bias[:, t:t + 1]).then_inc(pro_free, 1)

            def softplus_exp(g):
                act.wait_ge(pro_free, PRO * g + PRO)
                chain = Chain(act, act_chain, 2 * g)
                chain.link(nc.scalar.activation(tmp[1][:, :, :], tmp[0][:, :, :], ACT.Abs))
                chain.link(nc.scalar.activation(tmp[1][:, :, :], tmp[1][:, :, :], ACT.Exp, scale=-1.0))
                nc.scalar.activation(tmp[2][:, :, :], tmp[1][:, :, :], ACT.Ln, bias=1.0).then_inc(soft_ready, 1)

            def square(g):
                act.wait_ge(epi_free, EPI * g + MEAN + 1)
                nc.scalar.activation(tmp[1][:, :, :], tmp[0][:, :, :], ACT.Square).then_inc(sq_ready, 1)

            def deviation(g):
                act.wait_ge(epi_full, EPI * g + VAR + 1)
                nc.scalar.activation(std[:, :], aux[:, :T], ACT.Sqrt, bias=eps_col[:, :]).then_inc(epi_free, 1)

            def affine(g):
                act.wait_ge(yn_ready, g + 1)
                for t in range(DT):
                    last = nc.scalar.activation(tmp[3][:, t, :], tmp[0][:, t, :], ACT.Identity,
                                                bias=b_cols[:, t:t + 1], scale=g_cols[:, t:t + 1])
                last.then_inc(yo_ready, 1)

            def carry_out(g, n):
                act.wait_ge(in_ready, g * NS + n + 1)
                nc.scalar.activation(carry[:, n, :], hs[n % 2][:, :, T], ACT.Copy).then_inc(carried, 1)

            def decay(g, u, n):
                N, v = g * NS + n, n % 2
                wait(act, scanned, N - 1)
                if n >= 2:
                    carry_out(g, n - 2)
                elif not isinstance(g, int) or g > 0:
                    carry_out(g - 1, NS - 2 + n)
                wait(act, carried, N - NS + 1)
                nc.scalar.activation(wB[v][:, :, 0], carry[:, n, :], ACT.Copy,
                                     scale=keep_now[u][:, :]).then_inc(in_ready, 1)
                for t in range(DT):
                    last = nc.scalar.activation(dA[v][:, t, 1:], dt[u][:, t, :], ACT.Exp, scale=A_sb[:, t, n:n + 1])
                last.then_inc(dA_ready, 1)

            def copy_C(g, n):
                N, v = g * NS + n, n % 2
                act.wait_ge(C_ready, N + 1)
                wait(act, hC_ready, N - 1)
                nc.scalar.activation(Csb[v][:, :], c_ps[:, :T], ACT.Copy).then_inc(C_copied, 1)

            def strip(g, u, epi, pro):
                nc.scalar.activation(keep_now[u][:, :], keep[:, bass.ds(g, 1)], ACT.Copy).then_inc(keep_ready, 1)
                act.wait_ge(keep_ready, g + 1)
                act.wait_ge(dt_ready, g + 1)
                for n in range(NS):
                    decay(g, u, n)
                    copy_C(g, n)
                    if epi:
                        if n == 5:
                            square(g - 1)
                        if n == 7:
                            deviation(g - 1)
                        if n == 10:
                            affine(g - 1)
                    if pro:
                        if n in (22, 27, 32, 37):
                            gelu(g + 1, 1 - u, (n - 22) // 5)
                        if n in (39, 41, 43, 45):
                            high_part(g + 1, 1 - u, (n - 39) // 2)
                        if n in (40, 42, 44, 46):
                            mid_part(g + 1, 1 - u, (n - 40) // 2)
                        if n in (41, 43, 45, 47):
                            place_mid(g + 1, 1 - u, (n - 41) // 2)
                        if n == 47:
                            low_rank(g + 1)
                        if n in (49, 51, 53, 55):
                            step_bias(g + 1, (n - 49) // 2)
                        if n == 56:
                            softplus_exp(g + 1)

            for t in range(DT):
                gelu(0, 0, t)
            for q in range(QUARTERS):
                high_part(0, 0, q)
                mid_part(0, 0, q)
                place_mid(0, 0, q)
            low_rank(0)
            for t in range(DT):
                step_bias(0, t)
            softplus_exp(0)
            run(act, strip)
            last = STRIPS - 1
            square(last)
            deviation(last)
            affine(last)


def program(nc, a, out):
    QT = nc.dram_tensor("QT", [STRIPS, P, NWIN * CT * WT], F32).ap()
    KT = nc.dram_tensor("KT", [STRIPS * NWIN, P, CT * WT], F32).ap()
    VT = nc.dram_tensor("VT", [NB, CT, P, VROWS * W], F32).ap()
    VN = nc.dram_tensor("VN", [STRIPS * NWIN, WT, C], F32).ap()
    IDX = nc.dram_tensor("IDX", [NB, WPI, TOPK], I32).ap()
    X2 = nc.dram_tensor("X2", [STRIPS, TK, NK * C], F32).ap()
    XI = nc.dram_tensor("XI", [NB, DT, P, XROWS * W], F32).ap()
    with ExitStack() as ctx:
        qsum = ctx.enter_context(nc.sbuf_tensor("qsum", [P, STRIPS * NWSUM], F32))
        ksum = ctx.enter_context(nc.sbuf_tensor("ksum", [P, STRIPS * NWSUM], F32))
        phase_qkv(nc, a["x"], a["L0_conv_ln1_g"], a["L0_conv_ln1_b"], a["L0_conv_qkv_w"], a["L0_conv_qkv_b"],
                  QT, KT, VT, VN, qsum, ksum)
        phase_route(nc, qsum, ksum, IDX)
    phase_attention(nc, a["x"], QT, KT, VT, VN, IDX, a["L0_conv_lepe_w"], a["L0_conv_lepe_b"], a["L0_conv_wo_w"],
                    a["L0_conv_wo_b"], a["L0_conv_ln2_g"], a["L0_conv_ln2_b"], a["L0_conv_mlp_w1"],
                    a["L0_conv_mlp_b1"], a["L0_conv_mlp_w2"], a["L0_conv_mlp_b2"], a["L1_conv_ln1_g"],
                    a["L1_conv_ln1_b"], a["L1_conv_w_in"], a["L1_conv_b_in"], X2, XI)
    phase_scan(nc, a, X2, XI, out)


_INS = ["x", "L0_conv_ln1_g", "L0_conv_ln1_b", "L0_conv_qkv_w", "L0_conv_qkv_b", "L0_conv_lepe_w",
        "L0_conv_lepe_b", "L0_conv_wo_w", "L0_conv_wo_b", "L0_conv_ln2_g", "L0_conv_ln2_b", "L0_conv_mlp_w1",
        "L0_conv_mlp_b1", "L0_conv_mlp_w2", "L0_conv_mlp_b2", "L1_conv_ln1_g", "L1_conv_ln1_b", "L1_conv_w_in",
        "L1_conv_b_in", "L1_conv_conv_w", "L1_conv_conv_b", "L1_conv_w_x", "L1_conv_w_dt", "L1_conv_dt_bias",
        "L1_conv_A_log", "L1_conv_D_skip", "L1_conv_ln2_g", "L1_conv_ln2_b", "L1_conv_w_out", "L1_conv_b_out"]


def kernel(**inputs):
    import numpy as _np
    import concourse.bacc as _bacc
    from concourse import mybir as _mybir
    from concourse.bass_utils import run_bass_kernel_spmd as _run

    nc = _bacc.Bacc("TRN2", target_bir_lowering=False, num_devices=1)
    arrays, args = {}, {}
    for name in _INS:
        a = _np.ascontiguousarray(inputs[name])
        arrays[f"in_{name}_dram"] = a
        args[name] = nc.dram_tensor(f"in_{name}_dram", a.shape, _mybir.dt.from_np(a.dtype), kind="ExternalInput").ap()
    out = nc.dram_tensor("out_0_dram", (NB, H, W, C), _mybir.dt.from_np(_np.dtype("float32")),
                         kind="ExternalOutput").ap()
    program(nc, args, out)
    r = _run(nc, [arrays], core_ids=[0])
    return r.results[0]["out_0_dram"]
```

```python
from contextlib import ExitStack

import concourse.bass as bass
from concourse import mybir

F32 = mybir.dt.float32
BF16 = mybir.dt.bfloat16
I32 = mybir.dt.int32
U32 = mybir.dt.uint32
ALU = mybir.AluOpType
ACT = mybir.ActivationFunctionType
AX = mybir.AxisListType

P = 128
NB, H, W, C = 8, 56, 56, 256
NWIN = 7
WS = H // NWIN
WT = WS * WS
WPI = NWIN * NWIN
T = WS * W
STRIPS = NB * NWIN
NK = 4
TK = T // NK
CT = C // P
HEADS, DH = 8, 32
TOPK = 4
HID = 4 * C
HT = HID // P
SCALE = float(C) ** -0.5
DN = 512
DT = DN // P
NS = 64
RK = 16
EPS0, EPS1 = 1e-6, 1e-5
VROWS = H + WS
LK, CK = 5, 3
XROWS = H + 2
NWSUM = NWIN * CT


class Chain:

    def __init__(self, eng, sem, base):
        self.eng, self.sem, self.base, self.n = eng, sem, base, 0

    def link(self, instruction):
        self.n += 1
        instruction.then_inc(self.sem, 1)
        self.eng.wait_ge(self.sem, self.base + self.n)


def by_window(tokens):
    return tokens.rearrange("p (w h x) -> p h w x", w=NWIN, h=WS)


def columns(v, n):
    return v.rearrange("(t p) -> p t", p=P)


def wait(eng, semaphore, value):
    if not isinstance(value, int) or value > 0:
        eng.wait_ge(semaphore, value)


def load(eng, dst, src, sem):
    eng.dma_start(dst, src, allow_slow_non_contiguous=True).then_inc(sem, 16)


def make_identity(nc, pool, tile, cleared, done):
    nc.gpsimd.memset(tile[:, :], 0.0).then_inc(cleared, 1)
    pool.wait_ge(cleared, 1)
    nc.gpsimd.affine_select(out=tile[:, :], in_=tile[:, :], compare_op=ALU.not_equal, fill=1.0, base=0,
                            pattern=[[-1, P]], channel_multiplier=1).then_inc(done, 1)


def layernorm_stats(nc, chain, x, stats, mv, var_eps, eps, var_ready):
    for k in range(NK - 1):
        nc.vector.bn_stats(stats[:TK, k, :], x[:TK, k, :])
    chain.link(nc.vector.bn_stats(stats[:TK, NK - 1, :], x[:TK, NK - 1, :]))
    even, odd = stats[:TK, :, 1], stats[:TK, :, 4]
    nc.vector.tensor_tensor(mv[:TK, :, 0], even, odd, ALU.add)
    nc.vector.tensor_tensor(mv[:TK, :, 1], even, odd, ALU.subtract)
    chain.link(nc.vector.tensor_tensor(mv[:TK, :, 2], stats[:TK, :, 2], stats[:TK, :, 5], ALU.add))
    nc.vector.tensor_scalar(mv[:TK, :, 0], mv[:TK, :, 0], 0.5, None, ALU.mult)
    nc.vector.tensor_tensor(mv[:TK, :, 1], mv[:TK, :, 1], mv[:TK, :, 1], ALU.mult)
    chain.link(nc.vector.tensor_scalar(mv[:TK, :, 2], mv[:TK, :, 2], 1.0 / C, eps, ALU.mult, ALU.add))
    nc.vector.scalar_tensor_tensor(var_eps[:TK, :], mv[:TK, :, 1], 0.25, mv[:TK, :, 2], ALU.mult,
                                   ALU.add).then_inc(var_ready, 1)


def normalise(nc, x, xn, mv, rstd):
    for k in range(NK):
        last = nc.vector.tensor_scalar(xn[:TK, k, :], x[:TK, k, :], mv[:TK, k, 0:1], rstd[:TK, k:k + 1],
                                       ALU.subtract, ALU.mult)
    return last


def phase_qkv(nc, x, ln_g, ln_b, qkv_w, qkv_b, QT, KT, VT, VN, qsum, ksum):
    with ExitStack() as ctx:
        def sb(name, shape, dt=F32):
            return ctx.enter_context(nc.sbuf_tensor("a_" + name, shape, dt))

        def ps(name, shape, dt=F32):
            return ctx.enter_context(nc.psum_tensor("a_" + name, shape, dt))

        def sem(name):
            return ctx.enter_context(nc.semaphore("a_" + name))

        ident = sb("ident", [P, P])
        w_sb = sb("w", [P, CT, 3 * C])
        b_cols = sb("b_cols", [P, 3 * CT])
        vb_rows = sb("vb_rows", [P, C])
        g_cols = sb("g_cols", [P, CT])
        bb_cols = sb("bb_cols", [P, CT])
        zeros = sb("zeros", [P, NB * CT, 2 * W])
        half = sb("half", [P, NK])
        xin = [sb(f"xin{u}", [P, NK, C]) for u in range(2)]
        xn = [sb(f"xn{u}", [P, NK, C]) for u in range(2)]
        stats = sb("stats", [P, NK, 6])
        mv = sb("mv", [P, NK, 3])
        var_eps = sb("var_eps", [P, NK])
        rstd = sb("rstd", [P, NK])
        xnT = [sb(f"xnT{u}", [P, CT, T]) for u in range(2)]
        q_out = [sb(f"q_out{u}", [P, NWIN, CT, WT]) for u in range(2)]
        k_out = [sb(f"k_out{u}", [P, NWIN, CT, WT]) for u in range(2)]
        vT_out = [sb(f"vT_out{u}", [P, CT, T]) for u in range(2)]
        vn_out = [sb(f"vn_out{u}", [P, NK, C]) for u in range(2)]

        tp = ps("tp", [P, CT, 512])
        qkv_ps = ps("qkv_ps", [P, 3, 512])
        vn_ps = ps("vn_ps", [P, 2, 512])

        s_const = sem("s_const")
        s_clear = sem("s_clear")
        s_ident = sem("s_ident")
        s_zeros = sem("s_zeros")
        s_halo = sem("s_halo")
        x_loaded = [sem(f"x_loaded{u}") for u in range(2)]
        dve_chain = sem("dve_chain")
        var_ready = sem("var_ready")
        rstd_ready = sem("rstd_ready")
        xn_ready = sem("xn_ready")
        tp_ready = sem("tp_ready")
        xnT_ready = sem("xnT_ready")
        qkv_ready = sem("qkv_ready")
        qkv_free = sem("qkv_free")
        vn_ready = sem("vn_ready")
        vn_free = sem("vn_free")
        wsum_done = sem("wsum_done")
        stored = [sem(f"stored{u}") for u in range(2)]
        NCONST = 6
        NSTORE = 5
        PAIRS = STRIPS // 2
        block = ctx.enter_context(nc.Block())

        x_tiles = x.rearrange("b h w c -> (b h w) c").rearrange("(g k p) c -> g p k c", g=STRIPS, k=NK)
        kt_strips = KT.rearrange("(g w) p n -> g p w n", g=STRIPS)
        vn_rows = VN.rearrange("w t c -> (w t) c").rearrange("(g r) c -> g r c", g=STRIPS)
        full = (T // P) * P

        def run(eng, strip):
            strip(0, 0, True)
            strip(1, 1, True)
            with eng.Fori(1, PAIRS - 1) as p:
                strip(2 * p, 0, True)
                strip(2 * p + 1, 1, True)
            strip(STRIPS - 2, 0, True)
            strip(STRIPS - 1, 1, False)

        @block.sync
        def _(sp):
            sp.dma_start(w_sb[:, :, :], qkv_w.rearrange("(t p) n -> p t n", p=P)).then_inc(s_const, 16)
            load(sp, b_cols[:, :], columns(qkv_b, 3 * CT), s_const)
            sp.dma_start(vb_rows[:, :], qkv_b[2 * C:3 * C].rearrange("(a n) -> a n", a=1).broadcast_to([P, C])
                         ).then_inc(s_const, 16)
            load(sp, g_cols[:, :], columns(ln_g, CT), s_const)
            load(sp, bb_cols[:, :], columns(ln_b, CT), s_const)
            sp.dma_start(xin[0][:TK, :, :], x_tiles[0]).then_inc(x_loaded[0], 16)
            sp.dma_start(xin[1][:TK, :, :], x_tiles[1]).then_inc(x_loaded[1], 16)
            sp.wait_ge(s_zeros, 1)
            vt_img = VT.rearrange("b t p n -> p (b t) n")
            sp.dma_start(vt_img[:, :, 0:2 * W], zeros[:, :, :]).then_inc(s_halo, 16)
            sp.dma_start(vt_img[:, :, (H + 2) * W:(H + 4) * W], zeros[:, :, :]).then_inc(s_halo, 16)

            def strip(p, u, prefetch):
                g = 2 * p + u
                img = g // NWIN
                row = (g % NWIN) * T + 2 * W
                sp.wait_ge(qkv_free, 6 * g + 9)
                sp.dma_start(QT[bass.ds(g, 1)].rearrange("g p n -> p (g n)"),
                             q_out[u][:, :, :, :].rearrange("p w t n -> p (w t n)")).then_inc(stored[u], 16)
                sp.dma_start(kt_strips[bass.ds(g, 1)].rearrange("g p w n -> p (g w) n"),
                             k_out[u][:, :, :, :].rearrange("p w t n -> p w (t n)")).then_inc(stored[u], 16)
                sp.dma_start(VT[bass.ds(img, 1), :, :, bass.ds(row, T)].rearrange("b t p n -> p (b t) n"),
                             vT_out[u][:, :, :]).then_inc(stored[u], 16)
                sp.wait_ge(vn_free, 4 * g + 6)
                rows = vn_rows[bass.ds(g, 1)]
                sp.dma_start(rows[:, 0:full, :].rearrange("g (k p) c -> p (g k) c", p=P),
                             vn_out[u][:, 0:T // P, :]).then_inc(stored[u], 16)
                sp.dma_start(rows[:, full:T, :].rearrange("g r c -> (g r) c"),
                             vn_out[u][0:WT, T // P, :]).then_inc(stored[u], 16)
                if prefetch:
                    sp.wait_ge(xn_ready, g + 1)
                    sp.dma_start(xin[u][:TK, :, :],
                                 x_tiles[bass.ds(g + 2, 1)].rearrange("g p k c -> p (g k) c")
                                 ).then_inc(x_loaded[u], 16)

            with sp.Fori(0, PAIRS - 1) as p:
                for u in range(2):
                    strip(p, u, True)
            for u in range(2):
                strip(PAIRS - 1, u, False)
            sp.wait_ge(s_halo, 32)
            for u in range(2):
                sp.wait_ge(stored[u], 16 * NSTORE * PAIRS)

        @block.gpsimd
        def _(pool):
            make_identity(nc, pool, ident, s_clear, s_ident)
            nc.gpsimd.memset(half[:, :], -0.5).then_inc(s_clear, 1)
            nc.gpsimd.memset(zeros[:, :, :], 0.0).then_inc(s_zeros, 1)
            pool.wait_ge(s_clear, 2)
            with pool.Fori(0, STRIPS) as g:
                pool.wait_ge(var_ready, g + 1)
                nc.gpsimd.tensor_tensor(rstd[:TK, :], var_eps[:TK, :], half[:TK, :], ALU.pow).then_inc(rstd_ready, 1)

        @block.vector
        def _(dve):
            dve.wait_ge(s_const, 16 * (NCONST - 1))
            dve.sem_inc(vn_free, 2)

            def norm(g, u):
                chain = Chain(dve, dve_chain, 3 * g)
                dve.wait_ge(x_loaded[u], 8 * g + 8 * (2 - u))
                layernorm_stats(nc, chain, xin[u], stats, mv, var_eps, EPS0, var_ready)
                dve.wait_ge(rstd_ready, g + 1)
                wait(dve, tp_ready, CT * g)
                normalise(nc, xin[u], xn[u], mv, rstd).then_inc(xn_ready, 1)

            def strip(g, u, ahead):
                if ahead:
                    norm(g + 1, 1 - u)
                wait(dve, stored[u], 8 * NSTORE * (g - u))
                for k in range(NK):
                    n = P if k < T // P else WT
                    dve.wait_ge(vn_ready, NK * g + k + 1)
                    nc.vector.tensor_tensor(vn_out[u][:n, k, :], vn_ps[:n, k % 2, :C], vb_rows[:n, :],
                                            ALU.add).then_inc(vn_free, 1)
                dve.wait_ge(qkv_free, 6 * g + 9)
                for src, dst in ((q_out, qsum), (k_out, ksum)):
                    nc.vector.tensor_reduce(dst[:, bass.ds(g * NWSUM, NWSUM)],
                                            src[u][:, :, :, :].rearrange("p w t n -> p (w t) n"), AX.X,
                                            ALU.add).then_inc(wsum_done, 1)

            norm(0, 0)
            run(dve, strip)

        @block.tensor
        def _(pe):
            pe.wait_ge(s_ident, 1)
            pe.wait_ge(s_const, 16 * (NCONST - 1))

            def transpose(g, u):
                pe.wait_ge(xn_ready, g + 1)
                wait(pe, xnT_ready, CT * g)
                for ct in range(CT):
                    for k in range(NK):
                        last = nc.tensor.transpose(tp[:, ct, k * TK:(k + 1) * TK],
                                                   xn[u][:TK, k, ct * P:(ct + 1) * P], ident[:TK, :TK])
                    last.then_inc(tp_ready, 1)

            def strip(g, u, ahead):
                pe.wait_ge(xnT_ready, CT * g + CT)
                for m in range(3 * CT):
                    pe.wait_ge(qkv_free, 6 * g + m + 1)
                    for ct in range(CT):
                        last = nc.tensor.matmul(qkv_ps[:, m % 3, :T], w_sb[:, ct, m * P:(m + 1) * P],
                                                xnT[u][:, ct, :], start=ct == 0, stop=ct == CT - 1)
                    last.then_inc(qkv_ready, 1)
                if ahead:
                    transpose(g + 1, 1 - u)
                for k in range(NK):
                    n = 2 if k < T // P else 1
                    pe.wait_ge(vn_free, NK * g + k + 1)
                    for ct in range(CT):
                        tokens = xnT[u][:, ct, 2 * k * WT:(2 * k + n) * WT]
                        last = nc.tensor.matmul(vn_ps[:n * WT, k % 2, :C], tokens, w_sb[:, ct, 2 * C:3 * C],
                                                start=ct == 0, stop=ct == CT - 1)
                    last.then_inc(vn_ready, 1)

            transpose(0, 0)
            run(pe, strip)

        @block.scalar
        def _(act):
            act.wait_ge(s_const, 16 * (NCONST - 1))
            act.sem_inc(qkv_free, 3)

            def affine(g, u):
                wait(act, vn_ready, NK * g - NK)
                for ct in range(CT):
                    act.wait_ge(tp_ready, CT * g + ct + 1)
                    nc.scalar.activation(by_window(xnT[u][:, ct, :]), tp[:, ct, :T], ACT.Identity,
                                         bias=bb_cols[:, ct:ct + 1], scale=g_cols[:, ct:ct + 1]
                                         ).then_inc(xnT_ready, 1)

            def strip(g, u, ahead):
                wait(act, stored[u], 8 * NSTORE * (g - u))
                wait(act, wsum_done, 2 * g)
                for m in range(3 * CT):
                    act.wait_ge(qkv_ready, 6 * g + m + 1)
                    if m < 2 * CT:
                        out, src = (q_out, k_out)[m // CT][u][:, :, m % CT, :], qkv_ps[:, m % 3, :T]
                    else:
                        out, src = vT_out[u][:, m % CT, :], by_window(qkv_ps[:, m % 3, :T])
                    nc.scalar.activation(out, src, ACT.Identity, bias=b_cols[:, m:m + 1]).then_inc(qkv_free, 1)
                if ahead:
                    affine(g + 1, 1 - u)

            affine(0, 0)
            run(act, strip)


def phase_route(nc, qsum, ksum, IDX):
    with ExitStack() as ctx:
        def sb(name, shape, dt=F32):
            return ctx.enter_context(nc.sbuf_tensor("r_" + name, shape, dt))

        def sem(name):
            return ctx.enter_context(nc.semaphore("r_" + name))

        logits_ps = ctx.enter_context(nc.psum_tensor("r_logits_ps", [P, NB, 512], F32))
        qmean = sb("qmean", [P, STRIPS * NWIN, CT])
        kmean = sb("kmean", [P, STRIPS * NWIN, CT])
        logits = sb("logits", [P, NB, WPI])
        top = sb("top", [P, NB, 8])
        top_at = sb("top_at", [P, NB, 8], U32)
        idx = sb("idx", [P, NB, TOPK], I32)
        means = sem("means")
        scored = sem("scored")
        chained = sem("chained")
        picked = sem("picked")
        stored = sem("stored")
        block = ctx.enter_context(nc.Block())

        @block.vector
        def _(dve):
            nc.vector.tensor_scalar(qmean[:, :, :].rearrange("p w t -> p (w t)"), qsum[:, :], 1.0 / WT, SCALE,
                                    ALU.mult, ALU.mult).then_inc(means, 1)
            nc.vector.tensor_scalar(kmean[:, :, :].rearrange("p w t -> p (w t)"), ksum[:, :], 1.0 / WT, None,
                                    ALU.mult).then_inc(means, 1)
            chain = Chain(dve, chained, 0)
            dve.wait_ge(scored, 1)
            chain.link(nc.vector.tensor_copy(logits[:WPI, :, :], logits_ps[:WPI, :, :WPI]))
            for b in range(NB):
                chain.link(nc.vector.max(top[:WPI, b, :], logits[:WPI, b, :]))
                chain.link(nc.vector.max_index(top_at[:WPI, b, :], top[:WPI, b, :], logits[:WPI, b, :]))
                nc.vector.tensor_scalar(idx[:WPI, b, :], top_at[:WPI, b, :TOPK], float(b * WPI), None,
                                        ALU.add).then_inc(picked, 1)

        @block.tensor
        def _(pe):
            pe.wait_ge(means, 2)
            for b in range(NB):
                for ct in range(CT):
                    last = nc.tensor.matmul(logits_ps[:WPI, b, :WPI], qmean[:, b * WPI:(b + 1) * WPI, ct],
                                            kmean[:, b * WPI:(b + 1) * WPI, ct], start=ct == 0, stop=ct == CT - 1)
            last.then_inc(scored, 1)

        @block.sync
        def _(sp):
            sp.wait_ge(picked, NB)
            sp.dma_start(IDX.rearrange("b w k -> w b k"), idx[:WPI, :, :]).then_inc(stored, 16)
            sp.wait_ge(stored, 16)


def phase_attention(nc, x, QT, KT, VT, VN, IDX, lepe_w, lepe_b, wo_w, wo_b, ln2_g, ln2_b, w1, b1, w2, b2,
                    l1_g, l1_b, w_in, b_in, X2, XI):
    with ExitStack() as ctx:
        def sb(name, shape, dt=F32):
            return ctx.enter_context(nc.sbuf_tensor("b_" + name, shape, dt))

        def ps(name, shape, dt=F32):
            return ctx.enter_context(nc.psum_tensor("b_" + name, shape, dt))

        def sem(name):
            return ctx.enter_context(nc.semaphore("b_" + name))

        PAIRS = STRIPS // 2
        NPAIR = HEADS // 2
        NKEY = TOPK * WT
        TAPS = LK * LK
        ident = sb("ident", [P, P])
        half = sb("half", [P, NK])
        zeros = sb("zeros", [P, NB * DT, W])
        idx = sb("idx", [1, STRIPS * NWIN * TOPK], I32)
        lepe_k = sb("lepe_k", [P, CT, TAPS])
        lepe_bias = sb("lepe_bias", [P, CT])
        wo_sb = sb("wo_sb", [P, CT, C])
        wob_rows = sb("wob_rows", [P, C])
        g2 = sb("g2", [P, CT])
        bb2 = sb("bb2", [P, CT])
        w1_sb = sb("w1_sb", [P, CT, HID])
        b1_cols = sb("b1_cols", [P, HT])
        w2_sb = sb("w2_sb", [P, HT, C])
        b2_rows = sb("b2_rows", [P, C])
        g3 = sb("g3", [P, CT])
        bb3 = sb("bb3", [P, CT])
        win_sb = sb("win_sb", [P, CT, DN])
        bin_cols = sb("bin_cols", [P, DT])

        xr = [sb(f"xr{u}", [P, NK, C]) for u in range(2)]
        q_blk = [sb(f"q_blk{u}", [P, NWIN, CT, 4, WT]) for u in range(2)]
        v_halo = sb("v_halo", [P, CT, (WS + LK - 1) * W])
        k_sel = [sb(f"k_sel{w}", [P, TOPK, CT, WT]) for w in range(2)]
        v_sel = [sb(f"v_sel{w}", [P, TOPK // 2, C]) for w in range(2)]
        row_max = sb("row_max", [P, 2, NPAIR])
        neg_max = sb("neg_max", [P, 2, NPAIR])
        row_sum = sb("row_sum", [P, 2, NPAIR])
        inv_sum = sb("inv_sum", [P, 2, NPAIR])
        probs = [sb(f"probs{w}", [P, NPAIR, NKEY]) for w in range(2)]
        probsT = [sb(f"probsT{w}", [P, 2, NPAIR, P]) for w in range(2)]
        attn = sb("attn", [P, CT, T])
        lepe = sb("lepe", [P, CT, T])
        stats = sb("stats", [P, NK, 6])
        mv = sb("mv", [P, NK, 3])
        var_eps = sb("var_eps", [P, NK])
        rstd = sb("rstd", [P, NK])
        xn = sb("xn", [P, NK, C])
        xnT = sb("xnT", [P, CT, T])
        hid = sb("hid", [P, HT, T])
        xi = sb("xi", [P, DT, T])

        scores = ps("scores", [P, 2, 512])
        tail_ps = ps("tail_ps", [P, 2, 512])
        spare = ps("spare", [P, 512])
        pt = ps("pt", [P, 2, 512])
        oT = ps("oT", [P, CT, 4 * WT])

        s_const = sem("s_const")
        s_clear = sem("s_clear")
        s_ident = sem("s_ident")
        s_zeros = sem("s_zeros")
        s_halo = sem("s_halo")
        q_zeroed = sem("q_zeroed")
        s_idx = sem("s_idx")
        x_loaded = [sem(f"x_loaded{u}") for u in range(2)]
        q_loaded = [sem(f"q_loaded{u}") for u in range(2)]
        v_loaded = sem("v_loaded")
        k_loaded = [sem(f"k_loaded{w}") for w in range(2)]
        vsel_loaded = [sem(f"vsel_loaded{w}") for w in range(2)]
        scored = sem("scored")
        negmax_ready = sem("negmax_ready")
        exp_done = sem("exp_done")
        probs_ready = sem("probs_ready")
        pt_ready = sem("pt_ready")
        pt_taken = sem("pt_taken")
        max_done = sem("max_done")
        inverted = sem("inverted")
        tapped = sem("tapped")
        taps_done = sem("taps_done")
        oT_ready = sem("oT_ready")
        oT_taken = sem("oT_taken")
        dve_chain = sem("dve_chain")
        biased = sem("biased")
        attn_ready = sem("attn_ready")
        y_ready = sem("y_ready")
        var_ready = sem("var_ready")
        rstd_ready = sem("rstd_ready")
        xn_ready = sem("xn_ready")
        tp_ready = sem("tp_ready")
        xnT_ready = sem("xnT_ready")
        hid_scored = sem("hid_scored")
        hid_ready = sem("hid_ready")
        mlp_ready = sem("mlp_ready")
        x2_ready = sem("x2_ready")
        xi_scored = sem("xi_scored")
        xi_ready = sem("xi_ready")
        x2_stored = [sem(f"x2_stored{u}") for u in range(2)]
        xi_stored = sem("xi_stored")
        block = ctx.enter_context(nc.Block())

        x_tiles = x.rearrange("b h w c -> (b h w) c").rearrange("(g k p) c -> g p k c", g=STRIPS, k=NK)
        qt_heads = QT.rearrange("g (a d) (w t n) -> g a d w t n", a=4, w=NWIN, t=CT)

        consts = [
            (lepe_k, lepe_w.rearrange("a b o (t p) -> p t (a b o)", p=P)),
            (lepe_bias, columns(lepe_b, CT)),
            (wo_sb, wo_w.rearrange("(t p) n -> p t n", p=P)),
            (wob_rows, wo_b.rearrange("(a n) -> a n", a=1).broadcast_to([P, C])),
            (g2, columns(ln2_g, CT)),
            (bb2, columns(ln2_b, CT)),
            (w1_sb, w1.rearrange("(t p) n -> p t n", p=P)),
            (b1_cols, columns(b1, HT)),
            (w2_sb, w2.rearrange("(t p) n -> p t n", p=P)),
            (b2_rows, b2.rearrange("(a n) -> a n", a=1).broadcast_to([P, C])),
            (g3, columns(l1_g, CT)),
            (bb3, columns(l1_b, CT)),
            (win_sb, w_in.rearrange("(t p) n -> p t n", p=P)),
            (bin_cols, columns(b_in, DT)),
        ]
        NCONST = len(consts) + CT - 1

        def loads(g, u, i):
            return 8 * TOPK * (7 * (g - u)) + 16 * TOPK * ((7 * u + i) // 2 + 1)

        def run(eng, strip):
            strip(0, 0, False, False)
            strip(1, 1, True, False)
            with eng.Fori(1, PAIRS) as p:
                strip(2 * p, 0, True, True)
                strip(2 * p + 1, 1, True, True)

        @block.sync
        def _(sp):
            sp.dma_start(idx[:, :], IDX.rearrange("b w k -> (b w k)").rearrange("(a n) -> a n", a=1)
                         ).then_inc(s_idx, 16)
            for t in range(CT):
                load(sp, lepe_k[:, t, :], lepe_w.rearrange("a b o (t p) -> t p (a b o)", p=P)[t], s_const)
            for dst, src in consts[1:]:
                load(sp, dst[(slice(None),) * len(dst.shape)], src, s_const)
            sp.wait_ge(s_zeros, 1)
            xi_img = XI.rearrange("b t p n -> p (b t) n")
            sp.dma_start(xi_img[:, :, 0:W], zeros[:, :, :]).then_inc(s_halo, 16)
            sp.dma_start(xi_img[:, :, (H + 1) * W:XROWS * W], zeros[:, :, :]).then_inc(s_halo, 16)
            sp.wait_ge(s_idx, 16)
            sp.wait_ge(q_zeroed, 2)

            def load_q(g, u):
                for h in range(4):
                    for t in range(CT):
                        sp.dma_start(q_blk[u][h * DH:(h + 1) * DH, :, t, h, :],
                                     qt_heads[bass.ds(g, 1), h, :, :, t, :].rearrange("g d w n -> d (g w) n")
                                     ).then_inc(q_loaded[u], 16)

            def load_window(g, u, i):
                w = (7 * u + i) % 2
                wins = [sp.value_load(idx[0:1, bass.ds(g * (NWIN * TOPK) + (i * TOPK + s), 1)],
                                      min_val=0, max_val=NB * WPI - 1) for s in range(TOPK)]
                wait(sp, scored, 7 * g + i - 1)
                for s, win in enumerate(wins):
                    sp.dma_start(k_sel[w][:, s, :, :].rearrange("p t n -> p (t n)"),
                                 KT[bass.ds(win, 1)].rearrange("w p n -> p (w n)")).then_inc(k_loaded[w], 16)
                wait(sp, oT_ready, 7 * g + i - 1)
                for s, win in enumerate(wins):
                    sp.dma_start(v_sel[w][(s % 2) * WT:(s % 2 + 1) * WT, s // 2, :],
                                 VN[bass.ds(win, 1)].rearrange("w t c -> t (w c)")).then_inc(vsel_loaded[w], 16)

            def store_x2(g, u):
                sp.wait_ge(x2_ready, g + 1)
                sp.wait_ge(xn_ready, 2 * g + 2)
                sp.dma_start(X2[bass.ds(g, 1)].rearrange("g p n -> p (g n)"),
                             xr[u][:TK, :, :].rearrange("p k c -> p (k c)")).then_inc(x2_stored[u], 16)

            def store_xi(g):
                sp.wait_ge(xi_ready, DT * g + DT)
                sp.dma_start(XI[bass.ds(g // NWIN, 1), :, :, bass.ds((g % NWIN) * T + W, T)]
                             .rearrange("b t p n -> p (b t) n"), xi[:, :, :]).then_inc(xi_stored, 16)

            def strip(g, u, tail, tail_end):
                wait(sp, taps_done, g)
                sp.dma_start(v_halo[:, :, :],
                             VT[bass.ds(g // NWIN, 1), :, :, bass.ds((g % NWIN) * T, (WS + LK - 1) * W)]
                             .rearrange("b t p n -> p (b t) n")).then_inc(v_loaded, 16)
                load_window(g, u, 1)
                if tail_end:
                    store_x2(g - 2, u)
                    sp.wait_ge(x2_stored[u], 8 * (g - u))
                sp.dma_start(xr[u][:TK, :, :], x_tiles[bass.ds(g, 1)].rearrange("g p k c -> p (g k) c")
                             ).then_inc(x_loaded[u], 16)
                load_window(g, u, 2)
                if not isinstance(g, int) or g > 0:
                    load_q(g + 1, 1 - u)
                for i in range(3, NWIN):
                    load_window(g, u, i)
                    if i == 3 and tail_end:
                        store_xi(g - 2)
                load_window(g + 1, 1 - u, 0)

            sp.sem_inc(xi_stored, 16)
            load_q(0, 0)
            load_q(1, 1)
            load_window(0, 0, 0)
            strip(0, 0, False, False)
            strip(1, 1, True, False)
            with sp.Fori(1, PAIRS - 1) as p:
                strip(2 * p, 0, True, True)
                strip(2 * p + 1, 1, True, True)
            strip(STRIPS - 2, 0, True, True)
            g, u = STRIPS - 1, 1
            sp.wait_ge(taps_done, g)
            sp.dma_start(v_halo[:, :, :],
                         VT[g // NWIN:g // NWIN + 1, :, :, (g % NWIN) * T:(g % NWIN) * T + (WS + LK - 1) * W]
                         .rearrange("b t p n -> p (b t) n")).then_inc(v_loaded, 16)
            load_window(g, u, 1)
            store_x2(g - 2, u)
            sp.wait_ge(x2_stored[u], 8 * (g - u))
            sp.dma_start(xr[u][:TK, :, :], x_tiles[g]).then_inc(x_loaded[u], 16)
            for i in range(2, NWIN):
                load_window(g, u, i)
            store_xi(g - 2)
            store_x2(g - 1, 0)
            store_xi(g - 1)
            store_x2(g, 1)
            store_xi(g)
            sp.wait_ge(s_halo, 32)
            sp.wait_ge(xi_stored, 16 * STRIPS + 16)
            for u in range(2):
                sp.wait_ge(x2_stored[u], 8 * STRIPS)

        @block.gpsimd
        def _(pool):
            make_identity(nc, pool, ident, s_clear, s_ident)
            nc.gpsimd.memset(half[:, :], -0.5).then_inc(s_clear, 1)
            nc.gpsimd.memset(zeros[:, :, :], 0.0).then_inc(s_zeros, 1)
            for u in range(2):
                nc.gpsimd.memset(q_blk[u][:, :, :, :, :], 0.0).then_inc(q_zeroed, 1)
            pool.wait_ge(s_const, 16 * NCONST)
            pool.wait_ge(s_clear, 2)

            def strip(p, u):
                g = 2 * p + u
                pool.wait_ge(x_loaded[u], 16 * p + 16)
                nc.gpsimd.tensor_tensor(xr[u][:TK, :, :], xr[u][:TK, :, :],
                                        wob_rows[:TK, :].rearrange("p (a n) -> p a n", a=1).broadcast_to([TK, NK, C]),
                                        ALU.add).then_inc(biased, 1)
                pool.wait_ge(var_ready, 2 * g + 1)
                nc.gpsimd.tensor_tensor(rstd[:TK, :], var_eps[:TK, :], half[:TK, :], ALU.pow).then_inc(rstd_ready, 1)
                pool.wait_ge(xn_ready, 2 * g + 1)
                nc.gpsimd.tensor_tensor(xr[u][:TK, :, :], xr[u][:TK, :, :],
                                        b2_rows[:TK, :].rearrange("p (a n) -> p a n", a=1).broadcast_to([TK, NK, C]),
                                        ALU.add).then_inc(biased, 1)
                pool.wait_ge(var_ready, 2 * g + 2)
                nc.gpsimd.tensor_tensor(rstd[:TK, :], var_eps[:TK, :], half[:TK, :], ALU.pow).then_inc(rstd_ready, 1)

            with pool.Fori(0, PAIRS) as p:
                for u in range(2):
                    strip(p, u)

        @block.vector
        def _(dve):
            dve.wait_ge(s_const, 16 * NCONST)
            ORDER = [(LK // 2, LK // 2)] + [(y, x) for y in range(LK) for x in range(LK)
                                            if (y, x) != (LK // 2, LK // 2)]

            def lepe_taps(g, first, last):
                for n in range(first, last):
                    y, x = ORDER[n]
                    dx = x - LK // 2
                    lo, hi = max(0, -dx), min(W, W - dx)
                    for t in range(CT):
                        wait(dve, tapped, CT * TAPS * g + CT * n + t - 1)
                        grid = lepe[:, t, :].rearrange("p (h w) -> p h w", h=WS)[:, :, lo:hi]
                        src = v_halo[:, t, :].rearrange("p (h w) -> p h w", w=W)[:, y:y + WS, lo + dx:hi + dx]
                        tap = lepe_k[:, t, y * LK + x:y * LK + x + 1]
                        if n == 0:
                            step = nc.vector.tensor_scalar(grid, src, tap, lepe_bias[:, t:t + 1], ALU.mult, ALU.add)
                        else:
                            step = nc.vector.scalar_tensor_tensor(grid, src, tap, grid, ALU.mult, ALU.add)
                        step.then_inc(tapped, 1)
                if last == TAPS:
                    dve.wait_ge(tapped, CT * TAPS * g + CT * TAPS)
                    dve.sem_inc(taps_done, 1)

            def maximum(g, u, i):
                w = (7 * u + i) % 2
                dve.wait_ge(scored, 7 * g + i + 1)
                nc.vector.tensor_reduce(row_max[:, w, :], scores[:, :, :].rearrange("p a (b n) -> p (a b) n", b=2),
                                        AX.X, ALU.max).then_inc(max_done, 1)
                dve.wait_ge(max_done, 7 * g + i + 1)
                nc.vector.tensor_scalar(neg_max[:, w, :], row_max[:, w, :], -SCALE, None,
                                        ALU.mult).then_inc(negmax_ready, 1)

            def divide(g, u, i):
                w = (7 * u + i) % 2
                dve.wait_ge(exp_done, 7 * g + i + 1)
                nc.vector.reciprocal(inv_sum[:, w, :], row_sum[:, w, :]).then_inc(inverted, 1)
                dve.wait_ge(inverted, 7 * g + i + 1)
                for j in range(NPAIR):
                    last = nc.vector.tensor_scalar(probs[w][:, j, :], probs[w][:, j, :], inv_sum[:, w, j:j + 1],
                                                   None, ALU.mult)
                last.then_inc(probs_ready, 1)

            def take_output(g, i):
                dve.wait_ge(oT_ready, 7 * g + i + 1)
                if i == 0:
                    wait(dve, y_ready, g)
                out = attn[:, :, :].rearrange("p t (h w x) -> p t w h x", h=WS, w=NWIN)[:, :, i]
                nc.vector.tensor_copy(out, oT[:, :, :WT].rearrange("p t (h x) -> p t h x", h=WS)
                                      ).then_inc(oT_taken, 1)

            def add_lepe(g):
                dve.wait_ge(oT_taken, 7 * g + NWIN)
                dve.wait_ge(taps_done, g + 1)
                nc.vector.tensor_tensor(attn[:, :, :], attn[:, :, :], lepe[:, :, :], ALU.add).then_inc(attn_ready, 1)

            def residual_norm(g, u):
                chain = Chain(dve, dve_chain, 7 * g)
                dve.wait_ge(y_ready, g + 1)
                dve.wait_ge(biased, 2 * g + 1)
                chain.link(nc.vector.tensor_tensor(xr[u][:TK, :, :], xr[u][:TK, :, :],
                                                   tail_ps[:TK, :, :].rearrange("p a (b n) -> p (a b) n", b=2),
                                                   ALU.add))
                layernorm_stats(nc, chain, xr[u], stats, mv, var_eps, EPS0, var_ready)
                dve.wait_ge(rstd_ready, 2 * g + 1)
                wait(dve, tp_ready, 4 * g)
                normalise(nc, xr[u], xn, mv, rstd).then_inc(xn_ready, 1)

            def mlp_norm(g, u):
                chain = Chain(dve, dve_chain, 7 * g + 4)
                dve.wait_ge(mlp_ready, g + 1)
                dve.wait_ge(biased, 2 * g + 2)
                nc.vector.tensor_tensor(xr[u][:TK, :, :], xr[u][:TK, :, :],
                                        tail_ps[:TK, :, :].rearrange("p a (b n) -> p (a b) n", b=2),
                                        ALU.add).then_inc(x2_ready, 1)
                dve.wait_ge(x2_ready, g + 1)
                layernorm_stats(nc, chain, xr[u], stats, mv, var_eps, EPS1, var_ready)
                dve.wait_ge(rstd_ready, 2 * g + 2)
                dve.wait_ge(tp_ready, 4 * g + 2)
                normalise(nc, xr[u], xn, mv, rstd).then_inc(xn_ready, 1)

            CUTS = [0, 4, 6, 11, 15, 19, 23, TAPS]

            def strip(g, u, tail, tail_end):
                for i in range(NWIN):
                    maximum(g, u, i)
                    if i > 0:
                        lepe_taps(g, CUTS[i], CUTS[i + 1])
                    divide(g, u, i)
                    if i > 0:
                        take_output(g, i - 1)
                    elif tail:
                        take_output(g - 1, NWIN - 1)
                        add_lepe(g - 1)
                    if i == 0:
                        dve.wait_ge(v_loaded, 16 * g + 16)
                        if tail:
                            dve.wait_ge(attn_ready, g)
                        lepe_taps(g, CUTS[0], CUTS[1])
                    if i == 1 and tail:
                        residual_norm(g - 1, 1 - u)
                    if i == 6 and tail:
                        mlp_norm(g - 1, 1 - u)

            run(dve, strip)
            last = STRIPS - 1
            take_output(last, NWIN - 1)
            add_lepe(last)
            residual_norm(last, 1)
            mlp_norm(last, 1)

        @block.tensor
        def _(pe):
            pe.wait_ge(s_ident, 1)
            pe.wait_ge(s_const, 16 * NCONST)
            banks = [tail_ps[:, 0, :], tail_ps[:, 1, :], spare[:, :]]

            def score(g, u, i):
                w = (7 * u + i) % 2
                if i == 0:
                    pe.wait_ge(q_loaded[u], 64 * (g - u) + 128)
                pe.wait_ge(k_loaded[w], loads(g, u, i))
                wait(pe, exp_done, 7 * g + i)
                for j in range(NPAIR):
                    last = nc.tensor.matmul(
                        scores[:, j // 2, (j % 2) * NKEY:(j % 2 + 1) * NKEY],
                        q_blk[u][:, i, j // 2, 2 * (j % 2):2 * (j % 2) + 2, :],
                        k_sel[w][:, :, j // 2, :], start=True, stop=True)
                last.then_inc(scored, 1)

            def transpose_probs(g, u, i):
                w = (7 * u + i) % 2
                pe.wait_ge(probs_ready, 7 * g + i + 1)
                wait(pe, pt_taken, 7 * g + i)
                for kk in range(2):
                    for j in range(NPAIR):
                        last = nc.tensor.transpose(pt[:, kk, j * P:(j + 1) * P],
                                                   probs[w][:, j, kk * P:(kk + 1) * P], ident[:, :])
                last.then_inc(pt_ready, 1)

            def attend(g, u, i):
                w = (7 * u + i) % 2
                pe.wait_ge(pt_taken, 7 * g + i + 1)
                wait(pe, oT_taken, 7 * g + i)
                pe.wait_ge(vsel_loaded[w], loads(g, u, i))
                for h in range(HEADS):
                    rows = slice((h % 4) * DH, (h % 4 + 1) * DH)
                    for kk in range(2):
                        last = nc.tensor.matmul(
                            oT[rows, h // 4, :WT], v_sel[w][:, kk, h * DH:(h + 1) * DH],
                            probsT[w][:, kk, h // 2, (h % 2) * WT:(h % 2 + 1) * WT],
                            start=kk == 0, stop=kk == 1)
                last.then_inc(oT_ready, 1)

            def project_out(g):
                pe.wait_ge(attn_ready, g + 1)
                wait(pe, xi_ready, DT * g)
                for k in range(NK):
                    for t in range(CT):
                        last = nc.tensor.matmul(tail_ps[:TK, k // 2, (k % 2) * C:(k % 2 + 1) * C],
                                                attn[:, t, k * TK:(k + 1) * TK], wo_sb[:, t, :],
                                                start=t == 0, stop=t == CT - 1)
                last.then_inc(y_ready, 1)

            def transpose_xn(g, n):
                pe.wait_ge(xn_ready, 2 * g + n)
                for ct in range(CT):
                    for k in range(NK):
                        last = nc.tensor.transpose(tail_ps[:, ct, k * TK:(k + 1) * TK],
                                                   xn[:TK, k, ct * P:(ct + 1) * P], ident[:TK, :TK])
                    last.then_inc(tp_ready, 1)

            def mlp_up(g, first, last):
                if first == 0:
                    pe.wait_ge(xnT_ready, 4 * g + 2)
                for m in range(first, last):
                    if m >= 3:
                        pe.wait_ge(hid_ready, HT * g + m - 2)
                    for ct in range(CT):
                        step = nc.tensor.matmul(banks[m % 3][:, :T], w1_sb[:, ct, m * P:(m + 1) * P],
                                                xnT[:, ct, :], start=ct == 0, stop=ct == CT - 1)
                    step.then_inc(hid_scored, 1)

            def mlp_down(g, k):
                if k == 0:
                    pe.wait_ge(hid_ready, HT * g + HT)
                for m in range(HT):
                    step = nc.tensor.matmul(tail_ps[:TK, k // 2, (k % 2) * C:(k % 2 + 1) * C],
                                            hid[:, m, k * TK:(k + 1) * TK], w2_sb[:, m, :],
                                            start=m == 0, stop=m == HT - 1)
                if k == NK - 1:
                    step.then_inc(mlp_ready, 1)

            def project_in(g):
                pe.wait_ge(xnT_ready, 4 * g + 4)
                for m in range(DT):
                    if m >= 3:
                        pe.wait_ge(xi_ready, DT * g + m - 2)
                    for ct in range(CT):
                        step = nc.tensor.matmul(banks[m % 3][:, :T], win_sb[:, ct, m * P:(m + 1) * P],
                                                xnT[:, ct, :], start=ct == 0, stop=ct == CT - 1)
                    step.then_inc(xi_scored, 1)

            def strip(g, u, tail, tail_end):
                for i in range(NWIN):
                    score(g, u, i)
                    if i == 0 and tail_end:
                        transpose_xn(g - 2, 2)
                    if i > 0 and tail:
                        if i == 1:
                            project_out(g - 1)
                        if i == 2:
                            transpose_xn(g - 1, 1)
                        if i == 3:
                            mlp_up(g - 1, 2, 4)
                        if i == 4:
                            mlp_up(g - 1, 6, 8)
                        if i == 5:
                            mlp_down(g - 1, 1)
                        if i == 6:
                            mlp_down(g - 1, 3)
                    if i > 0:
                        transpose_probs(g, u, i - 1)
                    elif tail:
                        transpose_probs(g - 1, 1 - u, NWIN - 1)
                    if i == 2 and tail:
                        mlp_up(g - 1, 0, 1)
                    if i == 3 and tail:
                        mlp_up(g - 1, 4, 5)
                    if i == 0 and tail_end:
                        project_in(g - 2)
                    if i > 0:
                        attend(g, u, i - 1)
                    elif tail:
                        attend(g - 1, 1 - u, NWIN - 1)
                    if tail:
                        if i == 2:
                            mlp_up(g - 1, 1, 2)
                        if i == 3:
                            mlp_up(g - 1, 5, 6)
                        if i == 4:
                            mlp_down(g - 1, 0)
                        if i == 5:
                            mlp_down(g - 1, 2)

            run(pe, strip)
            last = STRIPS - 1
            transpose_xn(last - 1, 2)
            transpose_probs(last, 1, NWIN - 1)
            project_in(last - 1)
            attend(last, 1, NWIN - 1)
            project_out(last)
            transpose_xn(last, 1)
            mlp_up(last, 0, HT)
            for k in range(NK):
                mlp_down(last, k)
            transpose_xn(last, 2)
            project_in(last)

        @block.scalar
        def _(act):
            act.wait_ge(s_const, 16 * NCONST)
            banks = [tail_ps[:, 0, :], tail_ps[:, 1, :], spare[:, :]]

            def exps(g, u, i):
                w = (7 * u + i) % 2
                act.wait_ge(negmax_ready, 7 * g + i + 1)
                wait(act, pt_ready, 7 * g + i - 1)
                for j in range(NPAIR):
                    last = nc.scalar.activation(
                        probs[w][:, j, :], scores[:, j // 2, (j % 2) * NKEY:(j % 2 + 1) * NKEY], ACT.Exp,
                        bias=neg_max[:, w, j:j + 1], scale=SCALE, accum_out=row_sum[:, w, j:j + 1])
                last.then_inc(exp_done, 1)

            def take_probs(g, u, i):
                w = (7 * u + i) % 2
                act.wait_ge(pt_ready, 7 * g + i + 1)
                wait(act, oT_ready, 7 * g + i - 1)
                nc.scalar.activation(probsT[w][:, :, :, :].rearrange("p k j q -> p k (j q)"), pt[:, :, :],
                                     ACT.Copy).then_inc(pt_taken, 1)

            def affine(g, n, gain, shift):
                for ct in range(CT):
                    act.wait_ge(tp_ready, 4 * g + 2 * n + ct + 1)
                    if ct == 0:
                        wait(act, xi_scored if n == 0 else hid_scored, DT * g if n == 0 else HT * g + HT)
                    nc.scalar.activation(xnT[:, ct, :], tail_ps[:, ct, :T], ACT.Identity,
                                         bias=shift[:, ct:ct + 1], scale=gain[:, ct:ct + 1]
                                         ).then_inc(xnT_ready, 1)

            def gelus(g, first, last):
                if first == 0:
                    wait(act, mlp_ready, g)
                for m in range(first, last):
                    act.wait_ge(hid_scored, HT * g + m + 1)
                    nc.scalar.activation(hid[:, m, :], banks[m % 3][:, :T], ACT.Gelu,
                                         bias=b1_cols[:, m:m + 1]).then_inc(hid_ready, 1)

            def take_xi(g):
                act.wait_ge(xi_stored, 16 * g + 16)
                for m in range(DT):
                    act.wait_ge(xi_scored, DT * g + m + 1)
                    nc.scalar.activation(xi[:, m, :], banks[m % 3][:, :T], ACT.Identity,
                                         bias=bin_cols[:, m:m + 1]).then_inc(xi_ready, 1)

            def strip(g, u, tail, tail_end):
                for i in range(NWIN):
                    if i == 0 and tail_end:
                        affine(g - 2, 1, g3, bb3)
                    exps(g, u, i)
                    if i == 2 and tail:
                        affine(g - 1, 0, g2, bb2)
                    if i > 0:
                        take_probs(g, u, i - 1)
                    elif tail:
                        take_probs(g - 1, 1 - u, NWIN - 1)
                    if i == 0 and tail_end:
                        take_xi(g - 2)
                    if tail:
                        if i in (2, 3, 4):
                            first = (0, 2, 6)[i - 2]
                            gelus(g - 1, first, (2, 6, 8)[i - 2])

            run(act, strip)
            last = STRIPS - 1
            affine(last - 1, 1, g3, bb3)
            take_probs(last, 1, NWIN - 1)
            take_xi(last - 1)
            affine(last, 0, g2, bb2)
            gelus(last, 0, HT)
            affine(last, 1, g3, bb3)
            take_xi(last)


def phase_scan(nc, a, X2, XI, out):
    with ExitStack() as ctx:
        def sb(name, shape, dt=F32):
            return ctx.enter_context(nc.sbuf_tensor("c_" + name, shape, dt))

        def ps(name, shape, dt=F32):
            return ctx.enter_context(nc.psum_tensor("c_" + name, shape, dt))

        def sem(name):
            return ctx.enter_context(nc.semaphore("c_" + name))

        QS = 32
        QUARTERS = 2 * NS // QS
        TRI = 3 * QS
        BC, DTR, DT0, PRO = DT, DT + QUARTERS, DT + QUARTERS + 1, DT + QUARTERS + 1 + DT
        MEAN, VAR, WO, EPI = 0, 1, 2, 4
        A_LOG_MAX = 80.0
        TAPS = CK * CK
        T1 = T + 1
        TV = T - 3 * W // 2

        ident = sb("ident", [P, P])
        tri_f = sb("tri_f", [P, QS])
        tri_b = sb("tri_b", [P, QS], BF16)
        averager = sb("averager", [P, P])
        eps_col = sb("eps_col", [P, 1])
        ones_row = sb("ones_row", [1, TK])
        keep = sb("keep", [P, STRIPS])
        keep_now = [sb(f"keep_now{u}", [P, 1]) for u in range(2)]
        conv_k = sb("conv_k", [P, DT, TAPS])
        conv_diag = sb("conv_diag", [P, TAPS, DT, P])
        conv_bias = sb("conv_bias", [P, DT])
        wx_sb = sb("wx_sb", [P, DT, QUARTERS * TRI + RK])
        wdt_sb = sb("wdt_sb", [RK, DN])
        dt_bias = sb("dt_bias", [P, DT])
        A_sb = sb("A_sb", [P, DT, NS])
        D_cols = sb("D_cols", [P, DT])
        g_cols = sb("g_cols", [P, DT])
        b_cols = sb("b_cols", [P, DT])
        wout_sb = sb("wout_sb", [P, DT, C])
        bout_row = sb("bout_row", [1, C])

        x_halo = sb("x_halo", [P, DT, (WS + CK - 1) * W])
        xres = [sb(f"xres{u}", [P, NK, C]) for u in range(2)]
        xg = [sb(f"xg{u}", [P, DT, T]) for u in range(2)]
        dt = [sb(f"dt{u}", [P, DT, T]) for u in range(2)]
        dtx = [sb(f"dtx{u}", [P, DT, T]) for u in range(2)]
        pack = [[sb(f"pack{q}{u}", [P, T], BF16) for u in range(2)] for q in range(QUARTERS)]
        rest = sb("rest", [P, T])
        mid = sb("mid", [P, T], BF16)
        dt_low = sb("dt_low", [RK, T])
        tmp = [sb(f"tmp{n}", [P, DT, T]) for n in range(4)]
        std = sb("std", [P, T])

        dA = [sb(f"dA{v}", [P, DT, T1]) for v in range(2)]
        wB = [sb(f"wB{v}", [P, DT, T1]) for v in range(2)]
        hs = [sb(f"hs{v}", [P, DT, T1]) for v in range(2)]
        hC = [sb(f"hC{v}", [P, DT, T]) for v in range(2)]
        B_rest = [sb(f"B_rest{v}", [P, T - TV]) for v in range(2)]
        Csb = [sb(f"Csb{v}", [P, T]) for v in range(2)]
        carry = sb("carry", [P, NS, DT])

        y_ps = ps("y_ps", [P, DT, 512])
        b_ps = ps("b_ps", [P, 512])
        c_ps = ps("c_ps", [P, 512])
        pro_ps = ps("pro_ps", [P, 512])
        epi_ps = ps("epi_ps", [P, 512])

        s_const = sem("s_const")
        s_clear = sem("s_clear")
        s_ready = sem("s_ready")
        diag_ready = sem("diag_ready")
        a_capped = sem("a_capped")
        a_exp = sem("a_exp")
        a_ready = sem("a_ready")
        halo_loaded = sem("halo_loaded")
        res_loaded = [sem(f"res_loaded{u}") for u in range(2)]
        out_stored = [sem(f"out_stored{u}") for u in range(2)]
        pro_full = sem("pro_full")
        pro_free = sem("pro_free")
        epi_full = sem("epi_full")
        epi_free = sem("epi_free")
        pack_ready = sem("pack_ready")
        mid_ready = sem("mid_ready")
        low_ready = sem("low_ready")
        pack_done = sem("pack_done")
        act_chain = sem("act_chain")
        soft_ready = sem("soft_ready")
        dve_chain = sem("dve_chain")
        dt_ready = sem("dt_ready")
        dtx_ready = sem("dtx_ready")
        keep_ready = sem("keep_ready")
        B_ready = sem("B_ready")
        C_ready = sem("C_ready")
        C_copied = sem("C_copied")
        B_copied = sem("B_copied")
        wB_ready = sem("wB_ready")
        wB_rest_ready = sem("wB_rest_ready")
        in_ready = sem("in_ready")
        dA_ready = sem("dA_ready")
        scanned = sem("scanned")
        carried = sem("carried")
        hC_ready = sem("hC_ready")
        summed = sem("summed")
        yv_ready = sem("yv_ready")
        sq_ready = sem("sq_ready")
        rs_ready = sem("rs_ready")
        yn_ready = sem("yn_ready")
        yo_ready = sem("yo_ready")
        block = ctx.enter_context(nc.Block())

        x2_tiles = X2.rearrange("g p (k c) -> g p k c", k=NK)
        out_tiles = out.rearrange("b h w c -> (b h w) c").rearrange("(g k p) c -> g p k c", g=STRIPS, k=NK)
        w_x = a["L1_conv_w_x"].rearrange("(t p) n -> p t n", p=P)
        consts = [
            (conv_bias[:, :], columns(a["L1_conv_conv_b"], DT)),
            (wx_sb[:, :, QUARTERS * TRI:], w_x[:, :, 0:RK]),
            (wdt_sb[:, :], a["L1_conv_w_dt"]),
            (dt_bias[:, :], columns(a["L1_conv_dt_bias"], DT)),
            (A_sb[:, :, :], a["L1_conv_A_log"].rearrange("(t p) n -> p t n", p=P)),
            (D_cols[:, :], columns(a["L1_conv_D_skip"], DT)),
            (g_cols[:, :], columns(a["L1_conv_ln2_g"], DT)),
            (b_cols[:, :], columns(a["L1_conv_ln2_b"], DT)),
            (wout_sb[:, :, :], a["L1_conv_w_out"].rearrange("(t p) n -> p t n", p=P)),
            (bout_row[:, :], a["L1_conv_b_out"].rearrange("(a n) -> a n", a=1)),
        ] + [(conv_k[:, t, :], a["L1_conv_conv_w"].rearrange("a b o (t p) -> t p (a b o)", p=P)[t])
             for t in range(DT)] + [
            (wx_sb[:, :, (3 * q + c) * QS:(3 * q + c + 1) * QS], w_x[:, :, RK + q * QS:RK + (q + 1) * QS])
            for q in range(QUARTERS) for c in range(3)]
        NCONST = len(consts)
        NREADY = 7

        def over_tiles(row):
            return row.rearrange("p (a n) -> p a n", a=1).broadcast_to([P, DT, row.shape[1]])

        def run(eng, strip):
            strip(0, 0, False, True)
            with eng.Fori(0, STRIPS // 2 - 1) as p:
                strip(2 * p + 1, 1, True, True)
                strip(2 * p + 2, 0, True, True)
            strip(STRIPS - 1, 1, True, False)

        @block.sync
        def _(sp):
            for dst, src in consts:
                load(sp, dst, src, s_const)

            def load_halo(g):
                sp.dma_start(x_halo[:, :, :],
                             XI[bass.ds(g // NWIN, 1), :, :, bass.ds((g % NWIN) * T, (WS + CK - 1) * W)]
                             .rearrange("b t p n -> p (b t) n")).then_inc(halo_loaded, 16)

            def load_residual(g, u):
                sp.dma_start(xres[u][:TK, :, :], x2_tiles[bass.ds(g, 1)].rearrange("g p k c -> p (g k) c")
                             ).then_inc(res_loaded[u], 16)

            def store(g, u):
                sp.wait_ge(epi_free, EPI * g + EPI)
                sp.dma_start(out_tiles[bass.ds(g, 1)].rearrange("g p k c -> p (g k) c"),
                             xres[u][:TK, :, :]).then_inc(out_stored[u], 16)

            def strip(g, u, epi, pro):
                if pro:
                    sp.wait_ge(pro_full, PRO * g + DT)
                    load_halo(g + 1)
                if epi:
                    store(g - 1, 1 - u)
                if pro:
                    if epi:
                        sp.wait_ge(out_stored[1 - u], 8 * (g + 1) if u else 8 * g)
                    load_residual(g + 1, 1 - u)

            load_halo(0)
            load_residual(0, 0)
            run(sp, strip)
            store(STRIPS - 1, 1)
            for u in range(2):
                sp.wait_ge(out_stored[u], 8 * STRIPS)

        @block.gpsimd
        def _(pool):
            make_identity(nc, pool, ident, s_clear, s_ready)
            nc.gpsimd.memset(averager[:, :], 1.0 / DN).then_inc(s_ready, 1)
            nc.gpsimd.memset(eps_col[:, :], EPS1).then_inc(s_ready, 1)
            nc.gpsimd.memset(ones_row[:, :], 1.0).then_inc(s_ready, 1)
            nc.gpsimd.memset(carry[:, :, :], 0.0).then_inc(s_ready, 1)
            nc.gpsimd.memset(keep[:, :], 1.0).then_inc(s_clear, 1)
            pool.wait_ge(s_clear, 2)
            nc.gpsimd.memset(keep[:, :].rearrange("p (b s) -> p b s", s=NWIN)[:, :, 0], 0.0).then_inc(s_ready, 1)
            for v in range(2):
                last = nc.gpsimd.memset(dA[v][:, :, 0], 0.0)
            last.then_inc(s_ready, 1)

            def inject(g, u, n):
                N, v = g * NS + n, n % 2
                pool.wait_ge(B_copied, N + 1)
                wait(pool, scanned, N - 1)
                nc.gpsimd.tensor_tensor(wB[v][:, :, 1 + TV:], dtx[u][:, :, TV:], over_tiles(B_rest[v][:, :]),
                                        ALU.mult).then_inc(wB_rest_ready, 1)

            def strip(g, u, epi, pro):
                for n in range(NS):
                    if n + 1 < NS:
                        inject(g, u, n + 1)
                    elif pro:
                        pool.wait_ge(dtx_ready, g + 2)
                        inject(g + 1, 1 - u, 0)
                    N, v = g * NS + n, n % 2
                    pool.wait_ge(scanned, N + 1)
                    pool.wait_ge(C_copied, N + 1)
                    wait(pool, summed, DT * (N - 1))
                    nc.gpsimd.tensor_tensor(hC[v][:, :, :], hs[v][:, :, 1:], over_tiles(Csb[v][:, :]),
                                            ALU.mult).then_inc(hC_ready, 1)

            pool.wait_ge(dtx_ready, 1)
            inject(0, 0, 0)
            run(pool, strip)

        @block.vector
        def _(dve):
            dve.wait_ge(s_ready, NREADY)
            dve.wait_ge(s_const, 16 * NCONST)
            nc.vector.tensor_tensor(tri_f[:, :], ident[:, 0:QS], ident[:, QS:2 * QS], ALU.add).then_inc(diag_ready, 1)
            dve.wait_ge(diag_ready, 1)
            nc.vector.tensor_tensor(tri_b[:, :], tri_f[:, :], ident[:, 2 * QS:TRI], ALU.add).then_inc(diag_ready, 1)
            nc.vector.tensor_scalar(A_sb[:, :, :], A_sb[:, :, :], A_LOG_MAX, None, ALU.min).then_inc(a_capped, 1)
            for tap in range(TAPS):
                for t in range(DT):
                    last = nc.vector.tensor_scalar(conv_diag[:, tap, t, :], ident[:, :], conv_k[:, t, tap:tap + 1],
                                                   None, ALU.mult)
            last.then_inc(diag_ready, 1)
            dve.wait_ge(a_exp, 1)
            nc.vector.tensor_scalar(A_sb[:, :, :], A_sb[:, :, :], -1.0, None, ALU.mult).then_inc(a_ready, 1)

            def residue(g, u, q):
                dve.wait_ge(pack_ready, QUARTERS * g + q + 1)
                wait(dve, low_ready, QUARTERS * g + q)
                nc.vector.tensor_tensor(rest[:TRI, :], pro_ps[:TRI, :T], pack[q][u][:TRI, :],
                                        ALU.subtract).then_inc(pro_free, 1)

            def low_part(g, u, q):
                dve.wait_ge(mid_ready, QUARTERS * g + q + 1)
                rows = slice(2 * QS, TRI)
                nc.vector.tensor_tensor(pack[q][u][rows, :], rest[rows, :], mid[rows, :],
                                        ALU.subtract).then_inc(low_ready, 1)

            def softplus(g, u, part):
                if part == 0:
                    dve.wait_ge(act_chain, 4 * g + 4)
                    nc.vector.tensor_scalar(tmp[3][:, :, :], tmp[1][:, :, :], 1.0, -1.0, ALU.add, ALU.add
                                            ).then_inc(dve_chain, 1)
                elif part == 1:
                    dve.wait_ge(dve_chain, 3 * g + 1)
                    dve.wait_ge(soft_ready, g + 1)
                    nc.vector.tensor_tensor(tmp[1][:, :, :], tmp[1][:, :, :], tmp[3][:, :, :], ALU.subtract
                                            ).then_inc(dve_chain, 1)
                elif part == 2:
                    nc.vector.scalar_tensor_tensor(flat(tmp[2]), flat(tmp[0]), 0.0, flat(tmp[2]), ALU.max, ALU.add
                                                   ).then_inc(dve_chain, 1)
                else:
                    dve.wait_ge(dve_chain, 3 * g + 3)
                    nc.vector.tensor_tensor(dt[u][:, :, :], tmp[2][:, :, :], tmp[1][:, :, :], ALU.add
                                            ).then_inc(dt_ready, 1)

            def scale_input(g, u):
                dve.wait_ge(dt_ready, g + 1)
                nc.vector.tensor_tensor(dtx[u][:, :, :], dt[u][:, :, :], xg[u][:, :, :], ALU.mult
                                        ).then_inc(dtx_ready, 1)

            def skip(g, u):
                for t in range(DT):
                    dve.wait_ge(summed, DT * (NS * g + NS - 1) + t + 1)
                    nc.vector.scalar_tensor_tensor(tmp[0][:, t, :], xg[u][:, t, :], D_cols[:, t:t + 1],
                                                   y_ps[:, t, :T], ALU.mult, ALU.add).then_inc(yv_ready, 1)

            def centre(g, u):
                dve.wait_ge(epi_full, EPI * g + MEAN + 1)
                nc.vector.tensor_tensor(tmp[0][:, :, :], tmp[0][:, :, :], over_tiles(epi_ps[:, :T]),
                                        ALU.subtract).then_inc(epi_free, 1)

            def invert(g, half):
                dve.wait_ge(epi_free, EPI * g + VAR + 1)
                part = std[:, half * (T // 2):(half + 1) * (T // 2)]
                nc.vector.reciprocal(part, part).then_inc(rs_ready, 1)

            def rescale(g, u):
                dve.wait_ge(rs_ready, 2 * g + 2)
                nc.vector.tensor_tensor(tmp[0][:, :, :], tmp[0][:, :, :], over_tiles(std[:, :]),
                                        ALU.mult).then_inc(yn_ready, 1)

            def add_residual(g, u, half):
                dve.wait_ge(epi_full, EPI * g + WO + half + 1)
                if half == 0:
                    dve.wait_ge(res_loaded[u], 8 * g + 8 * (2 - u))
                rows = xres[u][:TK, 2 * half:2 * half + 2, :]
                nc.vector.tensor_tensor(rows, rows, epi_ps[:TK, :].rearrange("p (k c) -> p k c", k=2),
                                        ALU.add).then_inc(epi_free, 1)

            def flat(t):
                return t[:, :, :].rearrange("p a n -> p (a n)")

            def inject(g, u, n):
                N, v = g * NS + n, n % 2
                dve.wait_ge(B_copied, N + 1)
                wait(dve, scanned, N - 1)
                nc.vector.tensor_tensor(wB[v][:, :, 1:1 + TV], dtx[u][:, :, :TV], over_tiles(b_ps[:, :TV]),
                                        ALU.mult).then_inc(wB_ready, 1)

            def scan(g, n):
                N, v = g * NS + n, n % 2
                dve.wait_ge(wB_ready, N + 1)
                dve.wait_ge(wB_rest_ready, N + 1)
                dve.wait_ge(in_ready, N + 1)
                dve.wait_ge(dA_ready, N + 1)
                wait(dve, hC_ready, N - 1)
                wait(dve, carried, N - 1)
                nc.vector.tensor_tensor_scan(flat(hs[v]), flat(dA[v]), flat(wB[v]), 0.0, ALU.mult,
                                             ALU.add).then_inc(scanned, 1)

            def strip(g, u, epi, pro):
                for n in range(NS):
                    if epi and n == 2:
                        skip(g - 1, 1 - u)
                    if n + 1 < NS:
                        inject(g, u, n + 1)
                    elif pro:
                        dve.wait_ge(dtx_ready, g + 2)
                        inject(g + 1, 1 - u, 0)
                    scan(g, n)
                    if epi:
                        if n == 7:
                            centre(g - 1, 1 - u)
                        if n in (14, 15):
                            invert(g - 1, n - 14)
                        if n == 16:
                            rescale(g - 1, 1 - u)
                        if n in (27, 35):
                            add_residual(g - 1, 1 - u, (n - 27) // 8)
                    if pro:
                        if n in (38, 40, 42, 44):
                            residue(g + 1, 1 - u, (n - 38) // 2)
                        if n in (39, 41, 43, 45):
                            low_part(g + 1, 1 - u, (n - 39) // 2)
                        if n in (54, 56, 58, 60):
                            softplus(g + 1, 1 - u, (n - 54) // 2)
                        if n == 62:
                            scale_input(g + 1, 1 - u)

            for q in range(QUARTERS):
                residue(0, 0, q)
                low_part(0, 0, q)
            for part in range(4):
                softplus(0, 0, part)
            scale_input(0, 0)
            dve.wait_ge(dtx_ready, 1)
            inject(0, 0, 0)
            run(dve, strip)
            last = STRIPS - 1
            skip(last, 1)
            centre(last, 1)
            for half in range(2):
                invert(last, half)
            rescale(last, 1)
            for half in range(2):
                add_residual(last, 1, half)

        @block.tensor
        def _(pe):
            pe.wait_ge(s_ready, NREADY)
            pe.wait_ge(s_const, 16 * NCONST)
            pe.wait_ge(diag_ready, 3)

            def convolve(g, t, first, last):
                order = [(1, 1)] + [(y, x) for y in range(CK) for x in range(CK) if (y, x) != (1, 1)]
                if first == 0:
                    pe.wait_ge(halo_loaded, 16 * g + 16)
                    wait(pe, pro_free, PRO * g + t)
                for n in range(first, last):
                    y, x = order[n]
                    dx = x - 1
                    lo, hi = max(0, -dx), min(W, W - dx)
                    step = nc.tensor.matmul(
                        pro_ps[:, :T].rearrange("p (h w) -> p h w", w=W)[:, :, lo:hi], conv_diag[:, CK * y + x, t, :],
                        x_halo[:, t, :].rearrange("p (h w) -> p h w", w=W)[:, y:y + WS, lo + dx:hi + dx],
                        start=n == 0, stop=n == TAPS - 1)
                if last == TAPS:
                    step.then_inc(pro_full, 1)

            def project(g, u, use, first, last):
                if first == 0:
                    pe.wait_ge(pro_free, PRO * g + use)
                column = (use - BC) * TRI
                width = RK if use == DTR else TRI
                for t in range(first, last):
                    step = nc.tensor.matmul(pro_ps[:width, :T], wx_sb[:, t, column:column + width], xg[u][:, t, :],
                                            start=t == 0, stop=t == DT - 1)
                if last == DT:
                    step.then_inc(pro_full, 1)

            def step_size(g, t):
                pe.wait_ge(pro_free, PRO * g + DT0 + t)
                nc.tensor.matmul(pro_ps[:, :T], wdt_sb[:, t * P:(t + 1) * P], dt_low[:, :], start=True,
                                 stop=True).then_inc(pro_full, 1)

            def average(g, use, t):
                if use == MEAN:
                    pe.wait_ge(yv_ready, DT * g + t + 1)
                    if t == 0:
                        wait(pe, epi_free, EPI * g)
                else:
                    pe.wait_ge(sq_ready, DT * g + t + 1)
                    if t == 0:
                        pe.wait_ge(epi_free, EPI * g + use)
                src = tmp[0] if use == MEAN else tmp[1]
                step = nc.tensor.matmul(epi_ps[:, :T], averager[:, :], src[:, t, :], start=t == 0, stop=t == DT - 1)
                if t == DT - 1:
                    step.then_inc(epi_full, 1)

            def out_project(g, k, first, last):
                if k == 0:
                    pe.wait_ge(yo_ready, DT * g + DT)
                if k % 2 == 0 and first == 0:
                    pe.wait_ge(epi_free, EPI * g + WO + k // 2)
                dst = epi_ps[:TK, k % 2 * C:(k % 2 + 1) * C]
                if first == 0:
                    nc.tensor.matmul(dst, ones_row[:, :], bout_row[:, :], start=True, stop=False)
                for t in range(first, last):
                    step = nc.tensor.matmul(dst, tmp[3][:, t, k * TK:(k + 1) * TK], wout_sb[:, t, :], start=False,
                                            stop=t == DT - 1)
                if k % 2 and last == DT:
                    step.then_inc(epi_full, 1)

            def spread(g, u, n, s):
                N = g * NS + n
                if s == 0:
                    dst, semaphore = b_ps[:, :T], B_ready
                    wait(pe, wB_ready, N)
                else:
                    dst, semaphore = c_ps[:, :T], C_ready
                    wait(pe, C_copied, N)
                q, r = divmod(s * NS + n, QS)
                nc.tensor.matmul(dst, tri_b[:TRI, r:r + 1].broadcast_to([TRI, P]), pack[q][u][:TRI, :],
                                 start=True, stop=True).then_inc(semaphore, 1)

            def accumulate(g, n, first=0, last=DT):
                if first == 0:
                    pe.wait_ge(hC_ready, g * NS + n + 1)
                for t in range(first, last):
                    if n == 0:
                        wait(pe, yv_ready, DT * (g - 1) + t + 1)
                    nc.tensor.matmul(y_ps[:, t, :T], ident[:, :], hC[n % 2][:, t, :], start=n == 0,
                                     stop=n == NS - 1).then_inc(summed, 1)

            def packs_placed(g):
                pe.wait_ge(pack_done, QUARTERS * g + QUARTERS)
                pe.wait_ge(low_ready, QUARTERS * g + QUARTERS)

            def taps_before(n):
                return n - 2 + min(max(n - 15, 0), 2)

            def strip(g, u, epi, pro):
                for n in range(NS):
                    if n >= 2:
                        accumulate(g, n - 2, 0, 2)
                    elif epi:
                        accumulate(g - 1, NS - 2 + n, 0, 2)
                    if n + 2 < NS:
                        spread(g, u, n + 2, 0)
                    elif pro:
                        if n + 2 == NS:
                            packs_placed(g + 1)
                        spread(g + 1, 1 - u, n + 2 - NS, 0)
                    if n >= 2:
                        accumulate(g, n - 2, 2, DT)
                    elif epi:
                        accumulate(g - 1, NS - 2 + n, 2, DT)
                    if n + 1 < NS:
                        spread(g, u, n + 1, 1)
                    elif pro:
                        spread(g + 1, 1 - u, 0, 1)
                    if epi:
                        if 3 <= n < 7:
                            average(g - 1, MEAN, n - 3)
                        if 8 <= n < 12:
                            average(g - 1, VAR, n - 8)
                        if 19 <= n < 35:
                            k, t = divmod(n - 19, DT)
                            out_project(g - 1, k, t, t + 1)
                    if pro:
                        if 2 <= n < 36:
                            t, tap = divmod(taps_before(n), TAPS)
                            convolve(g + 1, t, tap, taps_before(n + 1) - t * TAPS)
                        if 36 <= n < 46:
                            first = n % 2 * (DT // 2)
                            project(g + 1, 1 - u, BC + (n - 36) // 2, first, first + DT // 2)
                        if 46 <= n < 50:
                            step_size(g + 1, n - 46)

            for t in range(DT):
                convolve(0, t, 0, TAPS)
            for use in range(BC, DT0):
                project(0, 0, use, 0, DT)
            for t in range(DT):
                step_size(0, t)
            packs_placed(0)
            for n in range(2):
                spread(0, 0, n, 0)
            spread(0, 0, 0, 1)
            run(pe, strip)
            last = STRIPS - 1
            accumulate(last, NS - 2)
            accumulate(last, NS - 1)
            for use in (MEAN, VAR):
                for t in range(DT):
                    average(last, use, t)
            for k in range(NK):
                out_project(last, k, 0, DT)

        @block.scalar
        def _(act):
            act.wait_ge(s_const, 16 * NCONST)
            act.wait_ge(a_capped, 1)
            nc.scalar.activation(A_sb[:, :, :], A_sb[:, :, :], ACT.Exp).then_inc(a_exp, 1)
            act.wait_ge(a_ready, 1)
            act.wait_ge(s_ready, NREADY)

            def gelu(g, u, t):
                act.wait_ge(pro_full, PRO * g + t + 1)
                if t == 0:
                    wait(act, yv_ready, DT * (g - 1))
                nc.scalar.activation(xg[u][:, t, :], pro_ps[:, :T], ACT.Gelu_apprx_tanh,
                                     bias=conv_bias[:, t:t + 1]).then_inc(pro_free, 1)

            def high_part(g, u, q):
                act.wait_ge(pro_full, PRO * g + BC + q + 1)
                nc.scalar.activation(pack[q][u][:TRI, :], pro_ps[:TRI, :T], ACT.Copy).then_inc(pack_ready, 1)

            def mid_part(g, u, q):
                act.wait_ge(pro_free, PRO * g + BC + q + 1)
                wait(act, low_ready, QUARTERS * g + q)
                wait(act, pack_done, QUARTERS * g + q)
                nc.scalar.activation(mid[:TRI, :], rest[:TRI, :], ACT.Copy).then_inc(mid_ready, 1)

            def place_mid(g, u, q):
                act.wait_ge(mid_ready, QUARTERS * g + q + 1)
                nc.scalar.activation(pack[q][u][QS:2 * QS, :], mid[QS:2 * QS, :], ACT.Copy).then_inc(pack_done, 1)

            def low_rank(g):
                act.wait_ge(pro_full, PRO * g + DTR + 1)
                nc.scalar.activation(dt_low[:, :], pro_ps[:RK, :T], ACT.Copy).then_inc(pro_free, 1)

            def step_bias(g, t):
                act.wait_ge(pro_full, PRO * g + DT0 + t + 1)
                nc.scalar.activation(tmp[0][:, t, :], pro_ps[:, :T], ACT.Identity,
                                     bias=dt_bias[:, t:t + 1]).then_inc(pro_free, 1)

            def softplus_logs(g, part, half):
                tiles = slice(half * DT // 2, (half + 1) * DT // 2)
                if part == 0:
                    act.wait_ge(pro_free, PRO * g + PRO)
                    nc.scalar.activation(tmp[1][:, tiles, :], tmp[0][:, tiles, :], ACT.Abs).then_inc(act_chain, 1)
                elif part == 1:
                    act.wait_ge(act_chain, 4 * g + half + 1)
                    nc.scalar.activation(tmp[1][:, tiles, :], tmp[1][:, tiles, :], ACT.Exp, scale=-1.0
                                         ).then_inc(act_chain, 1)
                elif half:
                    act.wait_ge(act_chain, 4 * g + 4)
                    nc.scalar.activation(tmp[2][:, :, :], tmp[1][:, :, :], ACT.Ln, bias=1.0).then_inc(soft_ready, 1)

            def square(g, t):
                act.wait_ge(epi_free, EPI * g + MEAN + 1)
                nc.scalar.activation(tmp[1][:, t, :], tmp[0][:, t, :], ACT.Square).then_inc(sq_ready, 1)

            def deviation(g):
                act.wait_ge(epi_full, EPI * g + VAR + 1)
                nc.scalar.activation(std[:, :], epi_ps[:, :T], ACT.Sqrt, bias=eps_col[:, :]).then_inc(epi_free, 1)

            def affine(g, t):
                act.wait_ge(yn_ready, g + 1)
                nc.scalar.activation(tmp[3][:, t, :], tmp[0][:, t, :], ACT.Identity, bias=b_cols[:, t:t + 1],
                                     scale=g_cols[:, t:t + 1]).then_inc(yo_ready, 1)

            def carry_out(g, n):
                act.wait_ge(in_ready, g * NS + n + 1)
                nc.scalar.activation(carry[:, n, :], hs[n % 2][:, :, T], ACT.Copy).then_inc(carried, 1)

            def decay(g, u, n):
                N, v = g * NS + n, n % 2
                wait(act, scanned, N - 1)
                if n >= 2:
                    carry_out(g, n - 2)
                elif not isinstance(g, int) or g > 0:
                    carry_out(g - 1, NS - 2 + n)
                wait(act, carried, N - NS + 1)
                nc.scalar.activation(wB[v][:, :, 0], carry[:, n, :], ACT.Copy,
                                     scale=keep_now[u][:, :]).then_inc(in_ready, 1)
                for t in range(DT):
                    last = nc.scalar.activation(dA[v][:, t, 1:], dt[u][:, t, :], ACT.Exp, scale=A_sb[:, t, n:n + 1])
                last.then_inc(dA_ready, 1)

            def copy_B(g, n):
                N, v = g * NS + n, n % 2
                act.wait_ge(B_ready, N + 1)
                wait(act, wB_rest_ready, N - 1)
                nc.scalar.activation(B_rest[v][:, :], b_ps[:, TV:T], ACT.Copy).then_inc(B_copied, 1)

            def copy_C(g, n):
                N, v = g * NS + n, n % 2
                act.wait_ge(C_ready, N + 1)
                wait(act, hC_ready, N - 1)
                nc.scalar.activation(Csb[v][:, :], c_ps[:, :T], ACT.Copy).then_inc(C_copied, 1)

            def strip(g, u, epi, pro):
                nc.scalar.activation(keep_now[u][:, :], keep[:, bass.ds(g, 1)], ACT.Copy).then_inc(keep_ready, 1)
                act.wait_ge(keep_ready, g + 1)
                act.wait_ge(dt_ready, g + 1)
                for n in range(NS):
                    if n + 1 < NS:
                        copy_B(g, n + 1)
                    elif pro:
                        copy_B(g + 1, 0)
                    decay(g, u, n)
                    copy_C(g, n)
                    if epi:
                        if 8 <= n < 12:
                            square(g - 1, n - 8)
                        if n == 12:
                            deviation(g - 1)
                        if n in (17, 18):
                            for t in range(2 * (n - 17), 2 * (n - 16)):
                                affine(g - 1, t)
                    if pro:
                        if n in (11, 18, 27, 36):
                            gelu(g + 1, 1 - u, n // TAPS - 1)
                        if n in (38, 40, 42, 44):
                            high_part(g + 1, 1 - u, (n - 38) // 2)
                        if n in (39, 41, 43, 45):
                            mid_part(g + 1, 1 - u, (n - 39) // 2)
                        if n in (40, 42, 44, 46):
                            place_mid(g + 1, 1 - u, (n - 40) // 2)
                        if n == 46:
                            low_rank(g + 1)
                        if 47 <= n < 51:
                            step_bias(g + 1, n - 47)
                        if 50 <= n < 56:
                            softplus_logs(g + 1, (n - 50) // 2, (n - 50) % 2)

            for t in range(DT):
                gelu(0, 0, t)
            for q in range(QUARTERS):
                high_part(0, 0, q)
                mid_part(0, 0, q)
                place_mid(0, 0, q)
            low_rank(0)
            for t in range(DT):
                step_bias(0, t)
            for part in range(3):
                for half in range(2):
                    softplus_logs(0, part, half)
            copy_B(0, 0)
            run(act, strip)
            last = STRIPS - 1
            for t in range(DT):
                square(last, t)
            deviation(last)
            for t in range(DT):
                affine(last, t)


def program(nc, a, out):
    QT = nc.dram_tensor("QT", [STRIPS, P, NWIN * CT * WT], F32).ap()
    KT = nc.dram_tensor("KT", [STRIPS * NWIN, P, CT * WT], F32).ap()
    VT = nc.dram_tensor("VT", [NB, CT, P, VROWS * W], F32).ap()
    VN = nc.dram_tensor("VN", [STRIPS * NWIN, WT, C], F32).ap()
    IDX = nc.dram_tensor("IDX", [NB, WPI, TOPK], I32).ap()
    X2 = nc.dram_tensor("X2", [STRIPS, TK, NK * C], F32).ap()
    XI = nc.dram_tensor("XI", [NB, DT, P, XROWS * W], F32).ap()
    with ExitStack() as ctx:
        qsum = ctx.enter_context(nc.sbuf_tensor("qsum", [P, STRIPS * NWSUM], F32))
        ksum = ctx.enter_context(nc.sbuf_tensor("ksum", [P, STRIPS * NWSUM], F32))
        phase_qkv(nc, a["x"], a["L0_conv_ln1_g"], a["L0_conv_ln1_b"], a["L0_conv_qkv_w"], a["L0_conv_qkv_b"],
                  QT, KT, VT, VN, qsum, ksum)
        phase_route(nc, qsum, ksum, IDX)
    phase_attention(nc, a["x"], QT, KT, VT, VN, IDX, a["L0_conv_lepe_w"], a["L0_conv_lepe_b"], a["L0_conv_wo_w"],
                    a["L0_conv_wo_b"], a["L0_conv_ln2_g"], a["L0_conv_ln2_b"], a["L0_conv_mlp_w1"],
                    a["L0_conv_mlp_b1"], a["L0_conv_mlp_w2"], a["L0_conv_mlp_b2"], a["L1_conv_ln1_g"],
                    a["L1_conv_ln1_b"], a["L1_conv_w_in"], a["L1_conv_b_in"], X2, XI)
    phase_scan(nc, a, X2, XI, out)


_INS = ["x", "L0_conv_ln1_g", "L0_conv_ln1_b", "L0_conv_qkv_w", "L0_conv_qkv_b", "L0_conv_lepe_w",
        "L0_conv_lepe_b", "L0_conv_wo_w", "L0_conv_wo_b", "L0_conv_ln2_g", "L0_conv_ln2_b", "L0_conv_mlp_w1",
        "L0_conv_mlp_b1", "L0_conv_mlp_w2", "L0_conv_mlp_b2", "L1_conv_ln1_g", "L1_conv_ln1_b", "L1_conv_w_in",
        "L1_conv_b_in", "L1_conv_conv_w", "L1_conv_conv_b", "L1_conv_w_x", "L1_conv_w_dt", "L1_conv_dt_bias",
        "L1_conv_A_log", "L1_conv_D_skip", "L1_conv_ln2_g", "L1_conv_ln2_b", "L1_conv_w_out", "L1_conv_b_out"]


def kernel(**inputs):
    import numpy as _np
    import concourse.bacc as _bacc
    from concourse import mybir as _mybir
    from concourse.bass_utils import run_bass_kernel_spmd as _run

    nc = _bacc.Bacc("TRN2", target_bir_lowering=False, num_devices=1)
    arrays, args = {}, {}
    for name in _INS:
        a = _np.ascontiguousarray(inputs[name])
        arrays[f"in_{name}_dram"] = a
        args[name] = nc.dram_tensor(f"in_{name}_dram", a.shape, _mybir.dt.from_np(a.dtype), kind="ExternalInput").ap()
    out = nc.dram_tensor("out_0_dram", (NB, H, W, C), _mybir.dt.from_np(_np.dtype("float32")),
                         kind="ExternalOutput").ap()
    program(nc, args, out)
    r = _run(nc, [arrays], core_ids=[0])
    return r.results[0]["out_0_dram"]
```
